# Optimizing a Trainium2 kernel written in Bass

```python
import numpy as np
import jax
import jax.numpy as jnp

def _softmax(x, axis=-1):
    return jax.nn.softmax(x, axis=axis)

def _gelu(x):
    return jax.nn.gelu(x, approximate=True)

def _silu(x):
    return jax.nn.silu(x)

def _sigmoid(x):
    return jax.nn.sigmoid(x)

def _layernorm(x, axis=-1, eps=1e-05):
    m = jnp.mean(x, axis=axis, keepdims=True)
    v = jnp.var(x, axis=axis, keepdims=True)
    return (x - m) / jnp.sqrt(v + eps)

def _scatter_add(tgt, idx, src, axis=0):
    return tgt.at[idx].add(src)

def _segment_sum(src, seg, n):
    return jax.ops.segment_sum(src, seg, n)
kernel_name = 'mk_gnn_resnorm_d2_gnn_r64_81f383'

def setup_inputs(seed: int=0):
    np.random.seed(seed)
    _w = jnp.asarray

    def _rec_inputs():
        import jax
        import jax.numpy as jnp
        _gk = jax.random.key(seed)
        x = -0.0003713 + 1 * jax.random.normal(jax.random.fold_in(_gk, 1), (50000, 128), jnp.float32)
        src = jax.random.randint(jax.random.fold_in(_gk, 2), (12500,), 0, 50000, jnp.int32)
        dst = jax.random.randint(jax.random.fold_in(_gk, 3), (12500,), 0, 50000, jnp.int32)
        _o = jnp.argsort(dst, stable=True)
        src = src[_o]
        dst = dst[_o]
        edge_type_3 = jax.random.randint(jax.random.fold_in(_gk, 12), (12500,), 0, 3, jnp.int32)
        node_type_3 = jax.random.randint(jax.random.fold_in(_gk, 13), (50000,), 0, 3, jnp.int32)
        return (x, src, dst, edge_type_3, node_type_3)
    x, src, dst, edge_type_3, node_type_3 = _rec_inputs()

    def _L0_gnn_setup():
        import jax, jax.numpy as jnp
        import numpy as np
        N = 100000
        E = 25000
        D = 128
        H = 4
        C = 32
        EPS = 1e-05
        NEG_SLOPE = 0.2

        def _gat_conv(x, src, dst, W, a_s, a_d, b):
            n = x.shape[0]
            h = (x @ W).reshape(n, H, C)
            al_s = (h * a_s).sum(-1)
            al_d = (h * a_d).sum(-1)
            e = jax.nn.leaky_relu(al_s[src] + al_d[dst], NEG_SLOPE)
            m = jax.ops.segment_max(e, dst, num_segments=n)
            ex = jnp.exp(e - m[dst])
            denom = jax.ops.segment_sum(ex, dst, num_segments=n)
            alpha = ex / denom[dst]
            msg = h[src] * alpha[:, :, None]
            out = jax.ops.segment_sum(msg, dst, num_segments=n)
            return out.reshape(n, H * C) + b

        def _layernorm(x, g, b):
            mu = x.mean(-1, keepdims=True)
            var = x.var(-1, keepdims=True)
            return (x - mu) * jax.lax.rsqrt(var + EPS) * g + b
        key = jax.random.key(seed)
        ks = jax.random.split(key, 24)
        inp = {'x': jax.random.normal(ks[0], (N, D), dtype=jnp.float32), 'edge_src': jax.random.randint(ks[1], (E,), 0, N, dtype=jnp.int32), 'edge_dst': jax.random.randint(ks[2], (E,), 0, N, dtype=jnp.int32)}
        dins = [D, H * C, H * C]
        for l in range(3):
            din = dins[l]
            scale = 1.0 / np.sqrt(din)
            inp[f'W{l}'] = jax.random.normal(ks[3 + 3 * l], (din, H * C), dtype=jnp.float32) * scale
            inp[f'a_src{l}'] = jax.random.normal(ks[4 + 3 * l], (H, C), dtype=jnp.float32) * 0.1
            inp[f'a_dst{l}'] = jax.random.normal(ks[5 + 3 * l], (H, C), dtype=jnp.float32) * 0.1
            inp[f'b{l}'] = jnp.zeros((H * C,), dtype=jnp.float32)
        for l in range(2):
            inp[f'ln{l}_g'] = jnp.ones((H * C,), dtype=jnp.float32)
            inp[f'ln{l}_b'] = jnp.zeros((H * C,), dtype=jnp.float32)
        return inp
    _L0_gnn_all = _L0_gnn_setup()
    _L0_gnn_in = {k: v for k, v in _L0_gnn_all.items() if k in ('W0', 'a_src0', 'a_dst0', 'b0', 'W1', 'a_src1', 'a_dst1', 'b1', 'W2', 'a_src2', 'a_dst2', 'b2', 'ln0_g', 'ln0_b', 'ln1_g', 'ln1_b')}
    del _L0_gnn_all

    def _L1_gnn_setup():
        import jax, jax.numpy as jnp
        import numpy as np
        N_NODES = 50000
        N_EDGES = 12500
        D = 128
        T = 3
        NODE_IN = D + T * D
        key = jax.random.key(seed)
        ks = jax.random.split(key, 8)
        scale = 0.05
        return {'node_feature': jax.random.normal(ks[0], (N_NODES, D), jnp.float32), 'W_e': jax.random.normal(ks[1], (T, D, D), jnp.float32) * scale, 'b_e': jnp.zeros((T, D), jnp.float32), 'W_n': jax.random.normal(ks[2], (T, D, NODE_IN), jnp.float32) * scale, 'b_n': jnp.zeros((T, D), jnp.float32), 'edge_src': jax.random.randint(ks[3], (N_EDGES,), 0, N_NODES, jnp.int32), 'edge_dst': jax.random.randint(ks[4], (N_EDGES,), 0, N_NODES, jnp.int32), 'edge_type': jax.random.randint(ks[5], (N_EDGES,), 0, T, jnp.int32), 'node_type': jax.random.randint(ks[6], (N_NODES,), 0, T, jnp.int32)}
    _L1_gnn_all = _L1_gnn_setup()
    _L1_gnn_in = {k: v for k, v in _L1_gnn_all.items() if k in ('W_e', 'b_e', 'W_n', 'b_n')}
    del _L1_gnn_all
    return {'x': x, 'src': src, 'dst': dst, 'edge_type_3': edge_type_3, 'node_type_3': node_type_3, 'L0_gnn_W0': _L0_gnn_in['W0'], 'L0_gnn_a_src0': _L0_gnn_in['a_src0'], 'L0_gnn_a_dst0': _L0_gnn_in['a_dst0'], 'L0_gnn_b0': _L0_gnn_in['b0'], 'L0_gnn_W1': _L0_gnn_in['W1'], 'L0_gnn_a_src1': _L0_gnn_in['a_src1'], 'L0_gnn_a_dst1': _L0_gnn_in['a_dst1'], 'L0_gnn_b1': _L0_gnn_in['b1'], 'L0_gnn_W2': _L0_gnn_in['W2'], 'L0_gnn_a_src2': _L0_gnn_in['a_src2'], 'L0_gnn_a_dst2': _L0_gnn_in['a_dst2'], 'L0_gnn_b2': _L0_gnn_in['b2'], 'L0_gnn_ln0_g': _L0_gnn_in['ln0_g'], 'L0_gnn_ln0_b': _L0_gnn_in['ln0_b'], 'L0_gnn_ln1_g': _L0_gnn_in['ln1_g'], 'L0_gnn_ln1_b': _L0_gnn_in['ln1_b'], 'L1_gnn_W_e': _L1_gnn_in['W_e'], 'L1_gnn_b_e': _L1_gnn_in['b_e'], 'L1_gnn_W_n': _L1_gnn_in['W_n'], 'L1_gnn_b_n': _L1_gnn_in['b_n']}

def reference(x, src, dst, edge_type_3, node_type_3, L0_gnn_W0, L0_gnn_a_src0, L0_gnn_a_dst0, L0_gnn_b0, L0_gnn_W1, L0_gnn_a_src1, L0_gnn_a_dst1, L0_gnn_b1, L0_gnn_W2, L0_gnn_a_src2, L0_gnn_a_dst2, L0_gnn_b2, L0_gnn_ln0_g, L0_gnn_ln0_b, L0_gnn_ln1_g, L0_gnn_ln1_b, L1_gnn_W_e, L1_gnn_b_e, L1_gnn_W_n, L1_gnn_b_n):
    import jax
    import jax.numpy as jnp

    def _L0_gnn_ref(x, edge_src, edge_dst, W0, a_src0, a_dst0, b0, W1, a_src1, a_dst1, b1, W2, a_src2, a_dst2, b2, ln0_g, ln0_b, ln1_g, ln1_b):
        import jax, jax.numpy as jnp
        import numpy as np
        N = 100000
        E = 25000
        D = 128
        H = 4
        C = 32
        EPS = 1e-05
        NEG_SLOPE = 0.2

        def _gat_conv(x, src, dst, W, a_s, a_d, b):
            n = x.shape[0]
            h = (x @ W).reshape(n, H, C)
            al_s = (h * a_s).sum(-1)
            al_d = (h * a_d).sum(-1)
            e = jax.nn.leaky_relu(al_s[src] + al_d[dst], NEG_SLOPE)
            m = jax.ops.segment_max(e, dst, num_segments=n)
            ex = jnp.exp(e - m[dst])
            denom = jax.ops.segment_sum(ex, dst, num_segments=n)
            alpha = ex / denom[dst]
            msg = h[src] * alpha[:, :, None]
            out = jax.ops.segment_sum(msg, dst, num_segments=n)
            return out.reshape(n, H * C) + b

        def _layernorm(x, g, b):
            mu = x.mean(-1, keepdims=True)
            var = x.var(-1, keepdims=True)
            return (x - mu) * jax.lax.rsqrt(var + EPS) * g + b
        n = x.shape[0]
        loops = jnp.arange(n, dtype=edge_src.dtype)
        src = jnp.concatenate([edge_src, loops])
        dst = jnp.concatenate([edge_dst, loops])
        h = _gat_conv(x, src, dst, W0, a_src0, a_dst0, b0)
        h = jax.nn.relu(_layernorm(h, ln0_g, ln0_b))
        h = _gat_conv(h, src, dst, W1, a_src1, a_dst1, b1)
        h = jax.nn.relu(_layernorm(h, ln1_g, ln1_b))
        h = _gat_conv(h, src, dst, W2, a_src2, a_dst2, b2)
        return h

    def _L1_gnn_ref(node_feature, W_e, b_e, W_n, b_n, edge_src, edge_dst, edge_type, node_type):
        import jax, jax.numpy as jnp
        import numpy as np
        N_NODES = 50000
        N_EDGES = 12500
        D = 128
        T = 3
        NODE_IN = D + T * D
        N, Din = node_feature.shape
        n_types = W_e.shape[0]
        out_dim = W_e.shape[1]
        src = node_feature[edge_src]
        parts = [jax.nn.relu(node_feature)]
        for t in range(n_types):
            msg = jax.nn.relu(src @ W_e[t].T + b_e[t])
            msg = jnp.where((edge_type == t)[:, None], msg, jnp.zeros((), msg.dtype))
            parts.append(jax.ops.segment_sum(msg, edge_dst, num_segments=N))
        agg = jnp.concatenate(parts, axis=1)
        updated = jnp.zeros((N, out_dim), node_feature.dtype)
        for t in range(n_types):
            o = agg @ W_n[t].T + b_n[t]
            updated = jnp.where((node_type == t)[:, None], o, updated)
        return updated + node_feature
    x = _layernorm(x + _L0_gnn_ref(x, src, dst, L0_gnn_W0, L0_gnn_a_src0, L0_gnn_a_dst0, L0_gnn_b0, L0_gnn_W1, L0_gnn_a_src1, L0_gnn_a_dst1, L0_gnn_b1, L0_gnn_W2, L0_gnn_a_src2, L0_gnn_a_dst2, L0_gnn_b2, L0_gnn_ln0_g, L0_gnn_ln0_b, L0_gnn_ln1_g, L0_gnn_ln1_b), axis=-1)
    x = _layernorm(x + _L1_gnn_ref(x, L1_gnn_W_e, L1_gnn_b_e, L1_gnn_W_n, L1_gnn_b_n, src, dst, edge_type_3, node_type_3), axis=-1)
    return x

_drawn_inputs = setup_inputs


def setup_inputs(seed=0):
    import zlib

    import numpy as np

    out = dict(_drawn_inputs(seed))
    spreads = {'L0_gnn_b0': (0.0, 0.1),
     'L0_gnn_b1': (0.0, 0.1),
     'L0_gnn_b2': (0.0, 0.1),
     'L0_gnn_ln0_g': (1.0, 0.2),
     'L0_gnn_ln0_b': (0.0, 0.1),
     'L0_gnn_ln1_g': (1.0, 0.2),
     'L0_gnn_ln1_b': (0.0, 0.1),
     'L1_gnn_b_e': (0.0, 0.8),
     'L1_gnn_b_n': (0.0, 0.1)}
    factors = {'L0_gnn_a_dst0': 6.025,
     'L0_gnn_a_src1': 6.674,
     'L0_gnn_a_dst1': 8.0,
     'L0_gnn_a_src2': 7.819,
     'L0_gnn_a_dst2': 8.0}
    for name, (base, spread) in spreads.items():
        noise = np.random.default_rng([zlib.crc32(name.encode()), seed]).standard_normal(out[name].shape)
        drawn = base * np.exp(spread * noise) if base else spread * noise
        out[name] = jnp.asarray(drawn.astype(out[name].dtype))
    for name, factor in factors.items():
        out[name] = (out[name] * factor).astype(out[name].dtype)
    return out
```

```python
from contextlib import ExitStack

import concourse.bass as bass
from concourse import mybir

ALU = mybir.AluOpType
ACT = mybir.ActivationFunctionType
AX_X = mybir.AxisListType.X
F32 = mybir.dt.float32
I32 = mybir.dt.int32
BF16 = mybir.dt.bfloat16

P = 128
EPS = 1e-5
NEG_SLOPE = 0.2
BIG = 1.0e30
SKIP = 1000000


class Steps:

    def __init__(self, eng, sem):
        self.eng, self.sem, self.base, self.c, self.i, self.per = eng, sem, 0, 0, 0, 0
        self.due = eng.alloc_register("due")

    def enter(self, i, per):
        self.i, self.per, self.c = i, per, 0

    def loop(self, bodies, per):
        self.base, self.c = self.base + self.c, 0

        def leave():
            self.base, self.i, self.per, self.c = self.base + bodies * per, 0, 0, 0
        return leave

    def wait(self, sem, value, first=None):
        if first and not isinstance(value, int):
            self.eng.reg_mov(self.due, value)
            value = self.due
            self.eng.wait_ge(*first)
        self.eng.wait_ge(sem, value)

    def did(self, ins, first=None):
        ins.then_inc(self.sem, 1)
        self.c += 1
        self.wait(self.sem, self.base + self.i * self.per + self.c, first)


def run(eng, body, lo, hi, peel=()):
    i = lo
    while i < hi:
        if i in peel:
            body(i)
            i += 1
            continue
        end = min([x for x in peel if x > i] + [hi])
        end = min(end, hi)
        if end - i == 1:
            body(i)
        else:
            with eng.Fori(i, end) as r:
                body(r)
        i = end


def build(nc, a, out):
    x, src, dst = a["x"], a["src"], a["dst"]
    etype, ntype = a["edge_type_3"], a["node_type_3"]
    W = [a[f"L0_gnn_W{l}"] for l in range(3)]
    A_S = [a[f"L0_gnn_a_src{l}"] for l in range(3)]
    A_D = [a[f"L0_gnn_a_dst{l}"] for l in range(3)]
    B = [a[f"L0_gnn_b{l}"] for l in range(3)]
    LN = [(a[f"L0_gnn_ln{l}_g"], a[f"L0_gnn_ln{l}_b"]) for l in range(2)]
    WE, BE, WN, BN = a["L1_gnn_W_e"], a["L1_gnn_b_e"], a["L1_gnn_W_n"], a["L1_gnn_b_n"]

    N, D = x.shape
    E = src.shape[0]
    H, C = A_S[0].shape
    K3 = WE.shape[0]
    assert D == P and H * C == P and K3 == 3

    G, Q = 4, 4
    R = G * Q
    SB = P * R
    NS = -(-N // SB)
    LAST = NS - 1
    T = -(-E // P)
    CH = 7
    assert T % (2 * CH) == 0
    IT = T // (2 * CH)
    TU = 2 * CH
    FULL = E // T
    TAIL = E - FULL * T
    assert FULL == P - 1 and 0 < TAIL < T
    WA = P + 2 * H + 1
    assert N % (NS * R) == 0 and N // (NS * R) <= P
    MB = [0, 4, 10]
    CUTS = [0, 8, 11, 14, NS]

    table = [nc.dram_tensor(f"target_rows_{l}", (T * P, D), F32).ap() for l in range(4)]
    src0 = nc.dram_tensor("source_x_rows", (T * P, D), F32).ap()
    hdd = nc.dram_tensor("target_h_rows", (T * P, D), F32).ap()
    edge_of = nc.dram_tensor("edge_of_node", (N, 1), I32).ap()

    def chunks(ap):
        return ap.rearrange("(p c r) d -> c p (r d)", p=P, r=CH)

    def sblocks(ap):
        return ap[0:LAST * SB, :].rearrange("(i p r) d -> i p (r d)", p=P, r=R)

    def tail_block(ap):
        return ap[N - SB:N, :].rearrange("(p r) d -> p (r d)", r=R)

    with ExitStack() as ctx:
        def sb(name, shape, dt=F32):
            return ctx.enter_context(nc.sbuf_tensor(name, shape, dt))

        def sem(name):
            return ctx.enter_context(nc.semaphore(name))

        rows = sb("rows", [P, T, D])
        msg = sb("msg", [P, D * T])
        msg_f = msg[:, :].rearrange("p (f t) -> p f t", t=T)
        msg_r = msg[:, :].rearrange("p (t f) -> p t f", f=D)
        bank = ctx.enter_context(nc.psum_tensor("bank", [P, 8, 512], F32))

        dx = sb("dx", [P, R, D])
        dxt = sb("dxt", [P, Q, G * D])
        dxh = sb("dxh", [P, R, D])
        dy = sb("dy", [P, R, D])
        dsel = sb("dsel", [P, G, D])
        dstd = sb("dstd", [P, 4, R])
        drs = sb("drs", [P, 4, R])
        dmv = sb("dmv", [P, R, 2])
        dst6 = sb("dst6", [P, R, 6])
        dmk = sb("dmk", [P, 2, R], I32)
        junk = sb("junk", [P, G, D])

        stg = sb("stg", [P, TU, D])
        std_ = sb("std_", [P, TU, D])
        st3 = sb("st3", [P, TU, D])
        xt2 = sb("xt2", [P, 2, 2 * D])
        ev = sb("ev", [P, 2, D])
        csm = sb("csm", [P, 8, TU])

        ls = sb("ls", [P, T, 2 * H + 1])
        ld = sb("ld", [P, T, 2 * H])
        em = ls[:, :, :].rearrange("p t h -> p (t h)")[:, 0:6 * D].rearrange("p (u n) -> p u n", u=2)
        emt = ld[:, :, :].rearrange("p t h -> p (t h)")[:, 0:6 * D].rearrange("p (u n) -> p u n", u=2)
        e_s = sb("e_s", [P, H, T])
        e_f = sb("e_f", [P, H, T])
        fm = sb("fm", [P, H, T])
        mp = sb("mp", [P, H, T + 1])
        ea = sb("ea", [P, H, T])
        es = sb("es", [P, H, T])
        ep = sb("ep", [P, H, T])
        sm = sb("sm", [P, 6, H])
        smr = sb("smr", [H, 2, P])
        smo = sb("smo", [H, P + 1])
        smb = sb("smb", [H, P])
        ci = sb("ci", [P, H])
        rowa = sb("rowa", [P, 2, P])
        rowt = sb("rowt", [P, 2, P])
        rowo = sb("rowo", [P, P + 1])
        cin = sb("cin", [P, P])

        dst_i = sb("dst_i", [P, 3, T], I32)
        dst_f = e_s[:, 0:3, :]
        src_i = sb("src_i", [P, T], I32)
        et_i = sb("et_i", [P, T], I32)
        nt_i = sb("nt_i", [P, T], I32)
        ns = sb("ns", [P, T])
        negns = sb("negns", [P, T])
        negseen = sb("negseen", [P, T])
        unlast = sb("unlast", [P, T])
        last_r = sb("last_r", [P, T])
        more_r = sb("more_r", [P, T])
        none_r = sb("none_r", [P, T])
        keep = sb("keep", [P, T])
        kept = sb("kept", [P, T])
        lastf = sb("lastf", [P, T])
        put_i = sb("put_i", [P, T], I32)
        pos_i = sb("pos_i", [P, T], I32)
        eid = sb("eid", [P, T], I32)
        zero = sb("zero", [P, T])
        etm = e_f[:, 0:3, :]
        ntm = sb("ntm", [P, 2, T], I32)
        ntc = sb("ntc", [P, 2, TU], I32)
        types = sb("types", [P, NS * R], I32)

        ident = sb("ident", [P, P])
        ones3 = sb("ones3", [3, P], BF16)
        eps = sb("eps", [P, 1])
        wall = sb("wall", [P, 3, WA])
        wcen = sb("wcen", [P, 3, D])
        wnt = sb("wnt", [P, 4, 3 * D])
        wet = sb("wet", [P, 3 * D])
        gb = sb("gb", [P, 4])
        hm = sb("hm", [P, H])
        av = sb("av", [P, 6])
        amat = sb("amat", [P, 2 * H])
        wmean = sb("wmean", [P, 24])
        BO = [l * WA for l in range(3)]
        BEO = 3 * WA
        BNO = BEO + 3 * D
        BCO = [BNO + 3 * D + l * D for l in range(3)]
        BT = BNO + 6 * D
        bias3 = sb("bias3", [3, BT], BF16)
        bmean = sb("bmean", [1, 8])

        wraw = msg[:, 0:3 * D].rearrange("p (l d) -> p l d", l=3)
        wnraw = msg[:, 3 * D:15 * D].rearrange("p (n k) -> p n k", n=3)
        weraw = msg[:, 15 * D:18 * D].rearrange("p (n k) -> p n k", n=3)

        wtr = msg[:, 90 * D:91 * D]
        brow = msg[0:1, 18 * D:18 * D + BT]
        brest = msg[0:1, 18 * D + BT:18 * D + 2 * BT]
        bpart = msg[0:1, 18 * D + 2 * BT:18 * D + 4 * BT].bitcast(BF16)[:, 0:3 * BT].rearrange("o (k n) -> o k n", k=3)

        s_w = sem("weights_loaded")
        s_i = sem("indices_loaded")
        s_nt = sem("node_types_loaded")
        s_ms = sem("memsets_done")
        s_id = sem("identity_ready")
        s_pd = sem("prelude_dve")
        s_ppe = sem("prelude_pe")
        s_ready = sem("weights_ready")
        s_b3 = sem("bias_parts_moved")
        s_put = sem("scatter_indices_ready")
        s_tabi = sem("edge_table_cleared")
        s_tabw = sem("edge_table_written")
        s_tabg = sem("edge_positions_gathered")
        s_ntg = sem("target_types_gathered")
        s_g = sem("source_rows_gathered")
        s_gd = sem("target_rows_gathered")
        s_sv = sem("x_rows_saved")
        s_out = sem("target_outputs_scattered")
        d_ld = sem("d_x_loaded")
        d_t = sem("d_transposed")
        d_xt = sem("d_xt_ready")
        d_h = sem("d_h_ready")
        d_ss = sem("d_squares_summed")
        d_std = sem("d_std_ready")
        d_xh = sem("d_normalised")
        d_var = sem("d_var_ready")
        d_p = sem("d_typed_ready")
        d_s0 = sem("d_type0_copied")
        d_sel = sem("d_selected")
        d_o = sem("d_out_ready")
        d_st = sem("d_stored")
        d_dve = sem("d_dve_steps")
        l_s = [sem(f"stage_source_{h}") for h in range(2)]
        l_d = [sem(f"stage_target_{h}") for h in range(2)]
        q_t = sem("q_transposed")
        q_xt = sem("q_xt_ready")
        q_h = sem("q_h_ready")
        q_ev = sem("q_source_h_out")
        q_ea = sem("q_target_h_out")
        q_st = [sem(f"q_h_stored_{h}") for h in range(2)]
        m_dve = sem("m_dve")
        m_act = sem("m_act")
        m_pe = sem("m_pe")
        m_log = sem("logit_weights_ready")
        p3 = sem("messages_written")
        l_h = [sem(f"target_h_loaded_{h}") for h in range(2)]
        r_dve = sem("r_dve")
        r_pe = sem("r_pe")
        r_act = sem("r_act")
        f_dve = sem("f_dve")
        f_sq = sem("f_squares_ready")
        f_y = sem("f_rows_ready")
        f_std = sem("f_std_ready")
        f_v = sem("f_sums_ready")
        f_out = sem("f_chunk_done")
        f_st = [sem(f"f_stored_{h}") for h in range(2)]
        l_x = [sem(f"x_chunks_loaded_{h}") for h in range(2)]
        v_t = sem("v_transposed")
        v_xt = sem("v_xt_ready")
        v_w = sem("v_messages_ready")
        v_m = sem("v_messages_masked")
        v_mt = sem("v_masked_transposed")
        v_mx = sem("v_masked_copied")
        v_v = sem("v_projected")
        v_s0 = sem("v_type0_copied")
        v_sel = sem("v_selected")
        v_put = sem("v_written")
        v_dve = sem("v_dve")
        l_v = [sem(f"v_staged_{h}") for h in range(2)]
        u_t = sem("u_transposed")
        u_xt = sem("u_xt_ready")
        u_p = sem("u_projected")
        u_s0 = sem("u_type0_copied")
        u_sel = sem("u_selected")
        u_dve = sem("u_dve")
        u_y = sem("u_rows_ready")
        u_sq = sem("u_squares_ready")
        u_v = sem("u_sums_ready")
        u_std = sem("u_std_ready")
        u_o = sem("u_out_ready")
        l_u = [sem(f"u_staged_{h}") for h in range(2)]

        def bc(ap, n):
            return ap.rearrange("p (a o) -> p a o", o=1).broadcast_to((ap.shape[0], ap.shape[1], n))

        def heads(ap, t0, n):
            v = ap[:, :, bass.ds(t0, n)].rearrange("p h (t o) -> p t h o", o=1)
            return v.broadcast_to((P, n, H, C))

        block = ctx.enter_context(nc.Block())

        @block.sync
        def _(sp):
            sp.dma_start(wraw[:, 0, :], W[0]).then_inc(s_w, 16)
            sp.dma_start(wraw[:, 1, :], W[1]).then_inc(s_w, 16)
            sp.dma_start(wraw[:, 2, :], W[2]).then_inc(s_w, 16)
            for l in range(3):
                sp.dma_start(av[:, 2 * l:2 * l + 1], A_S[l].rearrange("h (c o) -> (h c) o", o=1)).then_inc(s_w, 16)
                sp.dma_start(av[:, 2 * l + 1:2 * l + 2], A_D[l].rearrange("h (c o) -> (h c) o", o=1)).then_inc(s_w, 16)
            for l in range(2):
                for k in range(2):
                    sp.dma_start(gb[:, 2 * l + k:2 * l + k + 1],
                                 LN[l][k].rearrange("(c o) -> c o", o=1)).then_inc(s_w, 16)
            sp.dma_start(wnraw, WN.rearrange("n o k -> o n k")).then_inc(s_w, 16)
            sp.dma_start(weraw, WE.rearrange("n o k -> o n k")).then_inc(s_w, 16)
            sp.wait_ge(s_ms, 1)
            for l in range(3):
                for off in (BO[l], BCO[l]):
                    sp.dma_start(brow[:, off:off + D], B[l].rearrange("(o d) -> o d", o=1)).then_inc(s_w, 16)
            sp.dma_start(brow[:, BEO:BEO + 3 * D], BE.rearrange("(o n) d -> o (n d)", o=1)).then_inc(s_w, 16)
            sp.dma_start(brow[:, BNO:BNO + 3 * D], BN.rearrange("(o n) d -> o (n d)", o=1)).then_inc(s_w, 16)
            sp.dma_start(dx[:, :, :].rearrange("p r d -> p (r d)"), sblocks(x)[0, :, :]).then_inc(d_ld, 16)
            sp.wait_ge(s_ms, 2)
            sp.dma_start(edge_of.rearrange("(p r) o -> p (r o)", r=NS * R), types[0:N // (NS * R), :])\
                .then_inc(s_tabi, 16)
            sp.wait_ge(s_tabi, 16)
            sp.dma_start(types[:, 0:LAST * R].rearrange("p (i r) -> p i r", r=R),
                         ntype[0:LAST * SB].rearrange("(i p r) -> p i r", p=P, r=R)).then_inc(s_nt, 16)
            sp.dma_start(types[:, LAST * R:NS * R],
                         ntype[N - SB:N].rearrange("(p r) -> p r", r=R)).then_inc(s_nt, 16)
            sp.wait_ge(s_pd, 1)
            for k in range(3):
                sp.dma_start(bias3[k:k + 1, :], bpart[:, k, :]).then_inc(s_b3, 16)

            def dense(i):
                if not isinstance(i, int) or i < LAST:
                    nxt = tail_block(x) if isinstance(i, int) and i + 1 == LAST else sblocks(x)[i + 1, :, :]
                    sp.wait_ge(d_var, Q * i + Q)
                    sp.dma_start(dx[:, :, :].rearrange("p r d -> p (r d)"), nxt).then_inc(d_ld, 16)
                dest = tail_block(out) if isinstance(i, int) and i == LAST else sblocks(out)[i, :, :]
                sp.wait_ge(d_o, Q * i + Q)
                sp.dma_start(dest, dy[:, :, :].rearrange("p r d -> p (r d)")).then_inc(d_st, 16)

            def stage(buf, h):
                return buf[:, h * CH:(h + 1) * CH, :].rearrange("p r d -> p (r d)")

            def stage_rows(c, h, sems):
                sp.dma_start(stage(stg, h), rows[:, bass.ds(c * CH, CH), :].rearrange("p r d -> p (r d)"))\
                    .then_inc(sems[h], 16)

            def p1(l):
                n0 = l * T

                def body(i):
                    for h in range(2):
                        sp.wait_ge(q_t, n0 + i * TU + (h + 1) * CH)
                        stage_rows(2 * i + 2 + h, h, l_s)
                        sp.dma_start(stage(std_, h), chunks(table[l])[2 * i + 2 + h, :, :]).then_inc(l_d[h], 16)
                        sp.wait_ge(q_ea, n0 + i * TU + (h + 1) * CH)
                        sp.dma_start(chunks(hdd)[2 * i + h, :, :], stage(st3, h)).then_inc(q_st[h], 16)
                for h in range(2):
                    stage_rows(h, h, l_s)
                    sp.dma_start(stage(std_, h), chunks(table[l])[h, :, :]).then_inc(l_d[h], 16)
                run(sp, body, 0, IT - 1)
                for h in range(2):
                    sp.wait_ge(q_ea, n0 + (IT - 1) * TU + (h + 1) * CH)
                    sp.dma_start(chunks(hdd)[2 * (IT - 1) + h, :, :], stage(st3, h)).then_inc(q_st[h], 16)

            def load_h(l):
                c0 = l * 2 * IT

                def body(i):
                    for h in range(2):
                        sp.wait_ge(p3, c0 + 2 * i + h + 1)
                        sp.dma_start(stage(std_, h), chunks(hdd)[2 * i + 2 + h, :, :]).then_inc(l_h[h], 16)
                for h in range(2):
                    sp.wait_ge(q_st[0], (l + 1) * IT * 16)
                    sp.wait_ge(q_st[1], (l + 1) * IT * 16)
                    sp.dma_start(stage(std_, h), chunks(hdd)[h, :, :]).then_inc(l_h[h], 16)
                run(sp, body, 0, IT - 1)

            def finish(l):
                c0 = l * 2 * IT

                def load_x(c, h):
                    sp.dma_start(stage(std_, h), chunks(table[0])[c, :, :]).then_inc(l_x[h], 16)
                    sp.dma_start(stage(st3, h), chunks(src0)[c, :, :]).then_inc(l_x[h], 16)

                def body(i):
                    for h in range(2):
                        sp.wait_ge(f_out, c0 + 2 * i + h + 1)
                        if l == 2:
                            load_x(2 * i + 2 + h, h)
                        sp.dma_start(chunks(table[l + 1])[2 * i + h, :, :], stage(stg, h)).then_inc(f_st[h], 16)
                if l == 2:
                    sp.wait_ge(p3, (l + 1) * 2 * IT)
                    for h in range(2):
                        load_x(h, h)
                run(sp, body, 0, IT - 1 if l == 2 else IT)
                if l == 2:
                    for h in range(2):
                        sp.wait_ge(f_out, c0 + 2 * (IT - 1) + h + 1)
                        sp.dma_start(chunks(table[3])[2 * (IT - 1) + h, :, :], stage(stg, h)).then_inc(f_st[h], 16)

            def typed_messages():
                def body(i):
                    for h in range(2):
                        sp.wait_ge(v_t, i * TU + (h + 1) * CH)
                        stage_rows(2 * i + 2 + h, h, l_v)
                for h in range(2):
                    sp.wait_ge(f_st[h], 3 * IT * 16)
                    stage_rows(h, h, l_v)
                run(sp, body, 0, IT - 1)

            def typed_targets():
                def body(i):
                    for h in range(2):
                        sp.wait_ge(u_y, 2 * i + h + 1)
                        sp.dma_start(stage(std_, h), chunks(table[3])[2 * i + 2 + h, :, :]).then_inc(l_u[h], 16)
                for h in range(2):
                    sp.dma_start(stage(std_, h), chunks(table[3])[h, :, :]).then_inc(l_u[h], 16)
                run(sp, body, 0, IT - 1)

            run(sp, dense, CUTS[0], CUTS[1], (LAST - 1, LAST))
            for l in range(3):
                if l == 0:
                    sp.wait_ge(s_g, 16 * T)
                    sp.wait_ge(s_gd, 16 * T)
                    sp.dma_start(src0.rearrange("(p t) d -> p (t d)", p=P),
                                 rows[:, :, :].rearrange("p t d -> p (t d)")).then_inc(s_sv, 16)
                    sp.dma_start(table[0].rearrange("(p t) d -> p (t d)", p=P), msg[:, :]).then_inc(s_sv, 16)
                    sp.wait_ge(s_sv, 32)
                else:
                    sp.wait_ge(s_g, 16 * T * (l + 1))
                p1(l)
                load_h(l)
                finish(l)
                run(sp, dense, CUTS[l + 1], CUTS[l + 2] if l < 2 else CUTS[4], (LAST - 1, LAST))
            sp.wait_ge(s_g, 16 * T * 4)
            typed_messages()
            typed_targets()
            sp.wait_ge(d_st, 16 * NS)
            sp.wait_ge(s_out, 16 * T)

        @block.gpsimd
        def _(pool):
            pool.memset(ident[:, :], 0.0).then_inc(s_id, 1)
            pool.wait_ge(s_id, 1)
            pool.affine_select(out=ident[:, :], in_=ident[:, :], compare_op=ALU.not_equal, fill=1.0,
                               base=0, pattern=[[-1, P]], channel_multiplier=1).then_inc(s_id, 1)
            for n, (part, value) in enumerate(((dst_i[96:P, :, :], SKIP), (src_i[96:P, :], SKIP),
                                               (et_i[96:P, :], K3), (dst_i[0:1, 1, 0:1], -1))):
                pool.wait_ge(s_id, n + 2)
                pool.memset(part, value).then_inc(s_id, 1)
            pool.wait_ge(s_id, 6)
            flat = dst[0:FULL * T].rearrange("(p t) -> p t", t=T)
            pool.dma_start(dst_i[0:FULL, 0, :], flat).then_inc(s_i, 16)
            pool.dma_start(dst_i[FULL:P, 0, 0:TAIL], dst[FULL * T:E].rearrange("(o t) -> o t", o=1)).then_inc(s_i, 16)
            pool.dma_start(dst_i[0:1, 1, 1:T], dst[0:T - 1].rearrange("(o t) -> o t", o=1)).then_inc(s_i, 16)
            pool.dma_start(dst_i[1:FULL, 1, :], dst[T - 1:FULL * T - 1].rearrange("(p t) -> p t", t=T)).then_inc(s_i, 16)
            pool.dma_start(dst_i[FULL:P, 1, 0:TAIL + 1],
                           dst[FULL * T - 1:E].rearrange("(o t) -> o t", o=1)).then_inc(s_i, 16)
            pool.dma_start(dst_i[0:FULL, 2, :], dst[1:FULL * T + 1].rearrange("(p t) -> p t", t=T)).then_inc(s_i, 16)
            pool.dma_start(dst_i[FULL:P, 2, 0:TAIL - 1],
                           dst[FULL * T + 1:E].rearrange("(o t) -> o t", o=1)).then_inc(s_i, 16)
            pool.dma_start(src_i[0:FULL, :], src[0:FULL * T].rearrange("(p t) -> p t", t=T)).then_inc(s_i, 16)
            pool.dma_start(src_i[FULL:P, 0:TAIL], src[FULL * T:E].rearrange("(o t) -> o t", o=1)).then_inc(s_i, 16)
            pool.dma_start(et_i[0:FULL, :], etype[0:FULL * T].rearrange("(p t) -> p t", t=T)).then_inc(s_i, 16)
            pool.dma_start(et_i[FULL:P, 0:TAIL], etype[FULL * T:E].rearrange("(o t) -> o t", o=1)).then_inc(s_i, 16)
            pool.iota(eid[:, :], pattern=[[1, T]], base=0, channel_multiplier=T).then_inc(s_id, 1)
            pool.memset(pos_i[:, :], SKIP).then_inc(s_id, 1)
            pool.memset(nt_i[:, :], 0).then_inc(s_id, 1)
            pool.wait_ge(s_id, 9)
            pool.wait_ge(s_i, 16 * 11)
            pool.wait_ge(s_ms, 2)

            def gather(dest, tab, idx, done, bound):
                pool.indirect_dma_start(out=dest, out_offset=None, in_=tab,
                                        in_offset=bass.IndirectOffsetOnAxis(ap=idx, axis=0),
                                        bounds_check=bound, oob_is_err=False).then_inc(done, 16)

            for t in range(T):
                gather(rows[:, t, :], x, src_i[:, t:t + 1], s_g, N - 1)
            pool.wait_ge(s_b3, 48)
            pool.wait_ge(s_ready, 1)
            for t in range(T):
                gather(msg_r[:, t, :], x, dst_i[:, 0, t:t + 1], s_gd, N - 1)
            pool.wait_ge(s_put, 1)
            pool.wait_ge(s_tabi, 16)
            for t in range(T):
                pool.indirect_dma_start(out=edge_of, out_offset=bass.IndirectOffsetOnAxis(ap=put_i[:, t:t + 1], axis=0),
                                        in_=eid[:, t:t + 1], in_offset=None,
                                        bounds_check=N - 1, oob_is_err=False).then_inc(s_tabw, 16)
            ntab = ntype.rearrange("(n o) -> n o", o=1)
            for t in range(T):
                gather(nt_i[:, t:t + 1], ntab, dst_i[:, 0, t:t + 1], s_ntg, N - 1)
            pool.wait_ge(s_tabw, 16 * T)
            for t in range(T):
                gather(pos_i[:, t:t + 1], edge_of, src_i[:, t:t + 1], s_tabg, N - 1)
            pool.wait_ge(s_tabg, 16 * T)
            for l in range(1, 4):
                pool.wait_ge(f_out, l * 2 * IT)
                for h in range(2):
                    pool.wait_ge(f_st[h], 16 * l * IT)
                for t in range(T):
                    gather(rows[:, t, :], table[l], pos_i[:, t:t + 1], s_g, T * P - 1)
            pool.wait_ge(d_st, 16 * NS)
            for t in range(T):
                if t % CH == 0:
                    pool.wait_ge(u_o, t // CH + 1)
                pool.indirect_dma_start(out=out, out_offset=bass.IndirectOffsetOnAxis(ap=put_i[:, t:t + 1], axis=0),
                                        in_=rows[:, t, :], in_offset=None,
                                        bounds_check=N - 1, oob_is_err=False).then_inc(s_out, 16)
            pool.wait_ge(s_out, 16 * T)

        @block.tensor
        def _(pe):
            pe.wait_ge(s_w, 16 * 23)
            pe.wait_ge(s_id, 2)
            for l in range(3):
                if l:
                    pe.wait_ge(s_pd, 1 + 2 * l)
                pe.transpose(bank[:, 0, 0:P], wraw[:, l, :], ident[:, :]).then_inc(s_ppe, 1)
                pe.wait_ge(s_pd, 2 + 2 * l)
                pe.matmul(bank[:, 1, 0:2 * H], wtr, amat[:, :], start=True, stop=True).then_inc(s_ppe, 1)
            for j in range(4):
                for n in range(3):
                    pe.transpose(bank[:, 2 + j, n * D:(n + 1) * D], wnraw[:, n, j * D:(j + 1) * D], ident[:, :])
            for n in range(3):
                last = pe.transpose(bank[:, 6, n * D:(n + 1) * D], weraw[:, n, :], ident[:, :])
            last.then_inc(s_ppe, 1)
            pe.wait_ge(s_ready, 1)
            pe.wait_ge(s_b3, 48)

            def bias(dest, off, n, times, stop=True):
                src_ = bias3[:, off:off + n]
                if times > 1:
                    src_ = src_.rearrange("k (o n) -> k o n", o=1).broadcast_to((3, times, n))
                return pe.matmul(dest, ones3[:, :], src_, start=True, stop=stop)

            def dense(i):
                def turn(s, buf):
                    for q in range(Q):
                        if s:
                            pe.wait_ge(d_xh, i * 12 + (s - 1) * 4 + q + 1)
                        for j in range(G):
                            last = pe.transpose(bank[:, q, j * D:(j + 1) * D], buf[:, q * G + j, :], ident[:, :])
                        last.then_inc(d_t, 1)

                pe.wait_ge(d_ld, i * 16 + 16)
                for l in range(3):
                    turn(l, dx if l == 0 else dxh)
                    for q in range(Q):
                        pe.wait_ge(d_xt, i * 16 + l * 4 + q + 1)
                        bias(bank[:, q, :].rearrange("p (g d) -> p g d", g=G), BCO[l], D, G)
                        for j in range(G):
                            last = pe.matmul(bank[:, q, j * D:(j + 1) * D], dxt[:, q, j * D:(j + 1) * D],
                                             wcen[:, l, :], start=False, stop=True, skip_group_check=True)
                        last.then_inc(d_h, 1)
                turn(3, dxh)
                for q in range(Q):
                    pe.wait_ge(d_xt, i * 16 + 12 + q + 1)
                    for hh in range(2):
                        if not isinstance(i, int) or i * 8 + q * 2 + hh >= 2:
                            pe.wait_ge(d_sel, i * 8 + q * 2 + hh - 1)
                        for j in range(2 * hh, 2 * hh + 2):
                            bias(bank[:, 4 + j, 0:3 * D], BNO, 3 * D, 1)
                            last = pe.matmul(bank[:, 4 + j, 0:3 * D], dxt[:, q, j * D:(j + 1) * D],
                                             wnt[:, 0, :], start=False, stop=True, skip_group_check=True)
                        last.then_inc(d_p, 1)

            def p1(l):
                n0 = l * T

                pe.wait_ge(d_sel, 8 * CUTS[l + 1])

                def turn(i, tt):
                    n, h = n0 + i * TU + tt, tt // CH
                    if tt % CH == 0:
                        pe.wait_ge(l_s[h], 16 * (l * IT + i + 1))
                        pe.wait_ge(l_d[h], 16 * (l * IT + i + 1))
                    if not isinstance(n, int) or n >= 2:
                        pe.wait_ge(q_xt, n - 1)
                    pe.transpose(bank[:, tt % 2, 0:D], stg[:, tt, :], ident[:, :])
                    pe.transpose(bank[:, tt % 2, D:2 * D], std_[:, tt, :], ident[:, :]).then_inc(q_t, 1)

                def body(i):
                    turn(i, 0)
                    for tt in range(TU):
                        if tt + 1 < TU:
                            turn(i, tt + 1)
                        n = n0 + i * TU + tt
                        pe.wait_ge(q_xt, n + 1)
                        if not isinstance(n, int) or n >= 2:
                            pe.wait_ge(q_ev, n - 1)
                            pe.wait_ge(q_ea, n - 1)
                        for k in range(2):
                            o = bank[:, 2 + 2 * k + tt % 2, 0:WA]
                            bias(o, BO[l], WA, 1)
                            last = pe.matmul(o, xt2[:, tt % 2, k * D:(k + 1) * D], wall[:, l, :],
                                             start=False, stop=True, skip_group_check=True)
                        last.then_inc(q_h, 1)
                run(pe, body, 0, IT, (0,) if l == 0 else ())

            def logits(l):
                for n, k in enumerate((2, 0, 1) if l else (0, 1)):
                    pe.wait_ge(m_dve, MB[l] + 2 * n + 1)
                    pe.transpose(bank[0:H, 6, 0:P], sm[:, 2 * k, :], ident[:, :])
                    pe.transpose(bank[0:H, 6, P:2 * P], sm[:, 2 * k + 1, :], ident[:, :]).then_inc(m_pe, 1)
                    pe.wait_ge(m_dve, MB[l] + 2 * n + 2)
                    pe.transpose(bank[:, 7, 0:H], smb[:, :] if k == 2 else smo[:, 0:P], ident[0:H, 0:H])\
                        .then_inc(m_pe, 1)

            def carry(l):
                pe.wait_ge(r_dve, 2 * l + 1)
                pe.transpose(bank[:, 6, 0:P], rowa[:, 0, :], ident[:, :])
                pe.transpose(bank[:, 6, P:2 * P], rowa[:, 1, :], ident[:, :]).then_inc(r_pe, 1)
                pe.wait_ge(r_dve, 2 * l + 2)
                pe.transpose(bank[:, 7, 0:P], rowo[:, 0:P], ident[:, :]).then_inc(r_pe, 1)

            def typed_messages():
                pe.wait_ge(d_sel, 8 * NS)

                def turn(i, tt):
                    n, h = i * TU + tt, tt // CH
                    if tt % CH == 0:
                        pe.wait_ge(l_v[h], 16 * (i + 1))
                    if not isinstance(n, int) or n >= 2:
                        pe.wait_ge(v_xt, n - 1)
                    pe.transpose(bank[:, tt % 2, 0:D], stg[:, tt, :], ident[:, :]).then_inc(v_t, 1)

                def apply(i, tt):
                    n = i * TU + tt
                    pe.wait_ge(v_xt, n + 1)
                    if not isinstance(n, int) or n >= 2:
                        pe.wait_ge(v_m, n - 1)
                    bias(bank[:, 2 + tt % 2, 0:3 * D], BEO, 3 * D, 1)
                    pe.matmul(bank[:, 2 + tt % 2, 0:3 * D], xt2[:, tt % 2, 0:D], wet[:, :],
                              start=False, stop=True, skip_group_check=True).then_inc(v_w, 1)

                def project(i, tt):
                    n = i * TU + tt
                    pe.wait_ge(v_m, n + 1)
                    if not isinstance(n, int) or n >= 2:
                        pe.wait_ge(v_mx, n - 1)
                    for k in range(3):
                        last = pe.transpose(bank[:, 4 + tt % 2, k * D:(k + 1) * D],
                                            em[:, tt % 2, k * D:(k + 1) * D], ident[:, :])
                    last.then_inc(v_mt, 1)

                def project2(i, tt):
                    n = i * TU + tt
                    pe.wait_ge(v_mx, n + 1)
                    if not isinstance(n, int) or n >= 2:
                        pe.wait_ge(v_sel, n - 1)
                    for k in range(3):
                        last = pe.matmul(bank[:, 6 + tt % 2, 0:3 * D], emt[:, tt % 2, k * D:(k + 1) * D],
                                         wnt[:, 1 + k, :], start=(k == 0), stop=(k == 2))
                    last.then_inc(v_v, 1)

                def body(i):
                    turn(i, 0)
                    for tt in range(TU + 2):
                        if tt + 1 < TU:
                            turn(i, tt + 1)
                        if tt < TU:
                            apply(i, tt)
                        if 1 <= tt <= TU:
                            project(i, tt - 1)
                        if tt >= 2:
                            project2(i, tt - 2)
                run(pe, body, 0, IT, (0,))

            def typed_targets():
                def turn(i, tt):
                    n, h = i * TU + tt, tt // CH
                    if tt % CH == 0:
                        pe.wait_ge(l_u[h], 16 * (i + 1))
                    if not isinstance(n, int) or n >= 2:
                        pe.wait_ge(u_xt, n - 1)
                    pe.transpose(bank[:, tt % 2, 0:D], std_[:, tt, :], ident[:, :]).then_inc(u_t, 1)

                def body(i):
                    turn(i, 0)
                    for tt in range(TU):
                        if tt + 1 < TU:
                            turn(i, tt + 1)
                        n = i * TU + tt
                        pe.wait_ge(u_xt, n + 1)
                        if not isinstance(n, int) or n >= 2:
                            pe.wait_ge(u_sel, n - 1)
                        bias(bank[:, 2 + tt % 2, 0:3 * D], BNO, 3 * D, 1)
                        pe.matmul(bank[:, 2 + tt % 2, 0:3 * D], xt2[:, tt % 2, 0:D], wnt[:, 0, :],
                                  start=False, stop=True, skip_group_check=True).then_inc(u_p, 1)
                run(pe, body, 0, IT, (0,))

            run(pe, dense, CUTS[0], CUTS[1], (0,))
            for l in range(3):
                p1(l)
                logits(l)
                carry(l)
                run(pe, dense, CUTS[l + 1], CUTS[l + 2] if l < 2 else CUTS[4])
            typed_messages()
            carry(3)
            typed_targets()

        @block.scalar
        def _(act):
            act.wait_ge(s_ready, 1)
            act.wait_ge(s_ms, 2)

            def turned(dest, src_, s):
                if s in (1, 2):
                    return nc.scalar.activation(dest, src_, ACT.Relu, scale=gb[:, 2 * s - 2:2 * s - 1],
                                                bias=gb[:, 2 * s - 1:2 * s])
                return nc.scalar.activation(dest, src_, ACT.Relu if s == 3 else ACT.Copy)

            def dense(i):
                def turn(s):
                    for q in range(Q):
                        act.wait_ge(d_t, i * 16 + s * 4 + q + 1)
                        turned(dxt[:, q, :], bank[:, q, :], s).then_inc(d_xt, 1)

                def sums(k, q, tile):
                    s = (0, 1, 3)[k]
                    """The sum of squares of each row of a group, then its standard deviation."""
                    for j in range(G):
                        last = nc.scalar.activation(junk[:, j, :], tile(j), ACT.Square,
                                                    accum_out=dstd[:, s, q * G + j:q * G + j + 1])
                    last.then_inc(d_ss, 1)
                    act.wait_ge(d_ss, i * 12 + k * 4 + q + 1)
                    nc.scalar.activation(dstd[:, s, q * G:(q + 1) * G], dstd[:, s, q * G:(q + 1) * G], ACT.Sqrt,
                                         scale=1.0 / D, bias=eps[:, 0:1]).then_inc(d_std, 1)

                for l in range(2):
                    turn(l)
                    for q in range(Q):
                        act.wait_ge(d_h, i * 12 + l * 4 + q + 1)
                        sums(l, q, lambda j: bank[:, q, j * D:(j + 1) * D])
                turn(2)
                for q in range(Q):
                    act.wait_ge(d_var, i * 4 + q + 1)
                    nc.scalar.activation(dstd[:, 2, q * G:(q + 1) * G],
                                         dmv[:, q * G:(q + 1) * G, 1:2].rearrange("p g o -> p (g o)"),
                                         ACT.Sqrt, bias=eps[:, 0:1]).then_inc(d_std, 1)
                turn(3)
                for q in range(Q):
                    for hh in range(2):
                        n = i * 8 + q * 2 + hh
                        act.wait_ge(d_p, n + 1)
                        if not isinstance(n, int) or n >= 2:
                            act.wait_ge(d_sel, n - 1)
                        nc.scalar.activation(dsel[:, 2 * hh:2 * hh + 2, :],
                                             bank[:, 4 + 2 * hh:6 + 2 * hh, 0:D], ACT.Copy).then_inc(d_s0, 1)
                    if q:
                        act.wait_ge(d_sel, i * 8 + q * 2)
                        sums(2, q - 1, lambda j: dy[:, (q - 1) * G + j, :])
                act.wait_ge(d_sel, i * 8 + 8)
                sums(2, Q - 1, lambda j: dy[:, (Q - 1) * G + j, :])

            def p1(l):
                n0 = l * T

                def turn(i, tt):
                    n = n0 + i * TU + tt
                    act.wait_ge(q_t, n + 1)
                    if not isinstance(n, int) or n >= 2:
                        act.wait_ge(q_h, n - 1)
                    turned(xt2[:, tt % 2, :], bank[:, tt % 2, 0:2 * D], l).then_inc(q_xt, 1)

                def body(i):
                    turn(i, 0)
                    for tt in range(TU):
                        if tt + 1 < TU:
                            turn(i, tt + 1)
                        n, h = n0 + i * TU + tt, tt // CH
                        act.wait_ge(q_h, n + 1)
                        if tt % CH == 0 and (l or not isinstance(i, int) or i):
                            act.wait_ge(q_st[h], 16 * (l * IT + i))
                        nc.scalar.activation(st3[:, tt, :], bank[:, 4 + tt % 2, 0:D], ACT.Copy)
                        nc.scalar.activation(ld[:, bass.ds(i * TU + tt, 1), :],
                                             bank[:, 4 + tt % 2, D:D + 2 * H].rearrange("p (o n) -> p o n", o=1),
                                             ACT.Copy).then_inc(q_ea, 1)
                run(act, body, 0, IT, (0,) if l == 0 else ())

            def logits(l):
                for k in range(3):
                    act.wait_ge(m_log, 3 * l + k + 1)
                    buf = (ea, e_s, e_f)[k]
                    nc.scalar.activation(buf[:, :, :], buf[:, :, :], ACT.Exp).then_inc(m_act, 1)

            def finish(l):
                c0 = l * 2 * IT

                def body(i):
                    for h in range(2):
                        c = c0 + 2 * i + h
                        hs = slice(h * CH, (h + 1) * CH)
                        act.wait_ge(f_y, 2 * c + 1)
                        nc.scalar.activation(std_[:, hs, :], stg[:, hs, :], ACT.Square).then_inc(f_sq, 1)
                        act.wait_ge(f_y, 2 * c + 2)
                        nc.scalar.activation(st3[:, hs, :], rows[:, bass.ds((2 * i + h) * CH, CH), :],
                                             ACT.Square).then_inc(f_sq, 1)
                        act.wait_ge(f_v, c + 1)
                        nc.scalar.activation(csm[:, 0:2, hs], csm[:, 0:2, hs], ACT.Sqrt,
                                             scale=1.0 / D, bias=eps[:, 0:1]).then_inc(f_std, 1)
                run(act, body, 0, IT)

            def typed_messages():
                def turn(i, tt):
                    n = i * TU + tt
                    act.wait_ge(v_t, n + 1)
                    if not isinstance(n, int) or n >= 2:
                        act.wait_ge(v_w, n - 1)
                    turned(xt2[:, tt % 2, 0:D], bank[:, tt % 2, 0:D], 0).then_inc(v_xt, 1)

                def mask(i, tt):
                    n = i * TU + tt
                    act.wait_ge(v_w, n + 1)
                    if not isinstance(n, int) or n >= 2:
                        act.wait_ge(v_mt, n - 1)
                    for k in range(3):
                        last = nc.scalar.activation(em[:, tt % 2, k * D:(k + 1) * D],
                                                    bank[:, 2 + tt % 2, k * D:(k + 1) * D], ACT.Relu,
                                                    scale=etm[:, k, bass.ds(i * TU + tt, 1)])
                    last.then_inc(v_m, 1)

                def copy0(i, tt):
                    n = i * TU + tt
                    act.wait_ge(v_v, n + 1)
                    if not isinstance(n, int) or n >= 2:
                        act.wait_ge(v_put, n - 1)
                    nc.scalar.activation(ev[:, tt % 2, :], bank[:, 6 + tt % 2, 0:D], ACT.Copy).then_inc(v_s0, 1)

                def body(i):
                    turn(i, 0)
                    for tt in range(TU + 2):
                        if tt + 1 < TU:
                            turn(i, tt + 1)
                        if tt < TU:
                            mask(i, tt)
                        if tt >= 2:
                            copy0(i, tt - 2)
                run(act, body, 0, IT, (0,))

            def typed_targets():
                def turn(i, tt):
                    n = i * TU + tt
                    act.wait_ge(u_t, n + 1)
                    if not isinstance(n, int) or n >= 2:
                        act.wait_ge(u_p, n - 1)
                    turned(xt2[:, tt % 2, 0:D], bank[:, tt % 2, 0:D], 3).then_inc(u_xt, 1)

                def squares(i, h):
                    hs = slice(h * CH, (h + 1) * CH)
                    act.wait_ge(u_y, 2 * i + h + 1)
                    nc.scalar.activation(st3[:, hs, :], stg[:, hs, :], ACT.Square).then_inc(u_sq, 1)
                    act.wait_ge(u_v, 2 * i + h + 1)
                    nc.scalar.activation(csm[:, 0, hs], csm[:, 0, hs], ACT.Sqrt,
                                         scale=1.0 / D, bias=eps[:, 0:1]).then_inc(u_std, 1)

                def body(i):
                    turn(i, 0)
                    for tt in range(TU):
                        if tt + 1 < TU:
                            turn(i, tt + 1)
                        n = i * TU + tt
                        act.wait_ge(u_p, n + 1)
                        if tt % CH == 0 and (not isinstance(i, int) or i):
                            act.wait_ge(u_o, 2 * i + tt // CH - 1)
                        nc.scalar.activation(stg[:, tt, :], bank[:, 2 + tt % 2, 0:D], ACT.Copy).then_inc(u_s0, 1)
                        if tt == CH:
                            squares(i, 0)
                    squares(i, 1)
                run(act, body, 0, IT, (0,))

            run(act, dense, CUTS[0], CUTS[1], (0,))
            for l in range(3):
                p1(l)
                logits(l)
                finish(l)
                run(act, dense, CUTS[l + 1], CUTS[l + 2] if l < 2 else CUTS[4])
            act.wait_ge(m_log, 10)
            typed_messages()
            typed_targets()

        @block.vector
        def _(dve):
            v = nc.vector
            st = Steps(dve, d_dve)
            cut = [0]
            v.memset(brow[:, :], 0.0).then_inc(s_ms, 1)
            v.memset(eps[:, :], EPS)
            v.memset(ones3[:, :], 1.0)
            v.memset(zero[:, :], 0.0)
            v.memset(types[:, :], SKIP)
            v.memset(smo[:, 0:1], -BIG)
            v.memset(rowo[:, 0:1], 0.0)
            v.memset(hm[:, :], 0.0)
            last = v.memset(rows[96:P, TAIL:T, :], 0.0)
            last.then_inc(s_ms, 1)
            dve.wait_ge(s_ms, 2)
            for h in range(H):
                v.memset(hm[h * C:(h + 1) * C, h:h + 1], 1.0)
            dve.wait_ge(s_w, 16 * 23)
            cent = [(BCO[0], 1), (BCO[1], 1), (BNO, 3)]
            k = 0
            for off, n in cent:
                st.did(v.tensor_reduce(bmean[:, k:k + n], brow[:, off:off + n * D].rearrange("o (n d) -> o n d", n=n),
                                       AX_X, ALU.add))
                st.did(v.tensor_scalar(bmean[:, k:k + n], bmean[:, k:k + n], 1.0 / D, None, ALU.mult))
                w3 = brow[:, off:off + n * D].rearrange("o (n d) -> o n d", n=n)
                st.did(v.tensor_tensor(w3, w3, bc(bmean[:, k:k + n], D), ALU.subtract))
                if n == 1:
                    v.tensor_copy(brow[:, BO[k] + D + 2 * H:BO[k] + WA], bmean[:, k:k + 1])
                k += n
            st.did(v.tensor_copy(bpart[:, 0, :], brow[:, :]))
            st.did(v.tensor_tensor(brest[:, :], brow[:, :], bpart[:, 0, :], ALU.subtract))
            st.did(v.tensor_copy(bpart[:, 1, :], brest[:, :]))
            st.did(v.tensor_tensor(brest[:, :], brest[:, :], bpart[:, 1, :], ALU.subtract))
            v.tensor_copy(bpart[:, 2, :], brest[:, :]).then_inc(s_pd, 1)
            for l in range(3):
                for k in range(2):
                    last = v.tensor_scalar(amat[:, k * H:(k + 1) * H], hm[:, :], av[:, 2 * l + k:2 * l + k + 1],
                                           None, ALU.mult)
                st.did(last)
                dve.wait_ge(s_ppe, 2 * l + 1)
                v.tensor_copy(wtr, bank[:, 0, 0:P]).then_inc(s_pd, 1)
                v.tensor_copy(wall[:, l, 0:D], wraw[:, l, :])
                st.did(v.tensor_reduce(wmean[:, l:l + 1], wraw[:, l, :], AX_X, ALU.add))
                st.did(v.tensor_scalar(wmean[:, l:l + 1], wmean[:, l:l + 1], 1.0 / D, None, ALU.mult))
                v.tensor_copy(wall[:, l, D + 2 * H:WA], wmean[:, l:l + 1])
                if l < 2:
                    v.tensor_scalar(wcen[:, l, :], wraw[:, l, :], wmean[:, l:l + 1], None, ALU.subtract)
                else:
                    v.tensor_copy(wcen[:, l, :], wraw[:, l, :])
                dve.wait_ge(s_ppe, 2 * l + 2)
                v.tensor_copy(wall[:, l, D:D + 2 * H], bank[:, 1, 0:2 * H]).then_inc(s_pd, 1)
            dve.wait_ge(s_ppe, 7)
            w3 = wnt[:, :, :].rearrange("p j (n o) -> p (j n) o", n=3)
            for j in range(4):
                last = v.tensor_copy(wnt[:, j, :], bank[:, 2 + j, 0:3 * D])
            st.did(last)
            st.did(v.tensor_reduce(wmean[:, 4:16], w3, AX_X, ALU.add))
            st.did(v.tensor_scalar(wmean[:, 4:16], wmean[:, 4:16], 1.0 / D, None, ALU.mult))
            st.did(v.tensor_tensor(w3, w3, bc(wmean[:, 4:16], D), ALU.subtract))
            st.did(v.tensor_copy(wet[:, :], bank[:, 6, 0:3 * D]))
            v.memset(msg_r[96:P, TAIL:T, :], 0.0).then_inc(s_ready, 1)
            dve.wait_ge(s_i, 16 * 11)
            dve.wait_ge(s_id, 6)
            st.did(v.tensor_copy(dst_f[:, :, :], dst_i[:, :, :]))
            v.tensor_tensor(ns[:, :], dst_f[:, 0, :], dst_f[:, 1, :], ALU.not_equal)
            st.did(v.tensor_tensor(lastf[:, :], dst_f[:, 0, :], dst_f[:, 2, :], ALU.not_equal))
            v.tensor_scalar(negns[:, :], ns[:, :], -BIG, None, ALU.mult)
            v.tensor_scalar(keep[:, :], ns[:, :], -1.0, 1.0, ALU.mult, ALU.add)
            v.tensor_scalar(unlast[:, :], lastf[:, :], BIG, -BIG, ALU.mult, ALU.add)
            v.tensor_copy(last_r[:, :], lastf[:, ::-1])
            st.did(v.tensor_scalar(more_r[:, :], lastf[:, ::-1], -1.0, 1.0, ALU.mult, ALU.add))
            st.did(v.tensor_tensor_scan(none_r[:, :], more_r[:, :], zero[:, :], 1.0, ALU.mult, ALU.add))
            st.did(v.tensor_scalar(lastf[:, :], lastf[:, :], -float(SKIP), float(SKIP), ALU.mult, ALU.add))
            st.did(v.tensor_tensor(lastf[:, :], lastf[:, :], dst_f[:, 0, :], ALU.add))
            v.tensor_copy(put_i[:, :], lastf[:, :]).then_inc(s_put, 1)
            st.did(v.tensor_tensor_scan(kept[:, :], ns[:, :], ns[:, :], 0.0, ALU.max, ALU.max))
            st.did(v.tensor_scalar(negseen[:, :], kept[:, :], -BIG, None, ALU.mult))
            st.did(v.tensor_scalar(kept[:, :], kept[:, :], -1.0, 1.0, ALU.mult, ALU.add))
            dve.wait_ge(s_nt, 32)

            met = (s_ms, 2)

            def dense(i):
                DP = 40
                st.enter(i - cut[0], DP)
                for k in range(2):
                    v.tensor_scalar(dmk[:, k, :], types[:, bass.ds(i * R, R)], float(k + 1), None, ALU.is_equal)

                def rstd(q, s):
                    dve.wait_ge(d_std, i * 16 + s * 4 + q + 1)
                    st.did(v.reciprocal(drs[:, s, q * G:(q + 1) * G], dstd[:, s, q * G:(q + 1) * G]))

                for l in range(2):
                    for q in range(Q):
                        rstd(q, l)
                        v.tensor_tensor(dxh[:, q * G:(q + 1) * G, :],
                                        bank[:, q, :].rearrange("p (g d) -> p g d", g=G),
                                        bc(drs[:, l, q * G:(q + 1) * G], D), ALU.mult).then_inc(d_xh, 1)
                for q in range(Q):
                    g = slice(q * G, (q + 1) * G)
                    dve.wait_ge(d_h, i * 12 + 8 + q + 1)
                    ins = v.tensor_tensor(dxh[:, g, :], bank[:, q, :].rearrange("p (g d) -> p g d", g=G),
                                          dx[:, g, :], ALU.add)
                    st.did(ins)
                    for j in range(G):
                        last = v.bn_stats(dst6[:, q * G + j, :], dxh[:, q * G + j, :])
                    st.did(last, met)
                    for j in range(G):
                        last = v.bn_aggr(dmv[:, q * G + j, :], dst6[:, q * G + j, :])
                    last.then_inc(d_var, 1)
                for q in range(Q):
                    rstd(q, 2)
                    for j in range(q * G, (q + 1) * G):
                        last = v.tensor_scalar(dxh[:, j, :], dxh[:, j, :], dmv[:, j, 0:1], drs[:, 2, j:j + 1],
                                               ALU.subtract, ALU.mult)
                    last.then_inc(d_xh, 1)
                if not isinstance(i, int) or i:
                    dve.wait_ge(d_st, i * 16)

                def norm(q):
                    rstd(q, 3)
                    g = slice(q * G, (q + 1) * G)
                    v.tensor_tensor(dy[:, g, :], dy[:, g, :], bc(drs[:, 3, g], D), ALU.mult).then_inc(d_o, 1)

                for q in range(Q):
                    for hh in range(2):
                        n = i * 8 + q * 2 + hh
                        g = slice(q * G + 2 * hh, q * G + 2 * hh + 2)
                        st.wait(d_s0, n + 1, met)
                        sel = dsel[:, 2 * hh:2 * hh + 2, :]
                        for k in range(2):
                            st.did(v.copy_predicated(sel, bc(dmk[:, k, g], D),
                                                     bank[:, 4 + 2 * hh:6 + 2 * hh, (k + 1) * D:(k + 2) * D]), met)
                        v.scalar_tensor_tensor(out=dy[:, g, :], in0=dxh[:, g, :], scalar=2.0, in1=sel,
                                               op0=ALU.mult, op1=ALU.add).then_inc(d_sel, 1)
                    if q:
                        norm(q - 1)
                norm(Q - 1)
                assert st.c == DP, st.c

            def run_dense(lo, hi, peel=()):
                cut[0] = lo
                leave = st.loop(hi - lo, 40)
                run(dve, dense, lo, hi, peel)
                leave()

            def p1(l):
                n0 = l * T

                def body(i):
                    for tt in range(TU):
                        n = n0 + i * TU + tt
                        b = bank[:, 2 + tt % 2, :].rearrange("p (o n) -> p o n", o=1)
                        dve.wait_ge(q_h, n + 1)
                        v.tensor_copy(rows[:, bass.ds(i * TU + tt, 1), :], b[:, :, 0:D])
                        v.tensor_copy(ls[:, bass.ds(i * TU + tt, 1), :], b[:, :, D:WA]).then_inc(q_ev, 1)
                run(dve, body, 0, IT)

            def logits(l):
                def lrelu(dest, a_, b_):
                    st.did(v.tensor_tensor(dest[:, :, :], a_, b_, ALU.add))
                    st.did(v.scalar_tensor_tensor(out=dest[:, :, :], in0=dest[:, :, :], scalar=NEG_SLOPE,
                                                  in1=dest[:, :, :], op0=ALU.mult, op1=ALU.max))
                lsv, ldv = (b[:, :, :].rearrange("p t h -> p h t") for b in (ls, ld))
                dve.wait_ge(q_ea, (l + 1) * T)
                dve.wait_ge(q_ev, (l + 1) * T)
                pe0 = MB[l]
                row = (lambda z: z[:, :].rearrange("p (o t) -> p o t", o=1).broadcast_to((P, H, T)))
                of_target = ldv[:, H:2 * H, :]
                if l:
                    st.did(v.tensor_tensor(fm[:, :, :], ldv[:, H:2 * H, ::-1], row(last_r), ALU.mult))
                    for h in range(H):
                        last = v.tensor_tensor_scan(fm[:, h, :], more_r[:, :], fm[:, h, :], 0.0, ALU.mult, ALU.add)
                    st.did(last)
                    v.tensor_copy(sm[:, 4, :], none_r[:, T - 1:T].broadcast_to((P, H)))
                    v.tensor_copy(sm[:, 5, :], fm[:, :, T - 1:T].rearrange("p h o -> p (h o)")).then_inc(m_dve, 1)
                    dve.wait_ge(m_pe, pe0 + 1)
                    v.memset(smo[:, 0:1], 0.0)
                    st.did(v.tensor_copy(smr[:, :, :], bank[0:H, 6, 0:2 * P]
                                         .rearrange("h (k p) -> h k p", k=2)[:, :, ::-1]))
                    st.did(v.tensor_tensor_scan(smo[:, 1:P + 1], smr[:, 0, :], smr[:, 1, :], 0.0,
                                                ALU.mult, ALU.add))
                    v.tensor_copy(smb[:, :], smo[:, P - 1::-1]).then_inc(m_dve, 1)
                    dve.wait_ge(m_pe, pe0 + 2)
                    st.did(v.tensor_copy(ci[:, :], bank[:, 7, 0:H]))
                    for h in range(H):
                        last = v.scalar_tensor_tensor(out=fm[:, h, :], in0=none_r[:, :], scalar=ci[:, h:h + 1],
                                                      in1=fm[:, h, :], op0=ALU.mult, op1=ALU.add)
                    st.did(last)
                    of_target = fm[:, :, ::-1]
                    pe0 += 2
                lrelu(e_s, lsv[:, 0:H, :], of_target)
                lrelu(e_f, ldv[:, 0:H, :], ldv[:, H:2 * H, :])
                st.did(v.tensor_tensor(e_f[:, :, :], e_f[:, :, :], row(unlast), ALU.add))
                st.did(v.tensor_tensor(fm[:, :, :], e_s[:, :, :], e_f[:, :, :], ALU.max))
                for h in range(H):
                    last = v.tensor_tensor_scan(fm[:, h, :], negns[:, :], fm[:, h, :], -BIG, ALU.add, ALU.max)
                st.did(last)
                v.tensor_copy(sm[:, 0, :], negseen[:, T - 1:T].broadcast_to((P, H)))
                v.tensor_copy(sm[:, 1, :], fm[:, :, T - 1:T].rearrange("p h o -> p (h o)")).then_inc(m_dve, 1)
                dve.wait_ge(m_pe, pe0 + 1)
                st.did(v.tensor_copy(smr[:, :, :], bank[0:H, 6, 0:2 * P].rearrange("h (k p) -> h k p", k=2)))
                if l:
                    st.did(v.memset(smo[:, 0:1], -BIG))
                v.tensor_tensor_scan(smo[:, 1:P + 1], smr[:, 0, :], smr[:, 1, :], -BIG, ALU.add, ALU.max)\
                    .then_inc(m_dve, 1)
                dve.wait_ge(m_pe, pe0 + 2)
                st.did(v.tensor_copy(ci[:, :], bank[:, 7, 0:H]))
                v.tensor_copy(mp[:, :, 0:1].rearrange("p h o -> p (h o)"), ci[:, :])
                for h in range(H):
                    last = v.scalar_tensor_tensor(out=mp[:, h, 1:T + 1], in0=negseen[:, :], scalar=ci[:, h:h + 1],
                                                  in1=fm[:, h, :], op0=ALU.add, op1=ALU.max)
                st.did(last)
                m = mp[:, :, 1:T + 1]
                st.did(v.tensor_tensor(ea[:, :, :], mp[:, :, 0:T], m, ALU.subtract))
                v.tensor_tensor(ea[:, :, :], ea[:, :, :], row(negns), ALU.add).then_inc(m_log, 1)
                v.tensor_tensor(e_s[:, :, :], e_s[:, :, :], m, ALU.subtract).then_inc(m_log, 1)
                v.tensor_tensor(e_f[:, :, :], e_f[:, :, :], m, ALU.subtract).then_inc(m_log, 1)
                dve.wait_ge(m_act, 3 * l + 3)
                st.did(v.tensor_tensor(es[:, :, :], e_s[:, :, :], e_f[:, :, :], ALU.add))
                for h in range(H):
                    v.tensor_tensor_scan(es[:, h, :], ea[:, h, :], es[:, h, :], 0.0, ALU.mult, ALU.add)
                    last = v.tensor_tensor_scan(ep[:, h, :], ea[:, h, :], zero[:, :], 1.0, ALU.mult, ALU.add)
                st.did(last)
                v.tensor_copy(sm[:, 2, :], ep[:, :, T - 1:T].rearrange("p h o -> p (h o)"))
                v.tensor_copy(sm[:, 3, :], es[:, :, T - 1:T].rearrange("p h o -> p (h o)")).then_inc(m_dve, 1)
                dve.wait_ge(m_pe, pe0 + 3)
                v.memset(smo[:, 0:1], 0.0)
                st.did(v.tensor_copy(smr[:, :, :], bank[0:H, 6, 0:2 * P].rearrange("h (k p) -> h k p", k=2)))
                v.tensor_tensor_scan(smo[:, 1:P + 1], smr[:, 0, :], smr[:, 1, :], 0.0, ALU.mult, ALU.add)\
                    .then_inc(m_dve, 1)
                dve.wait_ge(m_pe, pe0 + 4)
                st.did(v.tensor_copy(ci[:, :], bank[:, 7, 0:H]))
                for h in range(H):
                    last = v.scalar_tensor_tensor(out=es[:, h, :], in0=ep[:, h, :], scalar=ci[:, h:h + 1],
                                                  in1=es[:, h, :], op0=ALU.mult, op1=ALU.add)
                st.did(last)
                st.did(v.reciprocal(es[:, :, :], es[:, :, :]))

            def messages(l):
                def body(i):
                    st.enter(i, 2)
                    for h in range(2):
                        t0 = (2 * i + h) * CH
                        hs = std_[:, h * CH:(h + 1) * CH, :].rearrange("p t (h c) -> p t h c", h=H)
                        dest = msg_f[:, :, bass.ds(t0, CH)].rearrange("p (h c) t -> p t h c", h=H)
                        dve.wait_ge(l_h[h], 16 * (l * IT + i + 1))
                        v.tensor_tensor(dest, rows[:, bass.ds(t0, CH), :].rearrange("p t (h c) -> p t h c", h=H),
                                        heads(e_s, t0, CH), ALU.mult)
                        st.did(v.tensor_tensor(hs, hs, heads(e_f, t0, CH), ALU.mult))
                        d2 = msg_f[:, :, bass.ds(t0, CH)].rearrange("p f t -> p t f")
                        ins = v.tensor_tensor(d2, d2, std_[:, h * CH:(h + 1) * CH, :], ALU.add)
                        ins.then_inc(p3, 1)
                leave = st.loop(IT, 2)
                run(dve, body, 0, IT)
                leave()

            def scans(l, a_of, p_of):
                if l < 3:
                    dve.wait_ge(p3, (l + 1) * 2 * IT)
                else:
                    dve.wait_ge(v_put, T)

                def scan(i):
                    for h in range(H):
                        f = msg_f[:, i + h * C, :]
                        last = v.tensor_tensor_scan(f, a_of(h), f, 0.0, ALU.mult, ALU.add)
                    return last
                with dve.Fori(0, C - 1) as i:
                    scan(i)
                st.did(scan(C - 1))
                for h in range(H):
                    v.tensor_copy(rowa[:, 0, h * C:(h + 1) * C], p_of(h)[:, T - 1:T].broadcast_to((P, C)))
                v.tensor_copy(rowa[:, 1, :], msg_f[:, :, T - 1:T].rearrange("p f o -> p (f o)")).then_inc(r_dve, 1)
                dve.wait_ge(r_pe, 2 * l + 1)
                st.did(v.tensor_copy(rowt[:, :, :], bank[:, 6, 0:2 * P].rearrange("f (k p) -> f k p", k=2)))
                v.tensor_tensor_scan(rowo[:, 1:P + 1], rowt[:, 0, :], rowt[:, 1, :], 0.0, ALU.mult, ALU.add)\
                    .then_inc(r_dve, 1)
                dve.wait_ge(r_pe, 2 * l + 2)
                st.did(v.tensor_copy(cin[:, :], bank[:, 7, 0:P]))

                def fix(i):
                    for h in range(H):
                        f = msg_f[:, i + h * C, :]
                        last = v.scalar_tensor_tensor(out=f, in0=p_of(h), scalar=cin[:, bass.ds(i + h * C, 1)],
                                                      in1=f, op0=ALU.mult, op1=ALU.add)
                    return last
                with dve.Fori(0, C - 1) as i:
                    fix(i)
                st.did(fix(C - 1))

            def finish(l):
                c0 = l * 2 * IT

                def body(i):
                    DP = 16 if l == 2 else 8
                    st.enter(i, DP)
                    for h in range(2):
                        c = c0 + 2 * i + h
                        t0 = (2 * i + h) * CH
                        hs = slice(h * CH, (h + 1) * CH)
                        if l or not isinstance(i, int) or i:
                            dve.wait_ge(f_st[h], 16 * (l * IT + i))
                        o = stg[:, hs, :]
                        r = rows[:, bass.ds(t0, CH), :]
                        ins = v.tensor_tensor(o.rearrange("p t (h c) -> p t h c", h=H),
                                              msg_f[:, :, bass.ds(t0, CH)].rearrange("p (h c) t -> p t h c", h=H),
                                              heads(es, t0, CH), ALU.mult)
                        st.did(ins)
                        todo = [(o, std_[:, hs, :], 2)]
                        if l == 2:
                            dve.wait_ge(l_x[h], 32 * (i + 1))
                            todo.append((r, st3[:, hs, :], 3))
                        for y, xx, k in todo:
                            m = csm[:, k, hs]
                            if l == 2:
                                st.did(v.tensor_tensor(y, y, xx, ALU.add), met)
                            st.did(v.tensor_reduce(m, y, AX_X, ALU.add))
                            st.did(v.tensor_scalar(m, m, 1.0 / D, None, ALU.mult))
                            v.tensor_tensor(y, y, bc(m, D), ALU.subtract).then_inc(f_y, 1)
                            if l == 2:
                                dve.wait_ge(f_y, 2 * c + k - 1)
                        if l < 2:
                            v.tensor_tensor(r, r, ls[:, bass.ds(t0, CH), 2 * H:2 * H + 1].broadcast_to((P, CH, D)),
                                            ALU.subtract).then_inc(f_y, 1)
                            dve.wait_ge(f_y, 2 * c + 2)
                        for k, z in ((0, std_), (1, st3)):
                            dve.wait_ge(f_sq, 2 * c + k + 1)
                            last = v.tensor_reduce(csm[:, k, hs], z[:, hs, :], AX_X, ALU.add)
                        last.then_inc(f_v, 1)
                        dve.wait_ge(f_std, c + 1)
                        st.did(v.reciprocal(csm[:, 4:6, hs], csm[:, 0:2, hs]))
                        v.tensor_tensor(o, o, bc(csm[:, 4, hs], D), ALU.mult)
                        v.tensor_tensor(r, r, bc(csm[:, 5, hs], D), ALU.mult).then_inc(f_out, 1)
                    assert st.c == DP, st.c
                leave = st.loop(IT, 16 if l == 2 else 8)
                run(dve, body, 0, IT, (0,) if l == 0 else ())
                leave()

            def typed_messages():
                def copy_t(i, tt):
                    n = i * TU + tt
                    dve.wait_ge(v_mt, n + 1)
                    if not isinstance(n, int) or n >= 2:
                        dve.wait_ge(v_v, n - 1)
                    v.tensor_copy(emt[:, tt % 2, :], bank[:, 4 + tt % 2, 0:3 * D]).then_inc(v_mx, 1)

                def select(i, tt):
                    n = i * TU + tt
                    st.wait(v_s0, n + 1, met)
                    st.did(v.copy_predicated(ev[:, tt % 2, :], ntc[:, 0, tt:tt + 1].broadcast_to((P, D)),
                                             bank[:, 6 + tt % 2, D:2 * D]), met)
                    v.copy_predicated(ev[:, tt % 2, :], ntc[:, 1, tt:tt + 1].broadcast_to((P, D)),
                                      bank[:, 6 + tt % 2, 2 * D:3 * D]).then_inc(v_sel, 1)
                    dve.wait_ge(v_sel, n + 1)
                    v.tensor_copy(msg_f[:, :, bass.ds(i * TU + tt, 1)].rearrange("p f o -> p (f o)"),
                                  ev[:, tt % 2, :]).then_inc(v_put, 1)

                def body(i):
                    DP = 1 + TU
                    st.enter(i, DP)
                    st.did(v.tensor_copy(ntc[:, :, :], ntm[:, :, bass.ds(i * TU, TU)]))
                    for tt in range(TU + 1):
                        if tt < TU:
                            copy_t(i, tt)
                        if tt >= 1:
                            select(i, tt - 1)
                    assert st.c == DP
                leave = st.loop(IT, 1 + TU)
                run(dve, body, 0, IT, (0,))
                leave()

            def typed_targets():
                def chunk(i, h):
                    c = 2 * i + h
                    hs = slice(h * CH, (h + 1) * CH)
                    o = stg[:, hs, :]
                    st.did(v.scalar_tensor_tensor(out=o, in0=std_[:, hs, :], scalar=2.0, in1=o,
                                                  op0=ALU.mult, op1=ALU.add))
                    v.tensor_tensor(o, o, msg_f[:, :, bass.ds(c * CH, CH)].rearrange("p f t -> p t f"),
                                    ALU.add).then_inc(u_y, 1)
                    dve.wait_ge(u_sq, c + 1)
                    v.tensor_reduce(csm[:, 0, hs], st3[:, hs, :], AX_X, ALU.add).then_inc(u_v, 1)
                    dve.wait_ge(u_std, c + 1)
                    st.did(v.reciprocal(csm[:, 4, hs], csm[:, 0, hs]))
                    v.tensor_tensor(rows[:, bass.ds(c * CH, CH), :], o, bc(csm[:, 4, hs], D), ALU.mult)\
                        .then_inc(u_o, 1)

                def body(i):
                    DP = 1 + TU + 4
                    st.enter(i, DP)
                    st.did(v.tensor_copy(ntc[:, :, :], ntm[:, :, bass.ds(i * TU, TU)]))
                    for tt in range(TU):
                        n = i * TU + tt
                        st.wait(u_s0, n + 1, met)
                        for k in range(2):
                            ins = v.copy_predicated(stg[:, tt, :], ntc[:, k, tt:tt + 1].broadcast_to((P, D)),
                                                    bank[:, 2 + tt % 2, (k + 1) * D:(k + 2) * D])
                            if k == 0:
                                st.did(ins, met)
                        ins.then_inc(u_sel, 1)
                        if tt % CH == CH - 1:
                            dve.wait_ge(u_sel, n + 1)
                            chunk(i, tt // CH)
                    assert st.c == DP
                leave = st.loop(IT, 1 + TU + 4)
                run(dve, body, 0, IT, (0,))
                leave()

            run_dense(CUTS[0], CUTS[1], (0,))
            for l in range(3):
                if l == 0:
                    dve.wait_ge(s_sv, 32)
                p1(l)
                logits(l)
                messages(l)
                scans(l, lambda h: ea[:, h, :], lambda h: ep[:, h, :])
                finish(l)
                run_dense(CUTS[l + 1], CUTS[l + 2] if l < 2 else CUTS[4])
            for k in range(K3):
                last = v.tensor_scalar(etm[:, k, :], et_i[:, :], float(k), None, ALU.is_equal)
            last.then_inc(m_log, 1)
            dve.wait_ge(s_ntg, 16 * T)
            for k in range(2):
                last = v.tensor_scalar(ntm[:, k, :], nt_i[:, :], float(k + 1), None, ALU.is_equal)
            st.did(last)
            typed_messages()
            scans(3, lambda h: keep[:, :], lambda h: kept[:, :])
            typed_targets()


_INS = ["x", "src", "dst", "edge_type_3", "node_type_3",
        *(f"L0_gnn_{n}{l}" for l in range(3) for n in ("W", "a_src", "a_dst", "b")),
        "L0_gnn_ln0_g", "L0_gnn_ln0_b", "L0_gnn_ln1_g", "L0_gnn_ln1_b",
        "L1_gnn_W_e", "L1_gnn_b_e", "L1_gnn_W_n", "L1_gnn_b_n"]


def kernel(**inputs):
    import numpy as _np
    import concourse.bacc as _bacc
    from concourse import mybir as _mybir
    from concourse.bass_utils import run_bass_kernel_spmd as _run

    nc = _bacc.Bacc("TRN2", target_bir_lowering=False, num_devices=1)
    arrays, aps = {}, {}
    for name in _INS:
        v = _np.ascontiguousarray(inputs[name])
        arrays[f"in_{name}_dram"] = v
        aps[name] = nc.dram_tensor(f"in_{name}_dram", v.shape, _mybir.dt.from_np(v.dtype), kind="ExternalInput").ap()
    shape = inputs["x"].shape
    out = nc.dram_tensor("out_0_dram", shape, _mybir.dt.from_np(_np.dtype("float32")), kind="ExternalOutput").ap()
    build(nc, aps, out)
    r = _run(nc, [arrays], core_ids=[0])
    return r.results[0]["out_0_dram"]
```

```python
from contextlib import ExitStack

import concourse.bass as bass
from concourse import mybir

ALU = mybir.AluOpType
ACT = mybir.ActivationFunctionType
AX_X = mybir.AxisListType.X
F32 = mybir.dt.float32
I32 = mybir.dt.int32
BF16 = mybir.dt.bfloat16

P = 128
EPS = 1e-5
NEG_SLOPE = 0.2
BIG = 1.0e30
SKIP = 1000000


class Steps:

    def __init__(self, eng, sem):
        self.eng, self.sem, self.base, self.c, self.i, self.per = eng, sem, 0, 0, 0, 0
        self.due = eng.alloc_register("due")

    def enter(self, i, per):
        self.i, self.per, self.c = i, per, 0

    def loop(self, bodies, per):
        self.base, self.c = self.base + self.c, 0

        def leave():
            self.base, self.i, self.per, self.c = self.base + bodies * per, 0, 0, 0
        return leave

    def wait(self, sem, value, first=None):
        if first and not isinstance(value, int):
            self.eng.reg_mov(self.due, value)
            value = self.due
            self.eng.wait_ge(*first)
        self.eng.wait_ge(sem, value)

    def did(self, ins, first=None):
        ins.then_inc(self.sem, 1)
        self.c += 1
        self.wait(self.sem, self.base + self.i * self.per + self.c, first)


def run(eng, body, lo, hi, peel=()):
    i = lo
    while i < hi:
        if i in peel:
            body(i)
            i += 1
            continue
        end = min([x for x in peel if x > i] + [hi])
        end = min(end, hi)
        if end - i == 1:
            body(i)
        else:
            with eng.Fori(i, end) as r:
                body(r)
        i = end


def build(nc, a, out):
    x, src, dst = a["x"], a["src"], a["dst"]
    etype, ntype = a["edge_type_3"], a["node_type_3"]
    W = [a[f"L0_gnn_W{l}"] for l in range(3)]
    A_S = [a[f"L0_gnn_a_src{l}"] for l in range(3)]
    A_D = [a[f"L0_gnn_a_dst{l}"] for l in range(3)]
    B = [a[f"L0_gnn_b{l}"] for l in range(3)]
    LN = [(a[f"L0_gnn_ln{l}_g"], a[f"L0_gnn_ln{l}_b"]) for l in range(2)]
    WE, BE, WN, BN = a["L1_gnn_W_e"], a["L1_gnn_b_e"], a["L1_gnn_W_n"], a["L1_gnn_b_n"]

    N, D = x.shape
    E = src.shape[0]
    H, C = A_S[0].shape
    K3 = WE.shape[0]
    assert D == P and H * C == P and K3 == 3

    G, Q = 4, 4
    R = G * Q
    SB = P * R
    NS = -(-N // SB)
    LAST = NS - 1
    T = -(-E // P)
    CH = 7
    assert T % (2 * CH) == 0
    IT = T // (2 * CH)
    TU = 2 * CH
    FULL = E // T
    TAIL = E - FULL * T
    assert FULL == P - 1 and 0 < TAIL < T
    WA = P + 2 * H + 1
    assert N % (NS * R) == 0 and N // (NS * R) <= P
    MB = [0, 4, 10]
    PRE, FILL = 5, (3, 3, 0)
    NM = 2 * IT
    first = [PRE]
    for l in range(3):
        first.append(first[l] + 4 + FILL[l])
    assert first[3] == NS - 2
    SLOTS = 4 * Q

    def pieces(slot, n):
        return range(n * slot // SLOTS, n * (slot + 1) // SLOTS)

    table = [nc.dram_tensor(f"target_rows_{l}", (T * P, D), F32).ap() for l in range(4)]
    src0 = nc.dram_tensor("source_x_rows", (T * P, D), F32).ap()
    hdd = nc.dram_tensor("target_h_rows", (T * P, D), F32).ap()
    edge_of = nc.dram_tensor("edge_of_node", (N, 1), I32).ap()

    def chunks(ap):
        return ap.rearrange("(p c r) d -> c p (r d)", p=P, r=CH)

    def sblocks(ap):
        return ap[0:LAST * SB, :].rearrange("(i p r) d -> i p (r d)", p=P, r=R)

    def tail_block(ap):
        return ap[N - SB:N, :].rearrange("(p r) d -> p (r d)", r=R)

    with ExitStack() as ctx:
        def sb(name, shape, dt=F32):
            return ctx.enter_context(nc.sbuf_tensor(name, shape, dt))

        def sem(name):
            return ctx.enter_context(nc.semaphore(name))

        rows = sb("rows", [P, T, D])
        msg = sb("msg", [P, D * T])
        msg_f = msg[:, :].rearrange("p (f t) -> p f t", t=T)
        msg_r = msg[:, :].rearrange("p (t f) -> p t f", f=D)
        bank = ctx.enter_context(nc.psum_tensor("bank", [P, 8, 512], F32))

        dx = sb("dx", [P, R, D])
        dxt = sb("dxt", [P, Q, G * D])
        dxh = sb("dxh", [P, R, D])
        dy = sb("dy", [P, R, D])
        dsel = sb("dsel", [P, G, D])
        dstd = sb("dstd", [P, 4, R])
        drs = sb("drs", [P, 4, R])
        dmv = sb("dmv", [P, R, 2])
        dst6 = sb("dst6", [P, R, 6])
        dmk = sb("dmk", [P, 2, R], I32)
        junk = sb("junk", [P, G, D])

        stg = sb("stg", [P, TU, D])
        std_ = sb("std_", [P, TU, D])
        st3 = sb("st3", [P, TU, D])
        xt2 = sb("xt2", [P, 2, 2 * D])
        ev = sb("ev", [P, 2, D])
        NR = 4
        csm = sb("csm", [P, 8, NR * CH])
        fst6 = sb("fst6", [P, 2, CH, 6])
        fmv = sb("fmv", [P, 2, NR * CH, 2])

        ls = sb("ls", [P, T, 2 * H + 1])
        ld = sb("ld", [P, T, 2 * H])
        em = ls[:, :, :].rearrange("p t h -> p (t h)")[:, 0:6 * D].rearrange("p (u n) -> p u n", u=2)
        e_s = sb("e_s", [P, H, T])
        e_f = sb("e_f", [P, H, T])
        fm = sb("fm", [P, H, T])
        mp = sb("mp", [P, H, T + 1])
        ea = sb("ea", [P, H, T])
        es = sb("es", [P, H, T])
        ep = sb("ep", [P, H, T])
        sm = sb("sm", [P, 6, H])
        smr = sb("smr", [H, 2, P])
        smo = sb("smo", [H, P + 1])
        smb = smr[:, 0, :]
        ci = sb("ci", [P, H])
        rowa = sb("rowa", [P, 2, P])
        rowt = sb("rowt", [P, 2, P])
        rowo = sb("rowo", [P, P + 1])
        cin = rowt[:, 0, :]

        dst_i = sb("dst_i", [P, 3, T], I32)
        dst_f = e_s[:, 0:3, :]
        src_i = sb("src_i", [P, T], I32)
        et_i = sb("et_i", [P, T], I32)
        row_i = sb("row_i", [P, T], I32)
        nt_i = sb("nt_i", [P, T], I32)
        ns = e_s[:, 3, :]
        negns = sb("negns", [P, T])
        negseen = sb("negseen", [P, T])
        unlast = sb("unlast", [P, T])
        last_r = sb("last_r", [P, T])
        more_r = sb("more_r", [P, T])
        none_r = sb("none_r", [P, T])
        keep = sb("keep", [P, T])
        kept = sb("kept", [P, T])
        lastf = e_f[:, 0, :]
        put_i = sb("put_i", [P, T], I32)
        pos_i = sb("pos_i", [P, T], I32)
        eid = sb("eid", [P, T], I32)
        zero = sb("zero", [P, T])
        etm = sb("etm", [P, 3, TU], BF16)
        ntm = sb("ntm", [P, 2, T], I32)
        ntc = sb("ntc", [P, 2, TU], I32)
        types = sb("types", [P, NS * R], I32)

        ident = sb("ident", [P, P])
        identb = sb("identb", [P, P], BF16)
        ones3 = sb("ones3", [3, P], BF16)
        eps = sb("eps", [P, 1])
        wall = sb("wall", [P, 3, WA])
        wcen = sb("wcen", [P, 3, D])
        wnt = sb("wnt", [P, 4, 3 * D])
        wet = sb("wet", [P, 3 * D])
        gb = sb("gb", [P, 4])
        hm = sb("hm", [P, H])
        av = sb("av", [P, 6])
        amat = sb("amat", [P, 2 * H])
        wmean = sb("wmean", [P, 24])
        BO = [l * WA for l in range(3)]
        BEO = 3 * WA
        BNO = BEO + 3 * D
        BCO = [BNO + 3 * D + l * D for l in range(3)]
        BT = BNO + 6 * D
        bias3 = sb("bias3", [3, BT], BF16)
        bmean = sb("bmean", [1, 8])

        wraw = msg[:, 0:3 * D].rearrange("p (l d) -> p l d", l=3)
        wnraw = msg[:, 3 * D:15 * D].rearrange("p (n k) -> p n k", n=3)
        weraw = msg[:, 15 * D:18 * D].rearrange("p (n k) -> p n k", n=3)

        wtr = msg[:, 90 * D:91 * D]
        brow = msg[0:1, 18 * D:18 * D + BT]
        brest = msg[0:1, 18 * D + BT:18 * D + 2 * BT]
        bpart = msg[0:1, 18 * D + 2 * BT:18 * D + 4 * BT].bitcast(BF16)[:, 0:3 * BT].rearrange("o (k n) -> o k n", k=3)

        s_w = sem("weights_loaded")
        s_i = sem("indices_loaded")
        s_nt = sem("node_types_loaded")
        s_ms = sem("memsets_done")
        s_id = sem("identity_ready")
        s_pd = sem("prelude_dve")
        s_ppe = sem("prelude_pe")
        s_ready = sem("weights_ready")
        s_b3 = sem("bias_parts_moved")
        s_put = sem("scatter_indices_ready")
        s_tabi = sem("edge_table_cleared")
        s_tabw = sem("edge_table_written")
        s_tabg = sem("edge_positions_gathered")
        s_ntg = sem("target_types_gathered")
        s_g = sem("source_rows_gathered")
        s_gd = sem("target_rows_gathered")
        s_sv = sem("x_rows_saved")
        s_out = sem("target_outputs_scattered")
        d_ld = sem("d_x_loaded")
        d_t = sem("d_transposed")
        d_xt = sem("d_xt_ready")
        d_h = sem("d_h_ready")
        d_ss = sem("d_squares_summed")
        d_std = sem("d_std_ready")
        d_xn = sem("d_x1_normalised")
        d_xh = sem("d_normalised")
        d_var = sem("d_var_ready")
        d_p = sem("d_typed_ready")
        d_s0 = sem("d_type0_copied")
        d_sel = sem("d_selected")
        d_o = sem("d_out_ready")
        d_st = sem("d_stored")
        d_dve = sem("d_dve_steps")
        l_s = [sem(f"stage_source_{h}") for h in range(2)]
        l_d = [sem(f"stage_target_{h}") for h in range(2)]
        q_t = sem("q_transposed")
        q_xt = sem("q_xt_ready")
        q_h = sem("q_h_ready")
        q_ev = sem("q_source_h_out")
        q_ea = sem("q_target_h_out")
        q_st = [sem(f"q_h_stored_{h}") for h in range(2)]
        m_dve = sem("m_dve")
        m_act = sem("m_act")
        m_pe = sem("m_pe")
        m_log = sem("logit_weights_ready")
        p3 = sem("messages_written")
        l_h = [sem(f"target_h_loaded_{h}") for h in range(2)]
        r_dve = sem("r_dve")
        r_pe = sem("r_pe")
        s_scan = sem("scan_pieces_done")
        f_sq = sem("f_squares_ready")
        f_y = sem("f_reciprocals_ready")
        f_std = sem("f_std_ready")
        f_src = sem("f_source_rows_ready")
        f_v = sem("f_variances_ready")
        f_out = sem("f_chunk_done")
        f_st = [sem(f"f_stored_{h}") for h in range(2)]
        l_x = [sem(f"x_chunks_loaded_{h}") for h in range(2)]
        v_t = sem("v_transposed")
        v_xt = sem("v_xt_ready")
        v_w = sem("v_messages_ready")
        v_et = sem("v_type_flags_ready")
        v_m = sem("v_messages_out")
        v_v = sem("v_projected")
        v_s0 = sem("v_type0_copied")
        v_sel = sem("v_selected")
        v_put = sem("v_written")
        v_dve = sem("v_dve")
        l_v = [sem(f"v_staged_{h}") for h in range(2)]
        u_t = sem("u_transposed")
        u_xt = sem("u_xt_ready")
        u_p = sem("u_projected")
        u_s0 = sem("u_type0_copied")
        u_sel = sem("u_selected")
        u_y = sem("u_own_part_ready")
        u_st = [sem(f"u_own_part_stored_{h}") for h in range(2)]
        w_y = sem("w_rows_ready")
        w_sq = sem("w_squares_ready")
        w_v = sem("w_sums_ready")
        w_std = sem("w_std_ready")
        u_o = sem("u_out_ready")
        l_w = [sem(f"w_staged_{h}") for h in range(2)]
        l_u = [sem(f"u_staged_{h}") for h in range(2)]

        def bc(ap, n):
            return ap.rearrange("p (a o) -> p a o", o=1).broadcast_to((ap.shape[0], ap.shape[1], n))

        def heads(ap, t0, n):
            v = ap[:, :, bass.ds(t0, n)].rearrange("p h (t o) -> p t h o", o=1)
            return v.broadcast_to((P, n, H, C))

        block = ctx.enter_context(nc.Block())

        @block.sync
        def _(sp):
            sp.dma_start(wraw[:, 0, :], W[0]).then_inc(s_w, 16)
            sp.dma_start(wraw[:, 1, :], W[1]).then_inc(s_w, 16)
            sp.dma_start(wraw[:, 2, :], W[2]).then_inc(s_w, 16)
            for l in range(3):
                sp.dma_start(av[:, 2 * l:2 * l + 1], A_S[l].rearrange("h (c o) -> (h c) o", o=1)).then_inc(s_w, 16)
                sp.dma_start(av[:, 2 * l + 1:2 * l + 2], A_D[l].rearrange("h (c o) -> (h c) o", o=1)).then_inc(s_w, 16)
            for l in range(2):
                for k in range(2):
                    sp.dma_start(gb[:, 2 * l + k:2 * l + k + 1],
                                 LN[l][k].rearrange("(c o) -> c o", o=1)).then_inc(s_w, 16)
            sp.dma_start(wnraw, WN.rearrange("n o k -> o n k")).then_inc(s_w, 16)
            sp.dma_start(weraw, WE.rearrange("n o k -> o n k")).then_inc(s_w, 16)
            sp.wait_ge(s_ms, 1)
            for l in range(3):
                for off in (BO[l], BCO[l]):
                    sp.dma_start(brow[:, off:off + D], B[l].rearrange("(o d) -> o d", o=1)).then_inc(s_w, 16)
            sp.dma_start(brow[:, BEO:BEO + 3 * D], BE.rearrange("(o n) d -> o (n d)", o=1)).then_inc(s_w, 16)
            sp.dma_start(brow[:, BNO:BNO + 3 * D], BN.rearrange("(o n) d -> o (n d)", o=1)).then_inc(s_w, 16)
            sp.dma_start(dx[:, :, :].rearrange("p r d -> p (r d)"), sblocks(x)[0, :, :]).then_inc(d_ld, 16)
            sp.wait_ge(s_ms, 2)
            sp.dma_start(edge_of.rearrange("(p r) o -> p (r o)", r=NS * R), types[0:N // (NS * R), :])\
                .then_inc(s_tabi, 16)
            sp.wait_ge(s_tabi, 16)
            sp.dma_start(types[:, 0:LAST * R].rearrange("p (i r) -> p i r", r=R),
                         ntype[0:LAST * SB].rearrange("(i p r) -> p i r", p=P, r=R)).then_inc(s_nt, 16)
            sp.dma_start(types[:, LAST * R:NS * R],
                         ntype[N - SB:N].rearrange("(p r) -> p r", r=R)).then_inc(s_nt, 16)
            sp.wait_ge(s_pd, 1)
            for k in range(3):
                sp.dma_start(bias3[k:k + 1, :], bpart[:, k, :]).then_inc(s_b3, 16)

            def dense(i, beside=None):
                for slot in range(SLOTS):
                    if beside:
                        beside(slot)
                    if slot == 3 * Q - 1 and (not isinstance(i, int) or i < LAST):
                        nxt = tail_block(x) if isinstance(i, int) and i + 1 == LAST else sblocks(x)[i + 1, :, :]
                        sp.wait_ge(d_var, Q * i + Q)
                        sp.dma_start(dx[:, :, :].rearrange("p r d -> p (r d)"), nxt).then_inc(d_ld, 16)
                dest = tail_block(out) if isinstance(i, int) and i == LAST else sblocks(out)[i, :, :]
                sp.wait_ge(d_o, Q * i + Q)
                sp.dma_start(dest, dy[:, :, :].rearrange("p r d -> p (r d)")).then_inc(d_st, 16)

            def stage(buf, h):
                return buf[:, h * CH:(h + 1) * CH, :].rearrange("p r d -> p (r d)")

            def stage_rows(c, h, sems):
                sp.dma_start(stage(stg, h), rows[:, bass.ds(c * CH, CH), :].rearrange("p r d -> p (r d)"))\
                    .then_inc(sems[h], 16)

            def p1(l):
                n0 = l * T

                def body(i):
                    for h in range(2):
                        sp.wait_ge(q_t, n0 + i * TU + (h + 1) * CH)
                        stage_rows(2 * i + 2 + h, h, l_s)
                        sp.dma_start(stage(std_, h), chunks(table[l])[2 * i + 2 + h, :, :]).then_inc(l_d[h], 16)
                        sp.wait_ge(q_ea, n0 + i * TU + (h + 1) * CH)
                        sp.dma_start(chunks(hdd)[2 * i + h, :, :], stage(st3, h)).then_inc(q_st[h], 16)
                for h in range(2):
                    stage_rows(h, h, l_s)
                    sp.dma_start(stage(std_, h), chunks(table[l])[h, :, :]).then_inc(l_d[h], 16)
                run(sp, body, 0, IT - 1)
                for h in range(2):
                    sp.wait_ge(q_ea, n0 + (IT - 1) * TU + (h + 1) * CH)
                    sp.dma_start(chunks(hdd)[2 * (IT - 1) + h, :, :], stage(st3, h)).then_inc(q_st[h], 16)

            def load_h(l, c):
                if c >= 2:
                    sp.wait_ge(p3, l * NM + c - 1)
                sp.dma_start(stage(std_, c % 2), chunks(hdd)[c, :, :]).then_inc(l_h[c % 2], 16)

            def messages(l, slot):
                for c in pieces(slot, NM - 2):
                    load_h(l, c + 2)

            def load_x(c):
                sp.dma_start(stage(std_, c % 2), chunks(table[0])[c, :, :]).then_inc(l_x[c % 2], 16)
                sp.dma_start(stage(st3, c % 2), chunks(src0)[c, :, :]).then_inc(l_x[c % 2], 16)

            def finish(l, slot):
                for c in pieces(slot, NM):
                    if l == 2 and c >= 2:
                        sp.wait_ge(f_v, l * NM + c - 1)
                        load_x(c)
                    if c >= 2:
                        store_rows(l, c - 2)

            def store_rows(l, c):
                sp.wait_ge(f_out, l * NM + c + 1)
                sp.dma_start(chunks(table[l + 1])[c, :, :], stage(stg, c % 2)).then_inc(f_st[c % 2], 16)

            def typed_messages():
                def body(i):
                    for h in range(2):
                        sp.wait_ge(v_t, i * TU + (h + 1) * CH)
                        stage_rows(2 * i + 2 + h, h, l_v)
                for h in range(2):
                    sp.wait_ge(u_st[h], IT * 16)
                    stage_rows(h, h, l_v)
                run(sp, body, 0, IT - 1)

            def typed_targets():
                def store(c, h):
                    sp.wait_ge(u_y, c + 1)
                    sp.dma_start(chunks(hdd)[c, :, :], stage(stg, h)).then_inc(u_st[h], 16)

                def body(i):
                    for h in range(2):
                        store(2 * i + h, h)
                        sp.dma_start(stage(std_, h), chunks(table[3])[2 * i + 2 + h, :, :]).then_inc(l_u[h], 16)
                for h in range(2):
                    sp.wait_ge(f_st[0], 3 * IT * 16)
                    sp.wait_ge(f_st[1], 3 * IT * 16)
                    sp.dma_start(stage(std_, h), chunks(table[3])[h, :, :]).then_inc(l_u[h], 16)
                run(sp, body, 0, IT - 1)
                for h in range(2):
                    store(2 * (IT - 1) + h, h)

            def last_rows():
                def body(i):
                    for h in range(2):
                        sp.wait_ge(w_y, 2 * i + h + 1)
                        sp.dma_start(stage(std_, h), chunks(hdd)[2 * i + 2 + h, :, :]).then_inc(l_w[h], 16)
                for h in range(2):
                    sp.wait_ge(u_st[h], IT * 16)
                    sp.dma_start(stage(std_, h), chunks(hdd)[h, :, :]).then_inc(l_w[h], 16)
                run(sp, body, 0, IT - 1)

            run(sp, dense, 0, PRE, (LAST - 1, LAST))
            for l in range(3):
                i = first[l]
                sp.wait_ge(s_g, 16 * T * (l + 1))
                if l == 0:
                    sp.wait_ge(s_sv, 16 * 2 * IT)
                p1(l)
                for h in range(2):
                    sp.wait_ge(q_st[h], (l + 1) * IT * 16)
                for c in range(2):
                    load_h(l, c)
                dense(i, lambda slot: messages(l, slot))
                dense(i + 1)
                dense(i + 2)
                if l == 2:
                    for c in range(2):
                        load_x(c)
                dense(i + 3, lambda slot: finish(l, slot))
                for c in range(NM - 2, NM):
                    store_rows(l, c)
                run(sp, dense, i + 4, first[l + 1], (LAST - 1, LAST))
            typed_targets()
            sp.wait_ge(s_g, 16 * T * 4)
            typed_messages()
            dense(NS - 2)
            dense(NS - 1)
            last_rows()
            sp.wait_ge(d_st, 16 * NS)
            sp.wait_ge(s_out, 16 * T)

        @block.gpsimd
        def _(pool):
            pool.memset(ident[:, :], 0.0).then_inc(s_id, 1)
            pool.wait_ge(s_id, 1)
            pool.affine_select(out=ident[:, :], in_=ident[:, :], compare_op=ALU.not_equal, fill=1.0,
                               base=0, pattern=[[-1, P]], channel_multiplier=1).then_inc(s_id, 1)
            for n, (part, value) in enumerate(((dst_i[96:P, :, :], SKIP), (src_i[96:P, :], 0),
                                               (et_i[96:P, :], K3), (dst_i[0:1, 1, 0:1], -1))):
                pool.wait_ge(s_id, n + 2)
                pool.memset(part, value).then_inc(s_id, 1)
            pool.wait_ge(s_id, 6)
            flat = dst[0:FULL * T].rearrange("(p t) -> p t", t=T)
            pool.dma_start(dst_i[0:FULL, 0, :], flat).then_inc(s_i, 16)
            pool.dma_start(dst_i[FULL:P, 0, 0:TAIL], dst[FULL * T:E].rearrange("(o t) -> o t", o=1)).then_inc(s_i, 16)
            pool.dma_start(dst_i[0:1, 1, 1:T], dst[0:T - 1].rearrange("(o t) -> o t", o=1)).then_inc(s_i, 16)
            pool.dma_start(dst_i[1:FULL, 1, :], dst[T - 1:FULL * T - 1].rearrange("(p t) -> p t", t=T)).then_inc(s_i, 16)
            pool.dma_start(dst_i[FULL:P, 1, 0:TAIL + 1],
                           dst[FULL * T - 1:E].rearrange("(o t) -> o t", o=1)).then_inc(s_i, 16)
            pool.dma_start(dst_i[0:FULL, 2, :], dst[1:FULL * T + 1].rearrange("(p t) -> p t", t=T)).then_inc(s_i, 16)
            pool.dma_start(dst_i[FULL:P, 2, 0:TAIL - 1],
                           dst[FULL * T + 1:E].rearrange("(o t) -> o t", o=1)).then_inc(s_i, 16)
            pool.dma_start(src_i[0:FULL, :], src[0:FULL * T].rearrange("(p t) -> p t", t=T)).then_inc(s_i, 16)
            pool.dma_start(src_i[FULL:P, 0:TAIL], src[FULL * T:E].rearrange("(o t) -> o t", o=1)).then_inc(s_i, 16)
            pool.dma_start(et_i[0:FULL, :], etype[0:FULL * T].rearrange("(p t) -> p t", t=T)).then_inc(s_i, 16)
            pool.dma_start(et_i[FULL:P, 0:TAIL], etype[FULL * T:E].rearrange("(o t) -> o t", o=1)).then_inc(s_i, 16)
            pool.iota(eid[:, :], pattern=[[1, T]], base=0, channel_multiplier=T).then_inc(s_id, 1)
            pool.memset(pos_i[:, :], SKIP).then_inc(s_id, 1)
            pool.memset(nt_i[:, :], 0).then_inc(s_id, 1)
            pool.wait_ge(s_id, 9)
            pool.wait_ge(s_i, 16 * 11)

            def gather(dest, tab, idx, done, bound):
                pool.indirect_dma_start(out=dest, out_offset=None, in_=tab,
                                        in_offset=bass.IndirectOffsetOnAxis(ap=idx, axis=0),
                                        bounds_check=bound, oob_is_err=False).then_inc(done, 16)

            def save(tab, buf, k, done):
                pool.wait_ge(done, 16 * TU * (k + 1))
                pool.dma_start(tab.rearrange("(p t) d -> p t d", p=P)[:, k * TU:(k + 1) * TU, :],
                               buf[:, k * TU:(k + 1) * TU, :]).then_inc(s_sv, 16)

            for t in range(T):
                if t and t % TU == 0:
                    save(src0, rows, t // TU - 1, s_g)
                gather(rows[:, t, :], x, src_i[:, t:t + 1], s_g, N - 1)
            save(src0, rows, IT - 1, s_g)
            pool.wait_ge(s_b3, 48)
            pool.wait_ge(s_ready, 1)
            for t in range(T):
                if t and t % TU == 0:
                    save(table[0], msg_r, t // TU - 1, s_gd)
                gather(msg_r[:, t, :], x, row_i[:, t:t + 1], s_gd, N - 1)
            save(table[0], msg_r, IT - 1, s_gd)
            pool.wait_ge(s_put, 1)
            pool.wait_ge(s_tabi, 16)
            for t in range(T):
                pool.indirect_dma_start(out=edge_of, out_offset=bass.IndirectOffsetOnAxis(ap=put_i[:, t:t + 1], axis=0),
                                        in_=eid[:, t:t + 1], in_offset=None,
                                        bounds_check=N - 1, oob_is_err=False).then_inc(s_tabw, 16)
            ntab = ntype.rearrange("(n o) -> n o", o=1)
            for t in range(T):
                gather(nt_i[:, t:t + 1], ntab, row_i[:, t:t + 1], s_ntg, N - 1)
            pool.wait_ge(s_tabw, 16 * T)
            for t in range(T):
                gather(pos_i[:, t:t + 1], edge_of, src_i[:, t:t + 1], s_tabg, N - 1)
            pool.wait_ge(s_tabg, 16 * T)
            for l in range(1, 4):
                for c in range(NM):
                    pool.wait_ge(f_y, (l - 1) * NM + c + 1)
                    for j in range(CH):
                        t, m = c * CH + j, c % NR * CH + j
                        if l < 3:
                            last = pool.tensor_scalar(rows[:, t, :], rows[:, t, :], ls[:, t, 2 * H:2 * H + 1],
                                                      csm[:, 5, m:m + 1], ALU.add, ALU.mult)
                        else:
                            last = pool.tensor_scalar(rows[:, t, :], rows[:, t, :], fmv[:, 1, m, 0:1],
                                                      csm[:, 5, m:m + 1], ALU.subtract, ALU.mult)
                    last.then_inc(f_src, 1)
                pool.wait_ge(f_src, l * NM)
                for h in range(2):
                    pool.wait_ge(f_st[h], 16 * l * IT)
                for t in range(T):
                    gather(rows[:, t, :], table[l], pos_i[:, t:t + 1], s_g, T * P - 1)
            pool.wait_ge(d_st, 16 * NS)
            for t in range(T):
                if t % CH == 0:
                    pool.wait_ge(u_o, t // CH + 1)
                pool.indirect_dma_start(out=out, out_offset=bass.IndirectOffsetOnAxis(ap=put_i[:, t:t + 1], axis=0),
                                        in_=rows[:, t, :], in_offset=None,
                                        bounds_check=N - 1, oob_is_err=False).then_inc(s_out, 16)
            pool.wait_ge(s_out, 16 * T)

        @block.tensor
        def _(pe):
            pe.wait_ge(s_w, 16 * 23)
            pe.wait_ge(s_id, 2)
            for l in range(3):
                if l:
                    pe.wait_ge(s_pd, 1 + 2 * l)
                pe.transpose(bank[:, 0, 0:P], wraw[:, l, :], ident[:, :]).then_inc(s_ppe, 1)
                pe.wait_ge(s_pd, 2 + 2 * l)
                pe.matmul(bank[:, 1, 0:2 * H], wtr, amat[:, :], start=True, stop=True).then_inc(s_ppe, 1)
            for j in range(4):
                for n in range(3):
                    pe.transpose(bank[:, 2 + j, n * D:(n + 1) * D], wnraw[:, n, j * D:(j + 1) * D], ident[:, :])
            for n in range(3):
                last = pe.transpose(bank[:, 6, n * D:(n + 1) * D], weraw[:, n, :], ident[:, :])
            last.then_inc(s_ppe, 1)
            pe.wait_ge(s_ready, 1)
            pe.wait_ge(s_b3, 48)

            def bias(dest, off, n, times, stop=True):
                src_ = bias3[:, off:off + n]
                if times > 1:
                    src_ = src_.rearrange("k (o n) -> k o n", o=1).broadcast_to((3, times, n))
                return pe.matmul(dest, ones3[:, :], src_, start=True, stop=stop)

            def dense(i):
                def turn(s, q):
                    if s == 3:
                        pe.wait_ge(d_xn, i * 4 + q + 1)
                    elif s:
                        pe.wait_ge(d_xh, i * 8 + (s - 1) * 4 + q + 1)
                    buf = dxh if s else dx
                    for j in range(G):
                        last = pe.transpose(bank[:, q, j * D:(j + 1) * D], buf[:, q * G + j, :], ident[:, :])
                    last.then_inc(d_t, 1)

                def layer(l, q):
                    pe.wait_ge(d_xt, i * 16 + l * 4 + q + 1)
                    bias(bank[:, q, :].rearrange("p (g d) -> p g d", g=G), BCO[l], D, G)
                    for j in range(G):
                        last = pe.matmul(bank[:, q, j * D:(j + 1) * D], dxt[:, q, j * D:(j + 1) * D],
                                         wcen[:, l, :], start=False, stop=True, skip_group_check=True)
                    last.then_inc(d_h, 1)

                def project(q):
                    pe.wait_ge(d_xt, i * 16 + 12 + q + 1)
                    for hh in range(2):
                        if not isinstance(i, int) or i * 8 + q * 2 + hh >= 2:
                            pe.wait_ge(d_sel, i * 8 + q * 2 + hh - 1)
                        for j in range(2 * hh, 2 * hh + 2):
                            bias(bank[:, 4 + j, 0:3 * D], BNO, 3 * D, 1)
                            last = pe.matmul(bank[:, 4 + j, 0:3 * D], dxt[:, q, j * D:(j + 1) * D],
                                             wnt[:, 0, :], start=False, stop=True, skip_group_check=True)
                        last.then_inc(d_p, 1)

                pe.wait_ge(d_ld, i * 16 + 16)
                for u in range(4 * Q + 1):
                    if u < 4 * Q:
                        turn(*divmod(u, Q))
                    if u:
                        s, q = divmod(u - 1, Q)
                        if s < 3:
                            layer(s, q)
                        else:
                            project(q)

            def p1(l):
                n0 = l * T

                pe.wait_ge(d_sel, 8 * first[l])

                def turn(i, tt):
                    n, h = n0 + i * TU + tt, tt // CH
                    if tt % CH == 0:
                        pe.wait_ge(l_s[h], 16 * (l * IT + i + 1))
                        pe.wait_ge(l_d[h], 16 * (l * IT + i + 1))
                    if not isinstance(n, int) or n >= 2:
                        pe.wait_ge(q_xt, n - 1)
                    pe.transpose(bank[:, tt % 2, 0:D], stg[:, tt, :], ident[:, :])
                    pe.transpose(bank[:, tt % 2, D:2 * D], std_[:, tt, :], ident[:, :]).then_inc(q_t, 1)

                def body(i):
                    turn(i, 0)
                    for tt in range(TU):
                        if tt + 1 < TU:
                            turn(i, tt + 1)
                        n = n0 + i * TU + tt
                        pe.wait_ge(q_xt, n + 1)
                        if not isinstance(n, int) or n >= 2:
                            pe.wait_ge(q_ev, n - 1)
                            pe.wait_ge(q_ea, n - 1)
                        for k in range(2):
                            o = bank[:, 2 + 2 * k + tt % 2, 0:WA]
                            bias(o, BO[l], WA, 1)
                            last = pe.matmul(o, xt2[:, tt % 2, k * D:(k + 1) * D], wall[:, l, :],
                                             start=False, stop=True, skip_group_check=True)
                        last.then_inc(q_h, 1)
                run(pe, body, 0, IT, (0,) if l == 0 else ())

            def logits(l):
                for n, k in enumerate((2, 0, 1) if l else (0, 1)):
                    pe.wait_ge(m_dve, MB[l] + 2 * n + 1)
                    pe.transpose(bank[0:H, 6, 0:P], sm[:, 2 * k, :], ident[:, :])
                    pe.transpose(bank[0:H, 6, P:2 * P], sm[:, 2 * k + 1, :], ident[:, :]).then_inc(m_pe, 1)
                    pe.wait_ge(m_dve, MB[l] + 2 * n + 2)
                    pe.transpose(bank[:, 7, 0:H], smb if k == 2 else smo[:, 0:P], ident[0:H, 0:H])\
                        .then_inc(m_pe, 1)

            def carry(l):
                pe.wait_ge(r_dve, 2 * l + 1)
                pe.transpose(bank[:, 6, 0:P], rowa[:, 0, :], ident[:, :])
                pe.transpose(bank[:, 6, P:2 * P], rowa[:, 1, :], ident[:, :]).then_inc(r_pe, 1)
                pe.wait_ge(r_dve, 2 * l + 2)
                pe.transpose(bank[:, 7, 0:P], rowo[:, 0:P], ident[:, :]).then_inc(r_pe, 1)

            def typed_messages():
                def turn(i, tt):
                    n, h = i * TU + tt, tt // CH
                    if tt % CH == 0:
                        pe.wait_ge(l_v[h], 16 * (i + 1))
                    if not isinstance(n, int) or n >= 2:
                        pe.wait_ge(v_xt, n - 1)
                    pe.transpose(bank[:, tt % 2, 0:D], stg[:, tt, :], ident[:, :]).then_inc(v_t, 1)

                def apply(i, tt):
                    n = i * TU + tt
                    pe.wait_ge(v_xt, n + 1)
                    if not isinstance(n, int) or n >= 2:
                        pe.wait_ge(v_m, n - 1)
                    for k in range(3):
                        o = bank[:, 2 + tt % 2, k * D:(k + 1) * D]
                        pe.matmul(o, bias3[:, BEO + k * D:BEO + (k + 1) * D], ones3[:, :], start=True, stop=True)
                        pe.matmul(o, etm[:, k, tt:tt + 1].broadcast_to((P, D)), identb[:, :],
                                  start=False, stop=True, skip_group_check=True)
                        last = pe.matmul(o, wet[:, k * D:(k + 1) * D], xt2[:, tt % 2, 0:D],
                                         start=False, stop=True, skip_group_check=True)
                    last.then_inc(v_w, 1)

                def project(i, tt):
                    n = i * TU + tt
                    pe.wait_ge(v_m, n + 1)
                    if not isinstance(n, int) or n >= 2:
                        pe.wait_ge(v_sel, n - 1)
                    for k in range(3):
                        last = pe.matmul(bank[:, 6 + tt % 2, 0:3 * D], em[:, tt % 2, k * D:(k + 1) * D],
                                         wnt[:, 1 + k, :], start=(k == 0), stop=(k == 2))
                    last.then_inc(v_v, 1)

                def body(i):
                    turn(i, 0)
                    pe.wait_ge(v_et, i + 1)
                    for tt in range(TU + 1):
                        if tt + 1 < TU:
                            turn(i, tt + 1)
                        if tt < TU:
                            apply(i, tt)
                        if tt:
                            project(i, tt - 1)
                run(pe, body, 0, IT, (0,))

            def typed_targets():
                pe.wait_ge(d_sel, 8 * (NS - 2))

                def turn(i, tt):
                    n, h = i * TU + tt, tt // CH
                    if tt % CH == 0:
                        pe.wait_ge(l_u[h], 16 * (i + 1))
                    if not isinstance(n, int) or n >= 2:
                        pe.wait_ge(u_xt, n - 1)
                    pe.transpose(bank[:, tt % 2, 0:D], std_[:, tt, :], ident[:, :]).then_inc(u_t, 1)

                def body(i):
                    turn(i, 0)
                    for tt in range(TU):
                        if tt + 1 < TU:
                            turn(i, tt + 1)
                        n = i * TU + tt
                        pe.wait_ge(u_xt, n + 1)
                        if not isinstance(n, int) or n >= 2:
                            pe.wait_ge(u_sel, n - 1)
                        bias(bank[:, 2 + tt % 2, 0:3 * D], BNO, 3 * D, 1)
                        pe.matmul(bank[:, 2 + tt % 2, 0:3 * D], xt2[:, tt % 2, 0:D], wnt[:, 0, :],
                                  start=False, stop=True, skip_group_check=True).then_inc(u_p, 1)
                run(pe, body, 0, IT, (0,))

            run(pe, dense, 0, PRE, (0,))
            for l in range(3):
                i = first[l]
                p1(l)
                logits(l)
                dense(i)
                dense(i + 1)
                carry(l)
                dense(i + 2)
                run(pe, dense, i + 3, first[l + 1])
            typed_targets()
            typed_messages()
            dense(NS - 2)
            dense(NS - 1)
            carry(3)

        @block.scalar
        def _(act):
            act.wait_ge(s_ready, 1)
            act.wait_ge(s_ms, 2)

            def turned(dest, src_, s):
                if s in (1, 2):
                    return nc.scalar.activation(dest, src_, ACT.Relu, scale=gb[:, 2 * s - 2:2 * s - 1],
                                                bias=gb[:, 2 * s - 1:2 * s])
                return nc.scalar.activation(dest, src_, ACT.Relu if s == 3 else ACT.Copy)

            def dense(i, beside=None):
                def turn(s, q):
                    act.wait_ge(d_t, i * 16 + s * 4 + q + 1)
                    turned(dxt[:, q, :], bank[:, q, :], s).then_inc(d_xt, 1)

                def sums(k, q, tile):
                    s = (0, 1, 3)[k]
                    """The sum of squares of each row of a group, then its standard deviation."""
                    for j in range(G):
                        last = nc.scalar.activation(junk[:, j, :], tile(j), ACT.Square,
                                                    accum_out=dstd[:, s, q * G + j:q * G + j + 1])
                    last.then_inc(d_ss, 1)
                    act.wait_ge(d_ss, i * 12 + k * 4 + q + 1)
                    nc.scalar.activation(dstd[:, s, q * G:(q + 1) * G], dstd[:, s, q * G:(q + 1) * G], ACT.Sqrt,
                                         scale=1.0 / D, bias=eps[:, 0:1]).then_inc(d_std, 1)

                def layer2_std(q):
                    act.wait_ge(d_var, i * 4 + q + 1)
                    nc.scalar.activation(dstd[:, 2, q * G:(q + 1) * G],
                                         dmv[:, q * G:(q + 1) * G, 1:2].rearrange("p g o -> p (g o)"),
                                         ACT.Sqrt, bias=eps[:, 0:1]).then_inc(d_std, 1)

                def type0(q):
                    for hh in range(2):
                        n = i * 8 + q * 2 + hh
                        act.wait_ge(d_p, n + 1)
                        if not isinstance(n, int) or n >= 2:
                            act.wait_ge(d_sel, n - 1)
                        nc.scalar.activation(dsel[:, 2 * hh:2 * hh + 2, :],
                                             bank[:, 4 + 2 * hh:6 + 2 * hh, 0:D], ACT.Copy).then_inc(d_s0, 1)

                def last_sums(q):
                    act.wait_ge(d_sel, i * 8 + q * 2 + 2)
                    sums(2, q, lambda j: dy[:, q * G + j, :])

                for u in range(4 * Q + 1):
                    if u < 4 * Q:
                        turn(*divmod(u, Q))
                    if 3 * Q - 2 <= u < 4 * Q - 2:
                        layer2_std(u - 3 * Q + 2)
                    if u:
                        s, q = divmod(u - 1, Q)
                        if s < 2:
                            act.wait_ge(d_h, i * 12 + s * 4 + q + 1)
                            sums(s, q, lambda j: bank[:, q, j * D:(j + 1) * D])
                        elif s == 3:
                            type0(q)
                            if q:
                                last_sums(q - 1)
                        if beside:
                            beside(u - 1)
                last_sums(Q - 1)

            def p1(l):
                n0 = l * T

                def turn(i, tt):
                    n = n0 + i * TU + tt
                    act.wait_ge(q_t, n + 1)
                    if not isinstance(n, int) or n >= 2:
                        act.wait_ge(q_h, n - 1)
                    turned(xt2[:, tt % 2, :], bank[:, tt % 2, 0:2 * D], l).then_inc(q_xt, 1)

                def body(i):
                    turn(i, 0)
                    for tt in range(TU):
                        if tt + 1 < TU:
                            turn(i, tt + 1)
                        n, h = n0 + i * TU + tt, tt // CH
                        act.wait_ge(q_h, n + 1)
                        if tt % CH == 0 and (l or not isinstance(i, int) or i):
                            act.wait_ge(q_st[h], 16 * (l * IT + i))
                        nc.scalar.activation(st3[:, tt, :], bank[:, 4 + tt % 2, 0:D], ACT.Copy)
                        nc.scalar.activation(ld[:, bass.ds(i * TU + tt, 1), :],
                                             bank[:, 4 + tt % 2, D:D + 2 * H].rearrange("p (o n) -> p o n", o=1),
                                             ACT.Copy).then_inc(q_ea, 1)
                run(act, body, 0, IT, (0,) if l == 0 else ())

            def logits(l):
                for k in range(3):
                    act.wait_ge(m_log, 3 * l + k + 1)
                    buf = (ea, e_s, e_f)[k]
                    nc.scalar.activation(buf[:, :, :], buf[:, :, :], ACT.Exp).then_inc(m_act, 1)

            def finish(l, slot):
                for c in pieces(slot, NM):
                    squares(l, c)
                    if c:
                        deviations(l, c - 1)

            def squares(l, c):
                if l < 2:
                    if l * NM + c >= NR:
                        act.wait_ge(f_src, l * NM + c + 1 - NR)
                    for j in range(CH):
                        t = c * CH + j
                        last = nc.scalar.activation(st3[:, c % 2 * CH + j, :], rows[:, t, :], ACT.Square,
                                                    bias=ls[:, t, 2 * H:2 * H + 1],
                                                    accum_out=csm[:, 1, c % NR * CH + j:c % NR * CH + j + 1])
                    last.then_inc(f_sq, 1)

            def deviations(l, c):
                cs = slice(c % NR * CH, (c % NR + 1) * CH)
                act.wait_ge(f_v, l * NM + c + 1)
                var = (lambda k: fmv[:, k, cs, 1:2].rearrange("p t o -> p (t o)"))
                nc.scalar.activation(csm[:, 2, cs], var(0), ACT.Sqrt, bias=eps[:, 0:1])
                if l < 2:
                    act.wait_ge(f_sq, l * NM + c + 1)
                    last = nc.scalar.activation(csm[:, 3, cs], csm[:, 1, cs], ACT.Sqrt, scale=1.0 / D,
                                                bias=eps[:, 0:1])
                else:
                    last = nc.scalar.activation(csm[:, 3, cs], var(1), ACT.Sqrt, bias=eps[:, 0:1])
                last.then_inc(f_std, 1)

            def typed_messages():
                def turn(i, tt):
                    n = i * TU + tt
                    act.wait_ge(v_t, n + 1)
                    if not isinstance(n, int) or n >= 2:
                        act.wait_ge(v_w, n - 1)
                    turned(xt2[:, tt % 2, 0:D], bank[:, tt % 2, 0:D], 0).then_inc(v_xt, 1)

                def message(i, tt):
                    n = i * TU + tt
                    act.wait_ge(v_w, n + 1)
                    if not isinstance(n, int) or n >= 2:
                        act.wait_ge(v_v, n - 1)
                    nc.scalar.activation(em[:, tt % 2, :], bank[:, 2 + tt % 2, 0:3 * D], ACT.Relu).then_inc(v_m, 1)

                def copy0(i, tt):
                    n = i * TU + tt
                    act.wait_ge(v_v, n + 1)
                    if not isinstance(n, int) or n >= 2:
                        act.wait_ge(v_put, n - 1)
                    nc.scalar.activation(ev[:, tt % 2, :], bank[:, 6 + tt % 2, 0:D], ACT.Copy).then_inc(v_s0, 1)

                def body(i):
                    turn(i, 0)
                    for tt in range(TU + 1):
                        if tt + 1 < TU:
                            turn(i, tt + 1)
                        if tt < TU:
                            message(i, tt)
                        if tt:
                            copy0(i, tt - 1)
                run(act, body, 0, IT, (0,))

            def typed_targets():
                def turn(i, tt):
                    n = i * TU + tt
                    act.wait_ge(u_t, n + 1)
                    if not isinstance(n, int) or n >= 2:
                        act.wait_ge(u_p, n - 1)
                    turned(xt2[:, tt % 2, 0:D], bank[:, tt % 2, 0:D], 3).then_inc(u_xt, 1)

                def body(i):
                    turn(i, 0)
                    for tt in range(TU):
                        if tt + 1 < TU:
                            turn(i, tt + 1)
                        n, h = i * TU + tt, tt // CH
                        act.wait_ge(u_p, n + 1)
                        if tt % CH == 0:
                            if isinstance(i, int) and i == 0:
                                act.wait_ge(f_st[h], 3 * IT * 16)
                            else:
                                act.wait_ge(u_st[h], 16 * i)
                        nc.scalar.activation(stg[:, tt, :], bank[:, 2 + tt % 2, 0:D], ACT.Copy).then_inc(u_s0, 1)
                run(act, body, 0, IT, (0,))

            def last_rows():
                def body(i):
                    for h in range(2):
                        hs = slice(h * CH, (h + 1) * CH)
                        act.wait_ge(w_y, 2 * i + h + 1)
                        nc.scalar.activation(st3[:, hs, :], stg[:, hs, :], ACT.Square).then_inc(w_sq, 1)
                        act.wait_ge(w_v, 2 * i + h + 1)
                        nc.scalar.activation(csm[:, 0, hs], csm[:, 0, hs], ACT.Sqrt,
                                             scale=1.0 / D, bias=eps[:, 0:1]).then_inc(w_std, 1)
                run(act, body, 0, IT)

            run(act, dense, 0, PRE, (0,))
            for l in range(3):
                i = first[l]
                p1(l)
                logits(l)
                dense(i)
                dense(i + 1)
                dense(i + 2)
                dense(i + 3, lambda slot: finish(l, slot))
                deviations(l, NM - 1)
                run(act, dense, i + 4, first[l + 1])
            typed_targets()
            typed_messages()
            dense(NS - 2)
            dense(NS - 1)
            last_rows()

        @block.vector
        def _(dve):
            v = nc.vector
            st = Steps(dve, d_dve)
            cut = [0]
            DENSE = 40
            v.memset(brow[:, :], 0.0).then_inc(s_ms, 1)
            v.memset(eps[:, :], EPS)
            v.memset(ones3[:, :], 1.0)
            v.memset(zero[:, :], 0.0)
            v.memset(types[:, :], SKIP)
            v.memset(smo[:, 0:1], -BIG)
            v.memset(rowo[:, 0:1], 0.0)
            v.memset(hm[:, :], 0.0).then_inc(s_ms, 1)
            dve.wait_ge(s_ms, 2)
            for h in range(H):
                v.memset(hm[h * C:(h + 1) * C, h:h + 1], 1.0)
            dve.wait_ge(s_w, 16 * 23)
            cent = [(BCO[0], 1), (BCO[1], 1), (BNO, 3)]
            k = 0
            for off, n in cent:
                st.did(v.tensor_reduce(bmean[:, k:k + n], brow[:, off:off + n * D].rearrange("o (n d) -> o n d", n=n),
                                       AX_X, ALU.add))
                st.did(v.tensor_scalar(bmean[:, k:k + n], bmean[:, k:k + n], 1.0 / D, None, ALU.mult))
                w3 = brow[:, off:off + n * D].rearrange("o (n d) -> o n d", n=n)
                st.did(v.tensor_tensor(w3, w3, bc(bmean[:, k:k + n], D), ALU.subtract))
                if n == 1:
                    v.tensor_scalar(brow[:, BO[k] + D + 2 * H:BO[k] + WA], bmean[:, k:k + 1], -1.0, None, ALU.mult)
                k += n
            st.did(v.tensor_copy(bpart[:, 0, :], brow[:, :]))
            st.did(v.tensor_tensor(brest[:, :], brow[:, :], bpart[:, 0, :], ALU.subtract))
            st.did(v.tensor_copy(bpart[:, 1, :], brest[:, :]))
            st.did(v.tensor_tensor(brest[:, :], brest[:, :], bpart[:, 1, :], ALU.subtract))
            v.tensor_copy(bpart[:, 2, :], brest[:, :]).then_inc(s_pd, 1)
            for l in range(3):
                for k in range(2):
                    last = v.tensor_scalar(amat[:, k * H:(k + 1) * H], hm[:, :], av[:, 2 * l + k:2 * l + k + 1],
                                           None, ALU.mult)
                st.did(last)
                dve.wait_ge(s_ppe, 2 * l + 1)
                v.tensor_copy(wtr, bank[:, 0, 0:P]).then_inc(s_pd, 1)
                v.tensor_copy(wall[:, l, 0:D], wraw[:, l, :])
                st.did(v.tensor_reduce(wmean[:, l:l + 1], wraw[:, l, :], AX_X, ALU.add))
                st.did(v.tensor_scalar(wmean[:, l:l + 1], wmean[:, l:l + 1], 1.0 / D, None, ALU.mult))
                v.tensor_scalar(wall[:, l, D + 2 * H:WA], wmean[:, l:l + 1], -1.0, None, ALU.mult)
                if l < 2:
                    v.tensor_scalar(wcen[:, l, :], wraw[:, l, :], wmean[:, l:l + 1], None, ALU.subtract)
                else:
                    v.tensor_copy(wcen[:, l, :], wraw[:, l, :])
                dve.wait_ge(s_ppe, 2 * l + 2)
                v.tensor_copy(wall[:, l, D:D + 2 * H], bank[:, 1, 0:2 * H]).then_inc(s_pd, 1)
            dve.wait_ge(s_ppe, 7)
            w3 = wnt[:, :, :].rearrange("p j (n o) -> p (j n) o", n=3)
            for j in range(4):
                last = v.tensor_copy(wnt[:, j, :], bank[:, 2 + j, 0:3 * D])
            st.did(last)
            st.did(v.tensor_reduce(wmean[:, 4:16], w3, AX_X, ALU.add))
            st.did(v.tensor_scalar(wmean[:, 4:16], wmean[:, 4:16], 1.0 / D, None, ALU.mult))
            st.did(v.tensor_tensor(w3, w3, bc(wmean[:, 4:16], D), ALU.subtract))
            v.tensor_copy(wet[:, :], bank[:, 6, 0:3 * D])
            st.did(v.tensor_copy(identb[:, :], ident[:, :]))
            dve.wait_ge(s_i, 16 * 11)
            v.tensor_scalar(row_i[:, :], dst_i[:, 0, :], float(N - 1), None, ALU.min).then_inc(s_ready, 1)
            dve.wait_ge(s_i, 16 * 11)
            dve.wait_ge(s_id, 6)
            st.did(v.tensor_copy(dst_f[:, :, :], dst_i[:, :, :]))
            v.tensor_tensor(ns[:, :], dst_f[:, 0, :], dst_f[:, 1, :], ALU.not_equal)
            st.did(v.tensor_tensor(lastf[:, :], dst_f[:, 0, :], dst_f[:, 2, :], ALU.not_equal))
            v.tensor_scalar(negns[:, :], ns[:, :], -BIG, None, ALU.mult)
            v.tensor_scalar(keep[:, :], ns[:, :], -1.0, 1.0, ALU.mult, ALU.add)
            v.tensor_scalar(unlast[:, :], lastf[:, :], BIG, -BIG, ALU.mult, ALU.add)
            v.tensor_copy(last_r[:, :], lastf[:, ::-1])
            st.did(v.tensor_scalar(more_r[:, :], lastf[:, ::-1], -1.0, 1.0, ALU.mult, ALU.add))
            st.did(v.tensor_tensor_scan(none_r[:, :], more_r[:, :], zero[:, :], 1.0, ALU.mult, ALU.add))
            st.did(v.tensor_scalar(lastf[:, :], lastf[:, :], -float(SKIP), float(SKIP), ALU.mult, ALU.add))
            st.did(v.tensor_tensor(lastf[:, :], lastf[:, :], dst_f[:, 0, :], ALU.add))
            v.tensor_copy(put_i[:, :], lastf[:, :]).then_inc(s_put, 1)
            st.did(v.tensor_tensor_scan(kept[:, :], ns[:, :], ns[:, :], 0.0, ALU.max, ALU.max))
            st.did(v.tensor_scalar(negseen[:, :], kept[:, :], -BIG, None, ALU.mult))
            st.did(v.tensor_scalar(kept[:, :], kept[:, :], -1.0, 1.0, ALU.mult, ALU.add))
            dve.wait_ge(s_nt, 32)

            met = (s_ms, 2)

            def dense(i, beside=None, extra=0):
                if not beside:
                    beside = (lambda slot: None)
                DP = DENSE + extra
                st.enter(i - cut[0], DP)
                for k in range(2):
                    v.tensor_scalar(dmk[:, k, :], types[:, bass.ds(i * R, R)], float(k + 1), None, ALU.is_equal)

                def rstd(q, s):
                    dve.wait_ge(d_std, i * 16 + s * 4 + q + 1)
                    st.did(v.reciprocal(drs[:, s, q * G:(q + 1) * G], dstd[:, s, q * G:(q + 1) * G]))

                for l in range(2):
                    for q in range(Q):
                        rstd(q, l)
                        v.tensor_tensor(dxh[:, q * G:(q + 1) * G, :],
                                        bank[:, q, :].rearrange("p (g d) -> p g d", g=G),
                                        bc(drs[:, l, q * G:(q + 1) * G], D), ALU.mult).then_inc(d_xh, 1)
                        beside(l * Q + q)
                def add_x(q):
                    g = slice(q * G, (q + 1) * G)
                    dve.wait_ge(d_h, i * 12 + 8 + q + 1)
                    st.did(v.tensor_tensor(dxh[:, g, :], bank[:, q, :].rearrange("p (g d) -> p g d", g=G),
                                           dx[:, g, :], ALU.add))
                    for j in range(G):
                        last = v.bn_stats(dst6[:, q * G + j, :], dxh[:, q * G + j, :])
                    st.did(last, met)
                    for j in range(G):
                        last = v.bn_aggr(dmv[:, q * G + j, :], dst6[:, q * G + j, :])
                    last.then_inc(d_var, 1)

                add_x(0)
                for q in range(Q):
                    if q + 1 < Q:
                        add_x(q + 1)
                    rstd(q, 2)
                    for j in range(q * G, (q + 1) * G):
                        last = v.tensor_scalar(dxh[:, j, :], dxh[:, j, :], dmv[:, j, 0:1], drs[:, 2, j:j + 1],
                                               ALU.subtract, ALU.mult)
                    last.then_inc(d_xn, 1)
                    beside(2 * Q + q)
                if not isinstance(i, int) or i:
                    dve.wait_ge(d_st, i * 16)

                def norm(q):
                    rstd(q, 3)
                    g = slice(q * G, (q + 1) * G)
                    v.tensor_tensor(dy[:, g, :], dy[:, g, :], bc(drs[:, 3, g], D), ALU.mult).then_inc(d_o, 1)

                for q in range(Q):
                    for hh in range(2):
                        n = i * 8 + q * 2 + hh
                        g = slice(q * G + 2 * hh, q * G + 2 * hh + 2)
                        st.wait(d_s0, n + 1, met)
                        sel = dsel[:, 2 * hh:2 * hh + 2, :]
                        for k in range(2):
                            st.did(v.copy_predicated(sel, bc(dmk[:, k, g], D),
                                                     bank[:, 4 + 2 * hh:6 + 2 * hh, (k + 1) * D:(k + 2) * D]), met)
                        v.scalar_tensor_tensor(out=dy[:, g, :], in0=dxh[:, g, :], scalar=2.0, in1=sel,
                                               op0=ALU.mult, op1=ALU.add).then_inc(d_sel, 1)
                    if q:
                        norm(q - 1)
                    beside(3 * Q + q)
                norm(Q - 1)
                assert st.c == DP, st.c

            def run_dense(lo, hi, peel=()):
                cut[0] = lo
                leave = st.loop(hi - lo, DENSE)
                run(dve, dense, lo, hi, peel)
                leave()

            def dense_beside(i, piece, n, extra):
                cut[0] = i
                leave = st.loop(1, DENSE + extra)

                def beside(slot):
                    for c in pieces(slot, n):
                        piece(c)
                dense(i, beside, extra)
                leave()

            def p1(l):
                n0 = l * T

                def body(i):
                    for tt in range(TU):
                        n = n0 + i * TU + tt
                        b = bank[:, 2 + tt % 2, :].rearrange("p (o n) -> p o n", o=1)
                        dve.wait_ge(q_h, n + 1)
                        v.tensor_copy(rows[:, bass.ds(i * TU + tt, 1), :], b[:, :, 0:D])
                        v.tensor_copy(ls[:, bass.ds(i * TU + tt, 1), :], b[:, :, D:WA]).then_inc(q_ev, 1)
                run(dve, body, 0, IT)

            def logits(l):
                def lrelu(dest, a_, b_):
                    st.did(v.tensor_tensor(dest[:, :, :], a_, b_, ALU.add))
                    st.did(v.scalar_tensor_tensor(out=dest[:, :, :], in0=dest[:, :, :], scalar=NEG_SLOPE,
                                                  in1=dest[:, :, :], op0=ALU.mult, op1=ALU.max))
                lsv, ldv = (b[:, :, :].rearrange("p t h -> p h t") for b in (ls, ld))
                dve.wait_ge(q_ea, (l + 1) * T)
                dve.wait_ge(q_ev, (l + 1) * T)
                pe0 = MB[l]
                row = (lambda z: z[:, :].rearrange("p (o t) -> p o t", o=1).broadcast_to((P, H, T)))
                of_target = ldv[:, H:2 * H, :]
                if l:
                    st.did(v.tensor_tensor(fm[:, :, :], ldv[:, H:2 * H, ::-1], row(last_r), ALU.mult))
                    for h in range(H):
                        last = v.tensor_tensor_scan(fm[:, h, :], more_r[:, :], fm[:, h, :], 0.0, ALU.mult, ALU.add)
                    st.did(last)
                    v.tensor_copy(sm[:, 4, :], none_r[:, T - 1:T].broadcast_to((P, H)))
                    v.tensor_copy(sm[:, 5, :], fm[:, :, T - 1:T].rearrange("p h o -> p (h o)")).then_inc(m_dve, 1)
                    dve.wait_ge(m_pe, pe0 + 1)
                    v.memset(smo[:, 0:1], 0.0)
                    st.did(v.tensor_copy(smr[:, :, :], bank[0:H, 6, 0:2 * P]
                                         .rearrange("h (k p) -> h k p", k=2)[:, :, ::-1]))
                    st.did(v.tensor_tensor_scan(smo[:, 1:P + 1], smr[:, 0, :], smr[:, 1, :], 0.0,
                                                ALU.mult, ALU.add))
                    v.tensor_copy(smb, smo[:, P - 1::-1]).then_inc(m_dve, 1)
                    dve.wait_ge(m_pe, pe0 + 2)
                    st.did(v.tensor_copy(ci[:, :], bank[:, 7, 0:H]))
                    for h in range(H):
                        last = v.scalar_tensor_tensor(out=fm[:, h, :], in0=none_r[:, :], scalar=ci[:, h:h + 1],
                                                      in1=fm[:, h, :], op0=ALU.mult, op1=ALU.add)
                    st.did(last)
                    of_target = fm[:, :, ::-1]
                    pe0 += 2
                lrelu(e_s, lsv[:, 0:H, :], of_target)
                lrelu(e_f, ldv[:, 0:H, :], ldv[:, H:2 * H, :])
                st.did(v.tensor_tensor(e_f[:, :, :], e_f[:, :, :], row(unlast), ALU.add))
                st.did(v.tensor_tensor(fm[:, :, :], e_s[:, :, :], e_f[:, :, :], ALU.max))
                for h in range(H):
                    last = v.tensor_tensor_scan(fm[:, h, :], negns[:, :], fm[:, h, :], -BIG, ALU.add, ALU.max)
                st.did(last)
                v.tensor_copy(sm[:, 0, :], negseen[:, T - 1:T].broadcast_to((P, H)))
                v.tensor_copy(sm[:, 1, :], fm[:, :, T - 1:T].rearrange("p h o -> p (h o)")).then_inc(m_dve, 1)
                dve.wait_ge(m_pe, pe0 + 1)
                st.did(v.tensor_copy(smr[:, :, :], bank[0:H, 6, 0:2 * P].rearrange("h (k p) -> h k p", k=2)))
                if l:
                    st.did(v.memset(smo[:, 0:1], -BIG))
                v.tensor_tensor_scan(smo[:, 1:P + 1], smr[:, 0, :], smr[:, 1, :], -BIG, ALU.add, ALU.max)\
                    .then_inc(m_dve, 1)
                dve.wait_ge(m_pe, pe0 + 2)
                st.did(v.tensor_copy(ci[:, :], bank[:, 7, 0:H]))
                v.tensor_copy(mp[:, :, 0:1].rearrange("p h o -> p (h o)"), ci[:, :])
                for h in range(H):
                    last = v.scalar_tensor_tensor(out=mp[:, h, 1:T + 1], in0=negseen[:, :], scalar=ci[:, h:h + 1],
                                                  in1=fm[:, h, :], op0=ALU.add, op1=ALU.max)
                st.did(last)
                m = mp[:, :, 1:T + 1]
                st.did(v.tensor_tensor(ea[:, :, :], mp[:, :, 0:T], m, ALU.subtract))
                v.tensor_tensor(ea[:, :, :], ea[:, :, :], row(negns), ALU.add).then_inc(m_log, 1)
                v.tensor_tensor(e_s[:, :, :], e_s[:, :, :], m, ALU.subtract).then_inc(m_log, 1)
                v.tensor_tensor(e_f[:, :, :], e_f[:, :, :], m, ALU.subtract).then_inc(m_log, 1)
                dve.wait_ge(m_act, 3 * l + 3)
                st.did(v.tensor_tensor(es[:, :, :], e_s[:, :, :], e_f[:, :, :], ALU.add))
                for h in range(H):
                    v.tensor_tensor_scan(es[:, h, :], ea[:, h, :], es[:, h, :], 0.0, ALU.mult, ALU.add)
                    last = v.tensor_tensor_scan(ep[:, h, :], ea[:, h, :], zero[:, :], 1.0, ALU.mult, ALU.add)
                st.did(last)
                v.tensor_copy(sm[:, 2, :], ep[:, :, T - 1:T].rearrange("p h o -> p (h o)"))
                v.tensor_copy(sm[:, 3, :], es[:, :, T - 1:T].rearrange("p h o -> p (h o)")).then_inc(m_dve, 1)
                dve.wait_ge(m_pe, pe0 + 3)
                v.memset(smo[:, 0:1], 0.0)
                st.did(v.tensor_copy(smr[:, :, :], bank[0:H, 6, 0:2 * P].rearrange("h (k p) -> h k p", k=2)))
                v.tensor_tensor_scan(smo[:, 1:P + 1], smr[:, 0, :], smr[:, 1, :], 0.0, ALU.mult, ALU.add)\
                    .then_inc(m_dve, 1)
                dve.wait_ge(m_pe, pe0 + 4)
                st.did(v.tensor_copy(ci[:, :], bank[:, 7, 0:H]))
                for h in range(H):
                    last = v.scalar_tensor_tensor(out=es[:, h, :], in0=ep[:, h, :], scalar=ci[:, h:h + 1],
                                                  in1=es[:, h, :], op0=ALU.mult, op1=ALU.add)
                st.did(last)
                st.did(v.reciprocal(es[:, :, :], es[:, :, :]))

            def message(l, c):
                h, ts = c % 2, slice(c * CH, (c + 1) * CH)
                hs = std_[:, h * CH:(h + 1) * CH, :].rearrange("p t (h c) -> p t h c", h=H)
                dest = msg_f[:, :, ts].rearrange("p (h c) t -> p t h c", h=H)
                v.tensor_tensor(dest, rows[:, ts, :].rearrange("p t (h c) -> p t h c", h=H),
                                heads(e_s, c * CH, CH), ALU.mult)
                dve.wait_ge(l_h[h], 16 * (l * IT + c // 2 + 1))
                st.did(v.tensor_tensor(hs, hs, heads(e_f, c * CH, CH), ALU.mult))
                d2 = msg_f[:, :, ts].rearrange("p f t -> p t f")
                v.tensor_tensor(d2, d2, std_[:, h * CH:(h + 1) * CH, :], ALU.add).then_inc(p3, 1)

            def scan(a_of, c):
                for h in range(H):
                    f = msg_f[:, c + h * C, :]
                    last = v.tensor_tensor_scan(f, a_of(h), f, 0.0, ALU.mult, ALU.add)
                return last

            def carry(l, p_of, after):
                dve.wait_ge(*after)
                for h in range(H):
                    v.tensor_copy(rowa[:, 0, h * C:(h + 1) * C], p_of(h)[:, T - 1:T].broadcast_to((P, C)))
                v.tensor_copy(rowa[:, 1, :], msg_f[:, :, T - 1:T].rearrange("p f o -> p (f o)")).then_inc(r_dve, 1)
                dve.wait_ge(r_pe, 2 * l + 1)
                st.did(v.tensor_copy(rowt[:, :, :], bank[:, 6, 0:2 * P].rearrange("f (k p) -> f k p", k=2)))
                v.tensor_tensor_scan(rowo[:, 1:P + 1], rowt[:, 0, :], rowt[:, 1, :], 0.0, ALU.mult, ALU.add)\
                    .then_inc(r_dve, 1)
                dve.wait_ge(r_pe, 2 * l + 2)
                st.did(v.tensor_copy(cin, bank[:, 7, 0:P]))

            def fix(p_of, c):
                for h in range(H):
                    f = msg_f[:, c + h * C, :]
                    last = v.scalar_tensor_tensor(out=f, in0=p_of(h), scalar=cin[:, bass.ds(c + h * C, 1)],
                                                  in1=f, op0=ALU.mult, op1=ALU.add)
                return last

            def finish(l, c):
                h, cs = c % 2, slice(c % NR * CH, (c % NR + 1) * CH)
                hs = slice(h * CH, (h + 1) * CH)
                if l * NM + c >= NR:
                    dve.wait_ge(f_src, l * NM + c + 1 - NR)
                o, r = stg[:, hs, :], rows[:, c * CH:(c + 1) * CH, :]
                if l * IT + c // 2:
                    dve.wait_ge(f_st[h], 16 * (l * IT + c // 2))
                st.did(v.tensor_tensor(o.rearrange("p t (h c) -> p t h c", h=H),
                                       msg_f[:, :, c * CH:(c + 1) * CH].rearrange("p (h c) t -> p t h c", h=H),
                                       heads(es, c * CH, CH), ALU.mult))
                kinds = ((0, o),)
                if l == 2:
                    dve.wait_ge(l_x[h], 32 * (c // 2 + 1))
                    v.tensor_tensor(o, o, std_[:, hs, :], ALU.add)
                    st.did(v.tensor_tensor(r, r, st3[:, hs, :], ALU.add))
                    kinds = ((0, o), (1, r))
                for k, y in kinds:
                    for j in range(CH):
                        last = v.bn_stats(fst6[:, k, j, :], y[:, j, :])
                st.did(last)
                for k, y in kinds:
                    for j in range(CH):
                        last = v.bn_aggr(fmv[:, k, c % NR * CH + j, :], fst6[:, k, j, :])
                last.then_inc(f_v, 1)
                if c:
                    normalise(l, c - 1)

            def normalise(l, c):
                h, cs = c % 2, slice(c % NR * CH, (c % NR + 1) * CH)
                dve.wait_ge(f_std, l * NM + c + 1)
                v.reciprocal(csm[:, 4:6, cs], csm[:, 2:4, cs]).then_inc(f_y, 1)
                dve.wait_ge(f_y, l * NM + c + 1)
                for j in range(CH):
                    m = c % NR * CH + j
                    o = stg[:, h * CH + j, :]
                    last = v.tensor_scalar(o, o, fmv[:, 0, m, 0:1], csm[:, 4, m:m + 1], ALU.subtract, ALU.mult)
                last.then_inc(f_out, 1)

            def typed_messages():
                def select(i, tt):
                    n = i * TU + tt
                    st.wait(v_s0, n + 1, met)
                    st.did(v.copy_predicated(ev[:, tt % 2, :], ntc[:, 0, tt:tt + 1].broadcast_to((P, D)),
                                             bank[:, 6 + tt % 2, D:2 * D]), met)
                    v.copy_predicated(ev[:, tt % 2, :], ntc[:, 1, tt:tt + 1].broadcast_to((P, D)),
                                      bank[:, 6 + tt % 2, 2 * D:3 * D]).then_inc(v_sel, 1)
                    dve.wait_ge(v_sel, n + 1)
                    v.tensor_copy(msg_f[:, :, bass.ds(i * TU + tt, 1)].rearrange("p f o -> p (f o)"),
                                  ev[:, tt % 2, :]).then_inc(v_put, 1)

                def body(i):
                    DP = 1 + TU
                    st.enter(i, DP)
                    if not isinstance(i, int) or i:
                        dve.wait_ge(v_w, i * TU)
                    for k in range(K3):
                        last = v.tensor_scalar(etm[:, k, :], et_i[:, bass.ds(i * TU, TU)], float(k), -BIG,
                                               ALU.not_equal, ALU.mult)
                    last.then_inc(v_et, 1)
                    st.did(v.tensor_copy(ntc[:, :, :], ntm[:, :, bass.ds(i * TU, TU)]))
                    for tt in range(TU):
                        select(i, tt)
                    assert st.c == DP
                leave = st.loop(IT, 1 + TU)
                run(dve, body, 0, IT, (0,))
                leave()

            def typed_targets():
                def chunk(h):
                    hs = slice(h * CH, (h + 1) * CH)
                    v.scalar_tensor_tensor(out=stg[:, hs, :], in0=std_[:, hs, :], scalar=2.0, in1=stg[:, hs, :],
                                           op0=ALU.mult, op1=ALU.add).then_inc(u_y, 1)

                def body(i):
                    DP = 1 + TU
                    st.enter(i, DP)
                    st.did(v.tensor_copy(ntc[:, :, :], ntm[:, :, bass.ds(i * TU, TU)]))
                    for tt in range(TU):
                        n = i * TU + tt
                        st.wait(u_s0, n + 1, met)
                        for k in range(2):
                            ins = v.copy_predicated(stg[:, tt, :], ntc[:, k, tt:tt + 1].broadcast_to((P, D)),
                                                    bank[:, 2 + tt % 2, (k + 1) * D:(k + 2) * D])
                            if k == 0:
                                st.did(ins, met)
                        ins.then_inc(u_sel, 1)
                        if tt % CH == CH - 1:
                            dve.wait_ge(u_sel, n + 1)
                            chunk(tt // CH)
                    assert st.c == DP
                leave = st.loop(IT, 1 + TU)
                run(dve, body, 0, IT, (0,))
                leave()

            def last_rows():
                def chunk(i, h):
                    c = 2 * i + h
                    hs = slice(h * CH, (h + 1) * CH)
                    o = stg[:, hs, :]
                    st.did(v.tensor_tensor(o, kept[:, bass.ds(c * CH, CH)].rearrange("p (t o) -> p t o", o=1)
                                           .broadcast_to((P, CH, D)),
                                           cin.rearrange("p (o f) -> p o f", o=1).broadcast_to((P, CH, D)),
                                           ALU.mult))
                    st.did(v.tensor_tensor(o, o, msg_f[:, :, bass.ds(c * CH, CH)].rearrange("p f t -> p t f"),
                                           ALU.add))
                    dve.wait_ge(l_w[h], 16 * (i + 1))
                    v.tensor_tensor(o, o, std_[:, hs, :], ALU.add).then_inc(w_y, 1)
                    dve.wait_ge(w_sq, c + 1)
                    v.tensor_reduce(csm[:, 0, hs], st3[:, hs, :], AX_X, ALU.add).then_inc(w_v, 1)
                    dve.wait_ge(w_std, c + 1)
                    st.did(v.reciprocal(csm[:, 4, hs], csm[:, 0, hs]))
                    v.tensor_tensor(rows[:, bass.ds(c * CH, CH), :], o, bc(csm[:, 4, hs], D), ALU.mult)\
                        .then_inc(u_o, 1)

                def body(i):
                    st.enter(i, 6)
                    for h in range(2):
                        chunk(i, h)
                    assert st.c == 6
                leave = st.loop(IT, 6)
                run(dve, body, 0, IT)
                leave()

            run_dense(0, PRE, (0,))
            a_gat, p_gat = (lambda h: ea[:, h, :]), (lambda h: ep[:, h, :])
            for l in range(3):
                i = first[l]
                if l == 0:
                    dve.wait_ge(s_sv, 16 * 2 * IT)
                p1(l)
                logits(l)
                dense_beside(i, lambda c: message(l, c), NM, NM)
                dve.wait_ge(p3, (l + 1) * NM)
                dense_beside(i + 1, lambda c: scan(a_gat, c).then_inc(s_scan, 1), C, 0)
                carry(l, p_gat, (s_scan, 2 * l * C + C))
                dense_beside(i + 2, lambda c: fix(p_gat, c).then_inc(s_scan, 1), C, 0)
                dve.wait_ge(s_scan, 2 * (l + 1) * C)
                dense_beside(i + 3, lambda c: finish(l, c), NM, NM * (3 if l == 2 else 2))
                normalise(l, NM - 1)
                run_dense(i + 4, first[l + 1])
            dve.wait_ge(s_ntg, 16 * T)
            for k in range(2):
                last = v.tensor_scalar(ntm[:, k, :], nt_i[:, :], float(k + 1), None, ALU.is_equal)
            st.did(last)
            typed_targets()
            typed_messages()
            dve.wait_ge(v_put, T)
            a_typed, half = (lambda h: keep[:, :]), C // 2
            dense_beside(NS - 2, lambda c: scan(a_typed, c).then_inc(s_scan, 1), half, 0)
            dense_beside(NS - 1, lambda c: scan(a_typed, c + half).then_inc(s_scan, 1), half, 0)
            carry(3, lambda h: kept[:, :], (s_scan, 7 * C))
            last_rows()


_INS = ["x", "src", "dst", "edge_type_3", "node_type_3",
        *(f"L0_gnn_{n}{l}" for l in range(3) for n in ("W", "a_src", "a_dst", "b")),
        "L0_gnn_ln0_g", "L0_gnn_ln0_b", "L0_gnn_ln1_g", "L0_gnn_ln1_b",
        "L1_gnn_W_e", "L1_gnn_b_e", "L1_gnn_W_n", "L1_gnn_b_n"]


def kernel(**inputs):
    import numpy as _np
    import concourse.bacc as _bacc
    from concourse import mybir as _mybir
    from concourse.bass_utils import run_bass_kernel_spmd as _run

    nc = _bacc.Bacc("TRN2", target_bir_lowering=False, num_devices=1)
    arrays, aps = {}, {}
    for name in _INS:
        v = _np.ascontiguousarray(inputs[name])
        arrays[f"in_{name}_dram"] = v
        aps[name] = nc.dram_tensor(f"in_{name}_dram", v.shape, _mybir.dt.from_np(v.dtype), kind="ExternalInput").ap()
    shape = inputs["x"].shape
    out = nc.dram_tensor("out_0_dram", shape, _mybir.dt.from_np(_np.dtype("float32")), kind="ExternalOutput").ap()
    build(nc, aps, out)
    r = _run(nc, [arrays], core_ids=[0])
    return r.results[0]["out_0_dram"]
```

```python
from contextlib import ExitStack

import concourse.bass as bass
from concourse import mybir

ALU = mybir.AluOpType
ACT = mybir.ActivationFunctionType
AX_X = mybir.AxisListType.X
F32 = mybir.dt.float32
I32 = mybir.dt.int32
BF16 = mybir.dt.bfloat16

P = 128
EPS = 1e-5
NEG_SLOPE = 0.2
BIG = 1.0e30
SKIP = 1000000


class Steps:

    def __init__(self, eng, sem):
        self.eng, self.sem, self.base, self.c, self.i, self.per = eng, sem, 0, 0, 0, 0
        self.due = eng.alloc_register("due")

    def enter(self, i, per):
        self.i, self.per, self.c = i, per, 0

    def loop(self, bodies, per):
        self.base, self.c = self.base + self.c, 0

        def leave():
            self.base, self.i, self.per, self.c = self.base + bodies * per, 0, 0, 0
        return leave

    def wait(self, sem, value, first=None):
        if first and not isinstance(value, int):
            self.eng.reg_mov(self.due, value)
            value = self.due
            self.eng.wait_ge(*first)
        self.eng.wait_ge(sem, value)

    def mark(self, ins):
        ins.then_inc(self.sem, 1)
        self.c += 1
        return self.base + self.i * self.per + self.c

    def until(self, mark, first=None):
        self.wait(self.sem, mark, first)

    def did(self, ins, first=None):
        ins.then_inc(self.sem, 1)
        self.c += 1
        self.wait(self.sem, self.base + self.i * self.per + self.c, first)


def run(eng, body, lo, hi, peel=()):
    i = lo
    while i < hi:
        if i in peel:
            body(i)
            i += 1
            continue
        end = min([x for x in peel if x > i] + [hi])
        end = min(end, hi)
        if end - i == 1:
            body(i)
        else:
            with eng.Fori(i, end) as r:
                body(r)
        i = end


def build(nc, a, out):
    x, src, dst = a["x"], a["src"], a["dst"]
    etype, ntype = a["edge_type_3"], a["node_type_3"]
    W = [a[f"L0_gnn_W{l}"] for l in range(3)]
    A_S = [a[f"L0_gnn_a_src{l}"] for l in range(3)]
    A_D = [a[f"L0_gnn_a_dst{l}"] for l in range(3)]
    B = [a[f"L0_gnn_b{l}"] for l in range(3)]
    LN = [(a[f"L0_gnn_ln{l}_g"], a[f"L0_gnn_ln{l}_b"]) for l in range(2)]
    WE, BE, WN, BN = a["L1_gnn_W_e"], a["L1_gnn_b_e"], a["L1_gnn_W_n"], a["L1_gnn_b_n"]

    N, D = x.shape
    E = src.shape[0]
    H, C = A_S[0].shape
    K3 = WE.shape[0]
    assert D == P and H * C == P and K3 == 3

    G, Q = 4, 4
    R = G * Q
    SB = P * R
    NS = -(-N // SB)
    LAST = NS - 1
    T = -(-E // P)
    CH = 7
    assert T % (2 * CH) == 0
    IT = T // (2 * CH)
    TU = 2 * CH
    FULL = E // T
    TAIL = E - FULL * T
    assert FULL == P - 1 and 0 < TAIL < T
    WA = P + 2 * H + 1
    assert N % (NS * R) == 0 and N // (NS * R) <= P
    MB = [0, 4, 10]
    PRE = 3
    NM = 2 * IT
    first = [PRE]
    for l in range(3):
        first.append(first[l] + 7)
    assert first[3] == NS - 1
    SOFTMAX = {0: 0, 1: 1, 3: 2, 4: 3, 6: 4, 7: 5, 9: 6, 10: 7}
    TRIPS = {1: 0, 2: 1, 4: 2, 5: 3, 8: 4, 10: 5}
    EXPS = 7
    SLOTS = 5 * Q

    def pieces(slot, n, part=0, parts=1, slots=SLOTS):
        k, all_ = part * slots + slot, parts * slots
        return range(n * k // all_, n * (k + 1) // all_) if slot < slots else ()

    LAYERS = 3 * Q + 2

    table = [nc.dram_tensor(f"target_rows_{l}", (T * P, D), F32).ap() for l in range(4)]
    src0 = nc.dram_tensor("source_x_rows", (T * P, D), F32).ap()
    hdd = nc.dram_tensor("target_h_rows", (T * P, D), F32).ap()
    edge_of = nc.dram_tensor("edge_of_node", (N, 1), I32).ap()

    def chunks(ap):
        return ap.rearrange("(p c r) d -> c p (r d)", p=P, r=CH)

    def sblocks(ap):
        return ap[0:LAST * SB, :].rearrange("(i p r) d -> i p (r d)", p=P, r=R)

    def tail_block(ap):
        return ap[N - SB:N, :].rearrange("(p r) d -> p (r d)", r=R)

    with ExitStack() as ctx:
        def sb(name, shape, dt=F32):
            return ctx.enter_context(nc.sbuf_tensor(name, shape, dt))

        def sem(name):
            return ctx.enter_context(nc.semaphore(name))

        rows = sb("rows", [P, T, D])
        msg = sb("msg", [P, D * T])
        msg_f = msg[:, :].rearrange("p (f t) -> p f t", t=T)
        msg_r = msg[:, :].rearrange("p (t f) -> p t f", f=D)
        bank = ctx.enter_context(nc.psum_tensor("bank", [P, 8, 512], F32))

        dx = sb("dx", [P, R, D])
        dxt = sb("dxt", [P, Q, G * D])
        dxh = sb("dxh", [P, R, D])
        dy = dxh
        dxt0 = sb("dxt0", [P, Q, G * D])
        dsel = sb("dsel", [P, G, D])
        dstd = sb("dstd", [P, 4, R])
        drs = sb("drs", [P, 4, R])
        dmk = sb("dmk", [P, 2, R], I32)
        junk = sb("junk", [P, G, D])

        stg = sb("stg", [P, TU, D])
        std_ = sb("std_", [P, TU, D])
        st3 = sb("st3", [P, TU, D])
        xt2 = sb("xt2", [P, 2, 2 * D])
        ev = sb("ev", [P, 2, D])
        NR = 4
        csm = sb("csm", [P, 8, NR * CH])
        fst6 = sb("fst6", [P, CH, 6])
        fmv = sb("fmv", [P, NR * CH, 2])

        ls = sb("ls", [P, T, 2 * H + 1])
        ld = sb("ld", [P, T, 2 * H])
        em = ls[:, :, :].rearrange("p t h -> p (t h)")[:, 0:6 * D].rearrange("p (u n) -> p u n", u=2)
        e_s = sb("e_s", [P, H, T])
        e_f = sb("e_f", [P, H, T])
        fm = sb("fm", [P, H, T])
        mp = sb("mp", [P, H, T + 1])
        ea = sb("ea", [P, H, T])
        es = sb("es", [P, H, T])
        ep = sb("ep", [P, H, T])
        sm = sb("sm", [P, 6, H])
        smr = sb("smr", [H, 2, P])
        smo = sb("smo", [H, P + 1])
        smb = smr[:, 0, :]
        ci = sb("ci", [P, H])
        rowa = sb("rowa", [P, 2, P])
        rowt = sb("rowt", [P, 2, P])
        rowo = sb("rowo", [P, P + 1])
        cin = rowt[:, 0, :]

        dst_i = sb("dst_i", [P, 3, T], I32)
        dst_f = e_s[:, 0:3, :]
        src_i = sb("src_i", [P, T], I32)
        et_i = sb("et_i", [P, T], I32)
        row_i = sb("row_i", [P, T], I32)
        nt_i = sb("nt_i", [P, T], I32)
        ns = e_s[:, 3, :]
        negns = sb("negns", [P, T])
        negseen = sb("negseen", [P, T])
        unlast = sb("unlast", [P, T])
        last_r = sb("last_r", [P, T])
        more_r = sb("more_r", [P, T])
        none_r = sb("none_r", [P, T])
        keep = sb("keep", [P, T])
        kept = sb("kept", [P, T])
        lastf = e_f[:, 0, :]
        put_i = sb("put_i", [P, T], I32)
        pos_i = sb("pos_i", [P, T], I32)
        eid = sb("eid", [P, T], I32)
        zero = sb("zero", [P, T])
        etm = sb("etm", [P, 3, TU], BF16)
        ntm = sb("ntm", [P, 2, T], I32)
        ntc = sb("ntc", [P, 2, TU], I32)
        types = sb("types", [P, NS * R], I32)

        ident = sb("ident", [P, P])
        centre = sb("centre", [P, P])
        identb = sb("identb", [P, P], BF16)
        ones3 = sb("ones3", [3, P], BF16)
        eps = sb("eps", [P, 1])
        wall = sb("wall", [P, 3, WA])
        wcen = sb("wcen", [P, 3, D])
        wnt = sb("wnt", [P, 4, 3 * D])
        wet = sb("wet", [P, 3 * D])
        gb = sb("gb", [P, 4])
        hm = sb("hm", [P, H])
        av = sb("av", [P, 6])
        amat = sb("amat", [P, 2 * H])
        wmean = sb("wmean", [P, 24])
        BO = [l * WA for l in range(3)]
        BEO = 3 * WA
        BNO = BEO + 3 * D
        BCO = [BNO + 3 * D + l * D for l in range(3)]
        BT = BNO + 6 * D
        bias3 = sb("bias3", [3, BT], BF16)
        bmean = sb("bmean", [1, 8])

        wraw = msg[:, 0:3 * D].rearrange("p (l d) -> p l d", l=3)
        wnraw = msg[:, 3 * D:15 * D].rearrange("p (n k) -> p n k", n=3)
        weraw = msg[:, 15 * D:18 * D].rearrange("p (n k) -> p n k", n=3)

        wtr = msg[:, 90 * D:91 * D]
        brow = msg[0:1, 18 * D:18 * D + BT]
        brest = msg[0:1, 18 * D + BT:18 * D + 2 * BT]
        bpart = msg[0:1, 18 * D + 2 * BT:18 * D + 4 * BT].bitcast(BF16)[:, 0:3 * BT].rearrange("o (k n) -> o k n", k=3)

        s_w = sem("weights_loaded")
        s_i = sem("indices_loaded")
        s_nt = sem("node_types_loaded")
        s_ms = sem("memsets_done")
        s_id = sem("identity_ready")
        s_pd = sem("prelude_dve")
        s_ppe = sem("prelude_pe")
        s_ready = sem("weights_ready")
        s_b3 = sem("bias_parts_moved")
        s_put = sem("scatter_indices_ready")
        s_tabi = sem("edge_table_cleared")
        s_tabw = sem("edge_table_written")
        s_tabg = sem("edge_positions_gathered")
        s_ntg = sem("target_types_gathered")
        s_g = [sem(f"source_rows_gathered_{h}") for h in range(2)]
        s_gd = [sem(f"target_rows_gathered_{h}") for h in range(2)]
        s_sv = sem("source_x_rows_saved")
        s_svd = sem("target_x_rows_saved")
        s_out = sem("target_outputs_scattered")
        d_ld = sem("d_x_loaded")
        d_t = sem("d_transposed")
        d_xt = sem("d_xt_ready")
        d_h = sem("d_h_ready")
        d_ss = sem("d_squares_summed")
        d_std = sem("d_std_ready")
        d_xh = sem("d_normalised")
        d_p = sem("d_typed_ready")
        d_s0 = sem("d_type0_copied")
        d_sel = sem("d_selected")
        d_o = sem("d_out_ready")
        d_st = sem("d_stored")
        d_dve = sem("d_dve_steps")
        l_s = [sem(f"stage_source_{h}") for h in range(2)]
        l_d = [sem(f"stage_target_{h}") for h in range(2)]
        q_t = sem("q_transposed")
        q_xt = sem("q_xt_ready")
        q_h = sem("q_h_ready")
        q_ev = sem("q_source_h_out")
        q_ea = sem("q_target_h_out")
        q_st = [sem(f"q_h_stored_{h}") for h in range(2)]
        m_dve = sem("m_dve")
        m_act = sem("m_act")
        m_pe = sem("m_pe")
        m_log = sem("logit_weights_ready")
        m_own = sem("own_terms_weighted")
        m_ci = sem("softmax_carries_read")
        p3 = sem("messages_written")
        l_h = [sem(f"target_h_loaded_{h}") for h in range(2)]
        r_dve = sem("r_dve")
        r_pe = sem("r_pe")
        s_scan = sem("scan_pieces_done")
        f_sq = sem("f_squares_ready")
        f_y = sem("f_reciprocals_ready")
        f_std = sem("f_std_ready")
        f_o = sem("f_target_rows_divided")
        f_x = sem("f_source_residual_added")
        f_mean = sem("f_source_means_ready")
        f_src = sem("f_source_rows_ready")
        f_v = sem("f_variances_ready")
        f_out = sem("f_chunk_done")
        f_st = [sem(f"f_stored_{h}") for h in range(2)]
        l_x = [sem(f"x_chunks_loaded_{h}") for h in range(2)]
        v_t = sem("v_transposed")
        v_xt = sem("v_xt_ready")
        v_w = sem("v_messages_ready")
        v_et = sem("v_type_flags_ready")
        v_m = sem("v_messages_out")
        v_v = sem("v_projected")
        v_s0 = sem("v_type0_copied")
        v_sel = sem("v_selected")
        v_put = sem("v_written")
        v_dve = sem("v_dve")
        l_v = [sem(f"v_staged_{h}") for h in range(2)]
        u_t = sem("u_transposed")
        u_xt = sem("u_xt_ready")
        u_p = sem("u_projected")
        u_s0 = sem("u_type0_copied")
        u_sel = sem("u_selected")
        u_y = sem("u_own_part_ready")
        u_st = [sem(f"u_own_part_stored_{h}") for h in range(2)]
        w_y = sem("w_rows_ready")
        w_sq = sem("w_squares_ready")
        w_v = sem("w_sums_ready")
        w_std = sem("w_std_ready")
        u_o = sem("u_out_ready")
        l_w = [sem(f"w_staged_{h}") for h in range(2)]
        l_u = [sem(f"u_staged_{h}") for h in range(2)]

        def bc(ap, n):
            return ap.rearrange("p (a o) -> p a o", o=1).broadcast_to((ap.shape[0], ap.shape[1], n))

        def heads(ap, t0, n):
            v = ap[:, :, bass.ds(t0, n)].rearrange("p h (t o) -> p t h o", o=1)
            return v.broadcast_to((P, n, H, C))

        block = ctx.enter_context(nc.Block())

        @block.sync
        def _(sp):
            sp.dma_start(wraw[:, 0, :], W[0]).then_inc(s_w, 16)
            sp.dma_start(wraw[:, 1, :], W[1]).then_inc(s_w, 16)
            sp.dma_start(wraw[:, 2, :], W[2]).then_inc(s_w, 16)
            for l in range(3):
                sp.dma_start(av[:, 2 * l:2 * l + 1], A_S[l].rearrange("h (c o) -> (h c) o", o=1)).then_inc(s_w, 16)
                sp.dma_start(av[:, 2 * l + 1:2 * l + 2], A_D[l].rearrange("h (c o) -> (h c) o", o=1)).then_inc(s_w, 16)
            for l in range(2):
                for k in range(2):
                    sp.dma_start(gb[:, 2 * l + k:2 * l + k + 1],
                                 LN[l][k].rearrange("(c o) -> c o", o=1)).then_inc(s_w, 16)
            sp.dma_start(wnraw, WN.rearrange("n o k -> o n k")).then_inc(s_w, 16)
            sp.dma_start(weraw, WE.rearrange("n o k -> o n k")).then_inc(s_w, 16)
            sp.wait_ge(s_ms, 1)
            for l in range(3):
                for off in (BO[l], BCO[l]):
                    sp.dma_start(brow[:, off:off + D], B[l].rearrange("(o d) -> o d", o=1)).then_inc(s_w, 16)
            sp.dma_start(brow[:, BEO:BEO + 3 * D], BE.rearrange("(o n) d -> o (n d)", o=1)).then_inc(s_w, 16)
            sp.dma_start(brow[:, BNO:BNO + 3 * D], BN.rearrange("(o n) d -> o (n d)", o=1)).then_inc(s_w, 16)
            sp.dma_start(dx[:, :, :].rearrange("p r d -> p (r d)"), sblocks(x)[0, :, :]).then_inc(d_ld, 16)
            sp.wait_ge(s_ms, 2)
            sp.dma_start(edge_of.rearrange("(p r) o -> p (r o)", r=NS * R), types[0:N // (NS * R), :])\
                .then_inc(s_tabi, 16)
            sp.wait_ge(s_tabi, 16)
            sp.dma_start(types[:, 0:LAST * R].rearrange("p (i r) -> p i r", r=R),
                         ntype[0:LAST * SB].rearrange("(i p r) -> p i r", p=P, r=R)).then_inc(s_nt, 16)
            sp.dma_start(types[:, LAST * R:NS * R],
                         ntype[N - SB:N].rearrange("(p r) -> p r", r=R)).then_inc(s_nt, 16)
            sp.wait_ge(s_pd, 1)
            for k in range(3):
                sp.dma_start(bias3[k:k + 1, :], bpart[:, k, :]).then_inc(s_b3, 16)

            def dense(i, beside=None):
                for slot in range(SLOTS):
                    if beside:
                        beside(slot)
                    if slot == Q - 1 and (not isinstance(i, int) or i < LAST):
                        nxt = tail_block(x) if isinstance(i, int) and i + 1 == LAST else sblocks(x)[i + 1, :, :]
                        sp.wait_ge(d_t, 4 * Q * i + Q)
                        sp.dma_start(dx[:, :, :].rearrange("p r d -> p (r d)"), nxt).then_inc(d_ld, 16)
                dest = tail_block(out) if isinstance(i, int) and i == LAST else sblocks(out)[i, :, :]
                for q in range(Q):
                    sp.wait_ge(d_o, Q * i + q + 1)
                    sp.dma_start(dest[:, q * G * D:(q + 1) * G * D],
                                 dy[:, q * G:(q + 1) * G, :].rearrange("p r d -> p (r d)")).then_inc(d_st, 16)

            def stage(buf, h):
                return buf[:, h * CH:(h + 1) * CH, :].rearrange("p r d -> p (r d)")

            def stage_rows(c, h, sems):
                sp.dma_start(stage(stg, h), rows[:, bass.ds(c * CH, CH), :].rearrange("p r d -> p (r d)"))\
                    .then_inc(sems[h], 16)

            def p1(l):
                n0 = l * T

                def stage_both(c, n, h):
                    if l:
                        sp.dma_start(stage(std_, h), chunks(table[l])[c, :, :]).then_inc(l_d[h], 16)
                        sp.wait_ge(s_g[h], 16 * CH * (l * IT + n + 1))
                        stage_rows(c, h, l_s)
                    else:
                        stage_rows(c, h, l_s)
                        sp.wait_ge(s_gd[h], 16 * CH * (n + 1))
                        sp.dma_start(stage(std_, h), msg_r[:, bass.ds(c * CH, CH), :].rearrange("p r d -> p (r d)"))\
                            .then_inc(l_d[h], 16)

                def body(i):
                    for h in range(2):
                        sp.wait_ge(q_t, n0 + i * TU + (h + 1) * CH)
                        stage_both(2 * i + 2 + h, i + 1, h)
                        sp.wait_ge(q_ea, n0 + i * TU + (h + 1) * CH)
                        sp.dma_start(chunks(hdd)[2 * i + h, :, :], stage(st3, h)).then_inc(q_st[h], 16)
                if l == 0:
                    for h in range(2):
                        sp.wait_ge(s_g[h], 16 * CH * IT)
                for h in range(2):
                    stage_both(h, 0, h)
                run(sp, body, 0, IT - 1, range(IT) if l == 0 else ())
                for h in range(2):
                    sp.wait_ge(q_ea, n0 + (IT - 1) * TU + (h + 1) * CH)
                    sp.dma_start(chunks(hdd)[2 * (IT - 1) + h, :, :], stage(st3, h)).then_inc(q_st[h], 16)

            def load_h(l, c):
                if c >= 2:
                    sp.wait_ge(p3, l * NM + c - 1)
                sp.dma_start(stage(std_, c % 2), chunks(hdd)[c, :, :]).then_inc(l_h[c % 2], 16)

            def messages(l, slot, part):
                for c in pieces(slot, NM - 2, part, 2):
                    load_h(l, c + 2)

            def load_x(c):
                sp.dma_start(stage(std_, c % 2), chunks(table[0])[c, :, :]).then_inc(l_x[c % 2], 16)
                sp.dma_start(stage(st3, c % 2), chunks(src0)[c, :, :]).then_inc(l_x[c % 2], 16)

            def finish(l, slot, part):
                for c in pieces(slot, NM, part, 2, LAYERS):
                    if l == 2 and c >= 2:
                        sp.wait_ge(f_v, l * NM + c - 1)
                        sp.wait_ge(f_sq, l * NM + c - 1)
                        load_x(c)
                    if c >= 2:
                        store_rows(l, c - 2)

            def store_rows(l, c):
                sp.wait_ge(f_out, l * NM + c + 1)
                sp.dma_start(chunks(table[l + 1])[c, :, :], stage(stg, c % 2)).then_inc(f_st[c % 2], 16)

            def typed_messages():
                def body(i):
                    for h in range(2):
                        sp.wait_ge(v_t, i * TU + (h + 1) * CH)
                        stage_rows(2 * i + 2 + h, h, l_v)
                for h in range(2):
                    sp.wait_ge(u_st[h], IT * 16)
                    sp.wait_ge(s_g[h], 16 * CH * 4 * IT)
                    stage_rows(h, h, l_v)
                run(sp, body, 0, IT - 1)

            def typed_targets():
                def store(c, h):
                    sp.wait_ge(u_y, c + 1)
                    sp.dma_start(chunks(hdd)[c, :, :], stage(stg, h)).then_inc(u_st[h], 16)

                def body(i):
                    for h in range(2):
                        store(2 * i + h, h)
                        sp.dma_start(stage(std_, h), chunks(table[3])[2 * i + 2 + h, :, :]).then_inc(l_u[h], 16)
                for h in range(2):
                    sp.wait_ge(f_st[0], 3 * IT * 16)
                    sp.wait_ge(f_st[1], 3 * IT * 16)
                    sp.dma_start(stage(std_, h), chunks(table[3])[h, :, :]).then_inc(l_u[h], 16)
                run(sp, body, 0, IT - 1)
                for h in range(2):
                    store(2 * (IT - 1) + h, h)

            def last_rows():
                def body(i):
                    for h in range(2):
                        sp.wait_ge(w_y, 2 * i + h + 1)
                        sp.dma_start(stage(std_, h), chunks(hdd)[2 * i + 2 + h, :, :]).then_inc(l_w[h], 16)
                for h in range(2):
                    sp.wait_ge(u_st[h], IT * 16)
                    sp.dma_start(stage(std_, h), chunks(hdd)[h, :, :]).then_inc(l_w[h], 16)
                run(sp, body, 0, IT - 1)

            run(sp, dense, 0, PRE, (LAST - 1, LAST))
            for l in range(3):
                i = first[l]
                if l:
                    for h in range(2):
                        sp.wait_ge(f_st[h], 16 * l * IT)
                p1(l)
                for h in range(2):
                    sp.wait_ge(q_st[h], (l + 1) * IT * 16)
                for c in range(2):
                    load_h(l, c)
                dense(i)
                dense(i + 1, lambda slot: messages(l, slot, 0))
                dense(i + 2, lambda slot: messages(l, slot, 1))
                dense(i + 3)
                dense(i + 4)
                if l == 2:
                    sp.wait_ge(s_sv, 16 * NM)
                    sp.wait_ge(s_svd, 16 * NM)
                    for c in range(2):
                        load_x(c)
                dense(i + 5, lambda slot: finish(l, slot, 0))
                dense(i + 6, lambda slot: finish(l, slot, 1))
                for c in range(NM - 2, NM):
                    store_rows(l, c)
            typed_targets()
            typed_messages()
            dense(NS - 1)
            last_rows()
            sp.wait_ge(d_st, 16 * Q * NS)
            sp.wait_ge(s_out, 16 * T)

        @block.gpsimd
        def _(pool):
            pool.memset(ident[:, :], 0.0).then_inc(s_id, 1)
            pool.wait_ge(s_id, 1)
            pool.affine_select(out=ident[:, :], in_=ident[:, :], compare_op=ALU.not_equal, fill=1.0,
                               base=0, pattern=[[-1, P]], channel_multiplier=1).then_inc(s_id, 1)
            for n, (part, value) in enumerate(((dst_i[96:P, :, :], SKIP), (src_i[96:P, :], 0),
                                               (et_i[96:P, :], K3), (dst_i[0:1, 1, 0:1], -1))):
                pool.wait_ge(s_id, n + 2)
                pool.memset(part, value).then_inc(s_id, 1)
            pool.wait_ge(s_id, 6)
            flat = dst[0:FULL * T].rearrange("(p t) -> p t", t=T)
            pool.dma_start(dst_i[0:FULL, 0, :], flat).then_inc(s_i, 16)
            pool.dma_start(dst_i[FULL:P, 0, 0:TAIL], dst[FULL * T:E].rearrange("(o t) -> o t", o=1)).then_inc(s_i, 16)
            pool.dma_start(dst_i[0:1, 1, 1:T], dst[0:T - 1].rearrange("(o t) -> o t", o=1)).then_inc(s_i, 16)
            pool.dma_start(dst_i[1:FULL, 1, :], dst[T - 1:FULL * T - 1].rearrange("(p t) -> p t", t=T)).then_inc(s_i, 16)
            pool.dma_start(dst_i[FULL:P, 1, 0:TAIL + 1],
                           dst[FULL * T - 1:E].rearrange("(o t) -> o t", o=1)).then_inc(s_i, 16)
            pool.dma_start(dst_i[0:FULL, 2, :], dst[1:FULL * T + 1].rearrange("(p t) -> p t", t=T)).then_inc(s_i, 16)
            pool.dma_start(dst_i[FULL:P, 2, 0:TAIL - 1],
                           dst[FULL * T + 1:E].rearrange("(o t) -> o t", o=1)).then_inc(s_i, 16)
            pool.dma_start(src_i[0:FULL, :], src[0:FULL * T].rearrange("(p t) -> p t", t=T)).then_inc(s_i, 16)
            pool.dma_start(src_i[FULL:P, 0:TAIL], src[FULL * T:E].rearrange("(o t) -> o t", o=1)).then_inc(s_i, 16)
            pool.dma_start(et_i[0:FULL, :], etype[0:FULL * T].rearrange("(p t) -> p t", t=T)).then_inc(s_i, 16)
            pool.dma_start(et_i[FULL:P, 0:TAIL], etype[FULL * T:E].rearrange("(o t) -> o t", o=1)).then_inc(s_i, 16)
            pool.iota(eid[:, :], pattern=[[1, T]], base=0, channel_multiplier=T).then_inc(s_id, 1)
            pool.memset(pos_i[:, :], SKIP).then_inc(s_id, 1)
            pool.memset(nt_i[:, :], 0).then_inc(s_id, 1)
            pool.wait_ge(s_id, 9)
            pool.wait_ge(s_i, 16 * 11)

            def gather(dest, tab, idx, done, bound):
                pool.indirect_dma_start(out=dest, out_offset=None, in_=tab,
                                        in_offset=bass.IndirectOffsetOnAxis(ap=idx, axis=0),
                                        bounds_check=bound, oob_is_err=False).then_inc(done, 16)

            def gather_rows(dest, tab, idx, done, rnd, bound, keep_in=None, kept=None):
                for c in range(NM + 1):
                    if c < NM:
                        if rnd * IT + c // 2:
                            pool.wait_ge(done[c % 2], 16 * CH * (rnd * IT + c // 2))
                        for t in range(c * CH, (c + 1) * CH):
                            gather(dest[:, t, :], tab, idx[:, t:t + 1], done[c % 2], bound)
                    if c and keep_in is not None:
                        pool.wait_ge(done[(c - 1) % 2], 16 * CH * ((c - 1) // 2 + 1))
                        pool.dma_start(keep_in.rearrange("(p t) d -> p t d", p=P)[:, (c - 1) * CH:c * CH, :],
                                       dest[:, (c - 1) * CH:c * CH, :]).then_inc(kept, 16)

            gather_rows(rows, x, src_i, s_g, 0, N - 1, src0, s_sv)
            pool.wait_ge(s_b3, 48)
            pool.wait_ge(s_ready, 1)
            gather_rows(msg_r, x, row_i, s_gd, 0, N - 1, table[0], s_svd)
            pool.wait_ge(s_put, 1)
            pool.wait_ge(s_tabi, 16)
            for t in range(T):
                pool.indirect_dma_start(out=edge_of, out_offset=bass.IndirectOffsetOnAxis(ap=put_i[:, t:t + 1], axis=0),
                                        in_=eid[:, t:t + 1], in_offset=None,
                                        bounds_check=N - 1, oob_is_err=False).then_inc(s_tabw, 16)
            ntab = ntype.rearrange("(n o) -> n o", o=1)
            for t in range(T):
                gather(nt_i[:, t:t + 1], ntab, row_i[:, t:t + 1], s_ntg, N - 1)
            pool.wait_ge(s_tabw, 16 * T)
            for t in range(T):
                gather(pos_i[:, t:t + 1], edge_of, src_i[:, t:t + 1], s_tabg, N - 1)
            pool.wait_ge(s_tabg, 16 * T)
            for l in range(1, 4):
                for c in range(NM + 1):
                    if l == 3 and c < NM:
                        h, r = c % 2, rows[:, c * CH:(c + 1) * CH, :]
                        if c == 0:
                            pool.wait_ge(p3, 3 * NM)
                        pool.wait_ge(l_x[h], 32 * (c // 2 + 1))
                        pool.tensor_tensor(r, r, st3[:, h * CH:(h + 1) * CH, :], ALU.add).then_inc(f_x, 1)
                    if c:
                        pool.wait_ge(f_y, (l - 1) * NM + c)
                        for j in range(CH):
                            t, m = (c - 1) * CH + j, (c - 1) % NR * CH + j
                            off = ls[:, t, 2 * H:2 * H + 1] if l < 3 else csm[:, 6, m:m + 1]
                            last = pool.tensor_scalar(rows[:, t, :], rows[:, t, :], off, csm[:, 5, m:m + 1],
                                                      ALU.add, ALU.mult)
                        last.then_inc(f_src, 1)
                pool.wait_ge(f_src, l * NM)
                for h in range(2):
                    pool.wait_ge(f_st[h], 16 * l * IT)
                gather_rows(rows, table[l], pos_i, s_g, l, T * P - 1)
            pool.wait_ge(d_st, 16 * Q * NS)
            for t in range(T):
                if t % CH == 0:
                    pool.wait_ge(u_o, t // CH + 1)
                pool.indirect_dma_start(out=out, out_offset=bass.IndirectOffsetOnAxis(ap=put_i[:, t:t + 1], axis=0),
                                        in_=rows[:, t, :], in_offset=None,
                                        bounds_check=N - 1, oob_is_err=False).then_inc(s_out, 16)
            pool.wait_ge(s_out, 16 * T)

        @block.tensor
        def _(pe):
            pe.wait_ge(s_w, 16 * 23)
            pe.wait_ge(s_id, 2)
            for l in range(3):
                if l:
                    pe.wait_ge(s_pd, 1 + 2 * l)
                pe.transpose(bank[:, 0, 0:P], wraw[:, l, :], ident[:, :]).then_inc(s_ppe, 1)
                pe.wait_ge(s_pd, 2 + 2 * l)
                pe.matmul(bank[:, 1, 0:2 * H], wtr, amat[:, :], start=True, stop=True).then_inc(s_ppe, 1)
            for j in range(4):
                for n in range(3):
                    pe.transpose(bank[:, 2 + j, n * D:(n + 1) * D], wnraw[:, n, j * D:(j + 1) * D], ident[:, :])
            for n in range(3):
                last = pe.transpose(bank[:, 6, n * D:(n + 1) * D], weraw[:, n, :], ident[:, :])
            last.then_inc(s_ppe, 1)
            pe.wait_ge(s_ready, 1)
            pe.wait_ge(s_b3, 48)

            def bias(dest, off, n, times, stop=True):
                src_ = bias3[:, off:off + n]
                if times > 1:
                    src_ = src_.rearrange("k (o n) -> k o n", o=1).broadcast_to((3, times, n))
                return pe.matmul(dest, ones3[:, :], src_, start=True, stop=stop)

            def dense(i, beside=None):
                def turn(s, q):
                    if s:
                        pe.wait_ge(d_xh, i * 12 + (s - 1) * 4 + q + 1)
                    buf = dxh if s else dx
                    for j in range(G):
                        last = pe.transpose(bank[:, q, j * D:(j + 1) * D], buf[:, q * G + j, :], ident[:, :])
                    last.then_inc(d_t, 1)

                def layer(l, q):
                    pe.wait_ge(d_xt, i * 16 + l * 4 + q + 1)
                    bias(bank[:, q, :].rearrange("p (g d) -> p g d", g=G), BCO[l], D, G)
                    for j in range(G):
                        o, g = bank[:, q, j * D:(j + 1) * D], slice(j * D, (j + 1) * D)
                        last = pe.matmul(o, (dxt if l else dxt0)[:, q, g], wcen[:, l, :],
                                         start=False, stop=True, skip_group_check=True)
                        if l == 2:
                            last = pe.matmul(o, dxt0[:, q, g], centre[:, :],
                                             start=False, stop=True, skip_group_check=True)
                    last.then_inc(d_h, 1)

                def project(q):
                    pe.wait_ge(d_xt, i * 16 + 12 + q + 1)
                    for hh in range(2):
                        if not isinstance(i, int) or i * 8 + q * 2 + hh >= 2:
                            pe.wait_ge(d_sel, i * 8 + q * 2 + hh - 1)
                        for j in range(2 * hh, 2 * hh + 2):
                            bias(bank[:, 4 + j, 0:3 * D], BNO, 3 * D, 1)
                            last = pe.matmul(bank[:, 4 + j, 0:3 * D], dxt[:, q, j * D:(j + 1) * D],
                                             wnt[:, 0, :], start=False, stop=True, skip_group_check=True)
                        last.then_inc(d_p, 1)

                pe.wait_ge(d_ld, i * 16 + 16)
                for u in range(4 * Q + 1):
                    if u < 4 * Q:
                        turn(*divmod(u, Q))
                    if u:
                        s, q = divmod(u - 1, Q)
                        if s < 3:
                            layer(s, q)
                        else:
                            project(q)
                        if beside and s < 3:
                            beside(u - 1)

            def p1(l):
                n0 = l * T

                pe.wait_ge(d_sel, 8 * first[l])

                def turn(i, tt):
                    n, h = n0 + i * TU + tt, tt // CH
                    if tt % CH == 0:
                        pe.wait_ge(l_s[h], 16 * (l * IT + i + 1))
                        pe.wait_ge(l_d[h], 16 * (l * IT + i + 1))
                    if not isinstance(n, int) or n >= 2:
                        pe.wait_ge(q_xt, n - 1)
                    pe.transpose(bank[:, tt % 2, 0:D], stg[:, tt, :], ident[:, :])
                    pe.transpose(bank[:, tt % 2, D:2 * D], std_[:, tt, :], ident[:, :]).then_inc(q_t, 1)

                def body(i):
                    turn(i, 0)
                    for tt in range(TU):
                        if tt + 1 < TU:
                            turn(i, tt + 1)
                        n = n0 + i * TU + tt
                        pe.wait_ge(q_xt, n + 1)
                        if not isinstance(n, int) or n >= 2:
                            pe.wait_ge(q_ev, n - 1)
                            pe.wait_ge(q_ea, n - 1)
                        for k in range(2):
                            o = bank[:, 2 + 2 * k + tt % 2, 0:WA]
                            bias(o, BO[l], WA, 1)
                            last = pe.matmul(o, xt2[:, tt % 2, k * D:(k + 1) * D], wall[:, l, :],
                                             start=False, stop=True, skip_group_check=True)
                        last.then_inc(q_h, 1)
                run(pe, body, 0, IT, (0,) if l == 0 else ())

            def trip(l, n):
                k, back = ((2, 0, 1)[n // 2], n % 2)
                if l == 0 and k == 2:
                    return
                pe.wait_ge(m_dve, MB[l] + n + (1 if l else -1))
                if back:
                    pe.transpose(bank[:, 7, 0:H], smb if k == 2 else smo[:, 0:P], ident[0:H, 0:H]).then_inc(m_pe, 1)
                else:
                    pe.transpose(bank[0:H, 6, 0:P], sm[:, 2 * k, :], ident[:, :])
                    pe.transpose(bank[0:H, 6, P:2 * P], sm[:, 2 * k + 1, :], ident[:, :]).then_inc(m_pe, 1)

            def softmax(l, slot):
                if slot == 0:
                    pe.wait_ge(d_sel, 8 * first[l])
                if slot in TRIPS:
                    trip(l, TRIPS[slot])
                if slot == 11:
                    pe.wait_ge(m_ci, l + 1)

            def carry(l):
                pe.wait_ge(r_dve, 2 * l + 1)
                pe.transpose(bank[:, 6, 0:P], rowa[:, 0, :], ident[:, :])
                pe.transpose(bank[:, 6, P:2 * P], rowa[:, 1, :], ident[:, :]).then_inc(r_pe, 1)
                pe.wait_ge(r_dve, 2 * l + 2)
                pe.transpose(bank[:, 7, 0:P], rowo[:, 0:P], ident[:, :]).then_inc(r_pe, 1)

            def typed_messages():
                def turn(i, tt):
                    n, h = i * TU + tt, tt // CH
                    if tt % CH == 0:
                        pe.wait_ge(l_v[h], 16 * (i + 1))
                    if not isinstance(n, int) or n >= 2:
                        pe.wait_ge(v_xt, n - 1)
                    pe.transpose(bank[:, tt % 2, 0:D], stg[:, tt, :], ident[:, :]).then_inc(v_t, 1)

                def apply(i, tt):
                    n = i * TU + tt
                    pe.wait_ge(v_xt, n + 1)
                    if not isinstance(n, int) or n >= 2:
                        pe.wait_ge(v_m, n - 1)
                    for k in range(3):
                        o = bank[:, 2 + tt % 2, k * D:(k + 1) * D]
                        pe.matmul(o, bias3[:, BEO + k * D:BEO + (k + 1) * D], ones3[:, :], start=True, stop=True)
                        pe.matmul(o, etm[:, k, tt:tt + 1].broadcast_to((P, D)), identb[:, :],
                                  start=False, stop=True, skip_group_check=True)
                        last = pe.matmul(o, wet[:, k * D:(k + 1) * D], xt2[:, tt % 2, 0:D],
                                         start=False, stop=True, skip_group_check=True)
                    last.then_inc(v_w, 1)

                def project(i, tt):
                    n = i * TU + tt
                    pe.wait_ge(v_m, n + 1)
                    if not isinstance(n, int) or n >= 2:
                        pe.wait_ge(v_sel, n - 1)
                    for k in range(3):
                        last = pe.matmul(bank[:, 6 + tt % 2, 0:3 * D], em[:, tt % 2, k * D:(k + 1) * D],
                                         wnt[:, 1 + k, :], start=(k == 0), stop=(k == 2))
                    last.then_inc(v_v, 1)

                def body(i):
                    turn(i, 0)
                    pe.wait_ge(v_et, i + 1)
                    for tt in range(TU + 1):
                        if tt + 1 < TU:
                            turn(i, tt + 1)
                        if tt < TU:
                            apply(i, tt)
                        if tt:
                            project(i, tt - 1)
                run(pe, body, 0, IT, (0,))

            def typed_targets():
                pe.wait_ge(d_sel, 8 * (NS - 1))

                def turn(i, tt):
                    n, h = i * TU + tt, tt // CH
                    if tt % CH == 0:
                        pe.wait_ge(l_u[h], 16 * (i + 1))
                    if not isinstance(n, int) or n >= 2:
                        pe.wait_ge(u_xt, n - 1)
                    pe.transpose(bank[:, tt % 2, 0:D], std_[:, tt, :], ident[:, :]).then_inc(u_t, 1)

                def body(i):
                    turn(i, 0)
                    for tt in range(TU):
                        if tt + 1 < TU:
                            turn(i, tt + 1)
                        n = i * TU + tt
                        pe.wait_ge(u_xt, n + 1)
                        if not isinstance(n, int) or n >= 2:
                            pe.wait_ge(u_sel, n - 1)
                        bias(bank[:, 2 + tt % 2, 0:3 * D], BNO, 3 * D, 1)
                        pe.matmul(bank[:, 2 + tt % 2, 0:3 * D], xt2[:, tt % 2, 0:D], wnt[:, 0, :],
                                  start=False, stop=True, skip_group_check=True).then_inc(u_p, 1)
                run(pe, body, 0, IT, (0,))

            run(pe, dense, 0, PRE, (0,))
            for l in range(3):
                i = first[l]
                p1(l)
                pe.wait_ge(q_ev, (l + 1) * T)
                pe.wait_ge(q_ea, (l + 1) * T)
                dense(i, lambda slot: softmax(l, slot))
                for j in range(1, 4):
                    dense(i + j)
                carry(l)
                for j in range(4, 7):
                    dense(i + j)
            typed_targets()
            typed_messages()
            dense(NS - 1)
            carry(3)

        @block.scalar
        def _(act):
            act.wait_ge(s_ready, 1)
            act.wait_ge(s_ms, 2)

            def turned(dest, src_, s):
                if s in (1, 2):
                    return nc.scalar.activation(dest, src_, ACT.Relu, scale=gb[:, 2 * s - 2:2 * s - 1],
                                                bias=gb[:, 2 * s - 1:2 * s])
                return nc.scalar.activation(dest, src_, ACT.Relu if s == 3 else ACT.Copy)

            def turn(i, s, q):
                act.wait_ge(d_t, i * 16 + s * 4 + q + 1)
                turned((dxt if s else dxt0)[:, q, :], bank[:, q, :], s).then_inc(d_xt, 1)

            def dense(i, beside=None, more=True):
                def sums(s, q, tile):
                    for j in range(G):
                        last = nc.scalar.activation(junk[:, j, :], tile(j), ACT.Square,
                                                    accum_out=dstd[:, s, q * G + j:q * G + j + 1])
                    last.then_inc(d_ss, 1)
                    act.wait_ge(d_ss, i * 16 + s * 4 + q + 1)
                    nc.scalar.activation(dstd[:, s, q * G:(q + 1) * G], dstd[:, s, q * G:(q + 1) * G], ACT.Sqrt,
                                         scale=1.0 / D, bias=eps[:, 0:1]).then_inc(d_std, 1)

                def type0(q):
                    for hh in range(2):
                        n = i * 8 + q * 2 + hh
                        act.wait_ge(d_p, n + 1)
                        if not isinstance(n, int) or n >= 2:
                            act.wait_ge(d_sel, n - 1)
                        nc.scalar.activation(dsel[:, 2 * hh:2 * hh + 2, :],
                                             bank[:, 4 + 2 * hh:6 + 2 * hh, 0:D], ACT.Copy).then_inc(d_s0, 1)

                def last_sums(q):
                    act.wait_ge(d_sel, i * 8 + q * 2 + 2)
                    sums(3, q, lambda j: dy[:, q * G + j, :])

                for u in range(4 * Q + 1):
                    if 2 <= u < 4 * Q:
                        turn(i, *divmod(u, Q))
                    if u:
                        s, q = divmod(u - 1, Q)
                        if s < 3:
                            act.wait_ge(d_h, i * 12 + s * 4 + q + 1)
                            sums(s, q, lambda j: bank[:, q, j * D:(j + 1) * D])
                        else:
                            type0(q)
                            if q:
                                last_sums(q - 1)
                        if beside and s < 3:
                            beside(u - 1)
                        elif beside:
                            beside(3 * Q + 2 * q)
                            beside(3 * Q + 2 * q + 1)
                if more:
                    for q in range(2):
                        turn(i + 1, 0, q)
                last_sums(Q - 1)

            def ahead(i):
                for q in range(2):
                    turn(i, 0, q)

            def p1(l):
                n0 = l * T

                def turn(i, tt):
                    n = n0 + i * TU + tt
                    act.wait_ge(q_t, n + 1)
                    if not isinstance(n, int) or n >= 2:
                        act.wait_ge(q_h, n - 1)
                    turned(xt2[:, tt % 2, :], bank[:, tt % 2, 0:2 * D], l).then_inc(q_xt, 1)

                def body(i):
                    turn(i, 0)
                    for tt in range(TU):
                        if tt + 1 < TU:
                            turn(i, tt + 1)
                        n, h = n0 + i * TU + tt, tt // CH
                        act.wait_ge(q_h, n + 1)
                        if tt % CH == 0 and (l or not isinstance(i, int) or i):
                            act.wait_ge(q_st[h], 16 * (l * IT + i))
                        nc.scalar.activation(st3[:, tt, :], bank[:, 4 + tt % 2, 0:D], ACT.Copy)
                        nc.scalar.activation(ld[:, bass.ds(i * TU + tt, 1), :],
                                             bank[:, 4 + tt % 2, D:D + 2 * H].rearrange("p (o n) -> p o n", o=1),
                                             ACT.Copy).then_inc(q_ea, 1)
                run(act, body, 0, IT, (0,) if l == 0 else ())

            def softmax(l, slot):
                for k in range(3 if slot == EXPS else 0):
                    act.wait_ge(m_log, 3 * l + k + 1)
                    buf = (ea, e_s, e_f)[k]
                    nc.scalar.activation(buf[:, :, :], buf[:, :, :], ACT.Exp).then_inc(m_act, 1)

            def finish(l, slot, part):
                for piece in pieces(slot, 3 * NM, part, 2, LAYERS):
                    c, step = divmod(piece, 3)
                    if step == 0 and c:
                        if l == 2:
                            squares(l, c - 1)
                        deviations(l, c - 1)
                    if step == 1 and l < 2:
                        squares(l, c)
                    elif step == 1:
                        means(c)

            def finish_last(l):
                if l == 2:
                    squares(l, NM - 1)
                deviations(l, NM - 1)

            def means(c):
                cs = slice(c % NR * CH, (c % NR + 1) * CH)
                act.wait_ge(f_src, 2 * NM + c + 1 - NR)
                act.wait_ge(f_x, c + 1)
                for j in range(CH):
                    m = c % NR * CH + j
                    last = nc.scalar.activation(st3[:, c % 2 * CH + j, :], rows[:, c * CH + j, :], ACT.Copy,
                                                accum_out=csm[:, 0, m:m + 1])
                last.then_inc(f_mean, 1)
                act.wait_ge(f_mean, 2 * c + 1)
                nc.scalar.activation(csm[:, 6, cs], csm[:, 0, cs], ACT.Copy, scale=-1.0 / D).then_inc(f_mean, 1)

            def squares(l, c):
                if l == 2:
                    act.wait_ge(f_mean, 2 * c + 2)
                elif l * NM + c >= NR:
                    act.wait_ge(f_src, l * NM + c + 1 - NR)
                for j in range(CH):
                    t, m = c * CH + j, c % NR * CH + j
                    last = nc.scalar.activation(st3[:, c % 2 * CH + j, :], rows[:, t, :], ACT.Square,
                                                bias=ls[:, t, 2 * H:2 * H + 1] if l < 2 else csm[:, 6, m:m + 1],
                                                accum_out=csm[:, 1, m:m + 1])
                last.then_inc(f_sq, 1)

            def deviations(l, c):
                cs = slice(c % NR * CH, (c % NR + 1) * CH)
                act.wait_ge(f_v, l * NM + c + 1)
                nc.scalar.activation(csm[:, 2, cs], fmv[:, cs, 1:2].rearrange("p t o -> p (t o)"), ACT.Sqrt,
                                     bias=eps[:, 0:1])
                act.wait_ge(f_sq, l * NM + c + 1)
                nc.scalar.activation(csm[:, 3, cs], csm[:, 1, cs], ACT.Sqrt, scale=1.0 / D, bias=eps[:, 0:1])\
                    .then_inc(f_std, 1)

            def typed_messages():
                def turn(i, tt):
                    n = i * TU + tt
                    act.wait_ge(v_t, n + 1)
                    if not isinstance(n, int) or n >= 2:
                        act.wait_ge(v_w, n - 1)
                    turned(xt2[:, tt % 2, 0:D], bank[:, tt % 2, 0:D], 0).then_inc(v_xt, 1)

                def message(i, tt):
                    n = i * TU + tt
                    act.wait_ge(v_w, n + 1)
                    if not isinstance(n, int) or n >= 2:
                        act.wait_ge(v_v, n - 1)
                    nc.scalar.activation(em[:, tt % 2, :], bank[:, 2 + tt % 2, 0:3 * D], ACT.Relu).then_inc(v_m, 1)

                def copy0(i, tt):
                    n = i * TU + tt
                    act.wait_ge(v_v, n + 1)
                    if not isinstance(n, int) or n >= 2:
                        act.wait_ge(v_put, n - 1)
                    nc.scalar.activation(ev[:, tt % 2, :], bank[:, 6 + tt % 2, 0:D], ACT.Copy).then_inc(v_s0, 1)

                def body(i):
                    turn(i, 0)
                    for tt in range(TU + 1):
                        if tt + 1 < TU:
                            turn(i, tt + 1)
                        if tt < TU:
                            message(i, tt)
                        if tt:
                            copy0(i, tt - 1)
                run(act, body, 0, IT, (0,))

            def typed_targets():
                def turn(i, tt):
                    n = i * TU + tt
                    act.wait_ge(u_t, n + 1)
                    if not isinstance(n, int) or n >= 2:
                        act.wait_ge(u_p, n - 1)
                    turned(xt2[:, tt % 2, 0:D], bank[:, tt % 2, 0:D], 3).then_inc(u_xt, 1)

                def body(i):
                    turn(i, 0)
                    for tt in range(TU):
                        if tt + 1 < TU:
                            turn(i, tt + 1)
                        n, h = i * TU + tt, tt // CH
                        act.wait_ge(u_p, n + 1)
                        if tt % CH == 0:
                            if isinstance(i, int) and i == 0:
                                act.wait_ge(f_st[h], 3 * IT * 16)
                            else:
                                act.wait_ge(u_st[h], 16 * i)
                        nc.scalar.activation(stg[:, tt, :], bank[:, 2 + tt % 2, 0:D], ACT.Copy).then_inc(u_s0, 1)
                run(act, body, 0, IT, (0,))

            def last_rows():
                def body(i):
                    for h in range(2):
                        hs = slice(h * CH, (h + 1) * CH)
                        act.wait_ge(w_y, 2 * i + h + 1)
                        nc.scalar.activation(st3[:, hs, :], stg[:, hs, :], ACT.Square).then_inc(w_sq, 1)
                        act.wait_ge(w_v, 2 * i + h + 1)
                        nc.scalar.activation(csm[:, 0, hs], csm[:, 0, hs], ACT.Sqrt,
                                             scale=1.0 / D, bias=eps[:, 0:1]).then_inc(w_std, 1)
                run(act, body, 0, IT)

            ahead(0)
            run(act, dense, 0, PRE - 1, (0,))
            dense(PRE - 1, more=False)
            for l in range(3):
                i = first[l]
                p1(l)
                ahead(i)
                dense(i, lambda slot: softmax(l, slot))
                dense(i + 1)
                dense(i + 2)
                dense(i + 3, more=False)
                ahead(i + 4)
                dense(i + 4)
                dense(i + 5, lambda slot: finish(l, slot, 0))
                dense(i + 6, lambda slot: finish(l, slot, 1), more=False)
                finish_last(l)
            typed_targets()
            typed_messages()
            ahead(NS - 1)
            dense(NS - 1, more=False)
            last_rows()

        @block.vector
        def _(dve):
            v = nc.vector
            st = Steps(dve, d_dve)
            cut = [0]
            DENSE = 32
            v.memset(brow[:, :], 0.0).then_inc(s_ms, 1)
            v.memset(eps[:, :], EPS)
            v.memset(ones3[:, :], 1.0)
            v.memset(zero[:, :], 0.0)
            v.memset(types[:, :], SKIP)
            v.memset(smo[:, 0:1], -BIG)
            v.memset(rowo[:, 0:1], 0.0)
            v.memset(hm[:, :], 0.0).then_inc(s_ms, 1)
            dve.wait_ge(s_ms, 2)
            for h in range(H):
                v.memset(hm[h * C:(h + 1) * C, h:h + 1], 1.0)
            dve.wait_ge(s_w, 16 * 23)
            cent = [(BCO[0], 1), (BCO[1], 1), (BCO[2], 1), (BNO, 3)]
            k = 0
            for off, n in cent:
                st.did(v.tensor_reduce(bmean[:, k:k + n], brow[:, off:off + n * D].rearrange("o (n d) -> o n d", n=n),
                                       AX_X, ALU.add))
                st.did(v.tensor_scalar(bmean[:, k:k + n], bmean[:, k:k + n], 1.0 / D, None, ALU.mult))
                w3 = brow[:, off:off + n * D].rearrange("o (n d) -> o n d", n=n)
                st.did(v.tensor_tensor(w3, w3, bc(bmean[:, k:k + n], D), ALU.subtract))
                if n == 1:
                    v.tensor_scalar(brow[:, BO[k] + D + 2 * H:BO[k] + WA], bmean[:, k:k + 1], -1.0, None, ALU.mult)
                k += n
            st.did(v.tensor_copy(bpart[:, 0, :], brow[:, :]))
            st.did(v.tensor_tensor(brest[:, :], brow[:, :], bpart[:, 0, :], ALU.subtract))
            st.did(v.tensor_copy(bpart[:, 1, :], brest[:, :]))
            st.did(v.tensor_tensor(brest[:, :], brest[:, :], bpart[:, 1, :], ALU.subtract))
            v.tensor_copy(bpart[:, 2, :], brest[:, :]).then_inc(s_pd, 1)
            for l in range(3):
                for k in range(2):
                    last = v.tensor_scalar(amat[:, k * H:(k + 1) * H], hm[:, :], av[:, 2 * l + k:2 * l + k + 1],
                                           None, ALU.mult)
                st.did(last)
                dve.wait_ge(s_ppe, 2 * l + 1)
                v.tensor_copy(wtr, bank[:, 0, 0:P]).then_inc(s_pd, 1)
                v.tensor_copy(wall[:, l, 0:D], wraw[:, l, :])
                st.did(v.tensor_reduce(wmean[:, l:l + 1], wraw[:, l, :], AX_X, ALU.add))
                st.did(v.tensor_scalar(wmean[:, l:l + 1], wmean[:, l:l + 1], 1.0 / D, None, ALU.mult))
                v.tensor_scalar(wall[:, l, D + 2 * H:WA], wmean[:, l:l + 1], -1.0, None, ALU.mult)
                v.tensor_scalar(wcen[:, l, :], wraw[:, l, :], wmean[:, l:l + 1], None, ALU.subtract)
                dve.wait_ge(s_ppe, 2 * l + 2)
                v.tensor_copy(wall[:, l, D:D + 2 * H], bank[:, 1, 0:2 * H]).then_inc(s_pd, 1)
            dve.wait_ge(s_ppe, 7)
            w3 = wnt[:, :, :].rearrange("p j (n o) -> p (j n) o", n=3)
            for j in range(4):
                last = v.tensor_copy(wnt[:, j, :], bank[:, 2 + j, 0:3 * D])
            st.did(last)
            st.did(v.tensor_reduce(wmean[:, 4:16], w3, AX_X, ALU.add))
            st.did(v.tensor_scalar(wmean[:, 4:16], wmean[:, 4:16], 1.0 / D, None, ALU.mult))
            st.did(v.tensor_tensor(w3, w3, bc(wmean[:, 4:16], D), ALU.subtract))
            v.tensor_copy(wet[:, :], bank[:, 6, 0:3 * D])
            v.tensor_scalar(centre[:, :], ident[:, :], 1.0 / D, None, ALU.subtract)
            st.did(v.tensor_copy(identb[:, :], ident[:, :]))
            dve.wait_ge(s_i, 16 * 11)
            v.tensor_scalar(row_i[:, :], dst_i[:, 0, :], float(N - 1), None, ALU.min).then_inc(s_ready, 1)
            dve.wait_ge(s_i, 16 * 11)
            dve.wait_ge(s_id, 6)
            st.did(v.tensor_copy(dst_f[:, :, :], dst_i[:, :, :]))
            v.tensor_tensor(ns[:, :], dst_f[:, 0, :], dst_f[:, 1, :], ALU.not_equal)
            st.did(v.tensor_tensor(lastf[:, :], dst_f[:, 0, :], dst_f[:, 2, :], ALU.not_equal))
            v.tensor_scalar(negns[:, :], ns[:, :], -BIG, None, ALU.mult)
            v.tensor_scalar(keep[:, :], ns[:, :], -1.0, 1.0, ALU.mult, ALU.add)
            v.tensor_scalar(unlast[:, :], lastf[:, :], BIG, -BIG, ALU.mult, ALU.add)
            v.tensor_copy(last_r[:, :], lastf[:, ::-1])
            st.did(v.tensor_scalar(more_r[:, :], lastf[:, ::-1], -1.0, 1.0, ALU.mult, ALU.add))
            st.did(v.tensor_tensor_scan(none_r[:, :], more_r[:, :], zero[:, :], 1.0, ALU.mult, ALU.add))
            st.did(v.tensor_scalar(lastf[:, :], lastf[:, :], -float(SKIP), float(SKIP), ALU.mult, ALU.add))
            st.did(v.tensor_tensor(lastf[:, :], lastf[:, :], dst_f[:, 0, :], ALU.add))
            v.tensor_copy(put_i[:, :], lastf[:, :]).then_inc(s_put, 1)
            st.did(v.tensor_tensor_scan(kept[:, :], ns[:, :], ns[:, :], 0.0, ALU.max, ALU.max))
            st.did(v.tensor_scalar(negseen[:, :], kept[:, :], -BIG, None, ALU.mult))
            st.did(v.tensor_scalar(kept[:, :], kept[:, :], -1.0, 1.0, ALU.mult, ALU.add))
            dve.wait_ge(s_nt, 32)

            met = (s_ms, 2)

            def dense(i, beside=None):
                if not beside:
                    st.enter(i - cut[0], DENSE)
                    beside = (lambda slot: None)
                for k in range(2):
                    v.tensor_scalar(dmk[:, k, :], types[:, bass.ds(i * R, R)], float(k + 1), None, ALU.is_equal)

                def rstd(q, s):
                    dve.wait_ge(d_std, i * 16 + s * 4 + q + 1)
                    st.did(v.reciprocal(drs[:, s, q * G:(q + 1) * G], dstd[:, s, q * G:(q + 1) * G]))

                if not isinstance(i, int) or i:
                    dve.wait_ge(d_st, i * 16 * Q)
                for l in range(3):
                    for q in range(Q):
                        rstd(q, l)
                        v.tensor_tensor(dxh[:, q * G:(q + 1) * G, :],
                                        bank[:, q, :].rearrange("p (g d) -> p g d", g=G),
                                        bc(drs[:, l, q * G:(q + 1) * G], D), ALU.mult).then_inc(d_xh, 1)
                        beside(l * Q + q)

                def recip(q):
                    dve.wait_ge(d_std, i * 16 + 12 + q + 1)
                    return st.mark(v.reciprocal(drs[:, 3, q * G:(q + 1) * G], dstd[:, 3, q * G:(q + 1) * G]))

                def norm(q, mark):
                    st.until(mark)
                    g = slice(q * G, (q + 1) * G)
                    v.tensor_tensor(dy[:, g, :], dy[:, g, :], bc(drs[:, 3, g], D), ALU.mult).then_inc(d_o, 1)

                def choose(q, hh, k):
                    g = slice(q * G + 2 * hh, q * G + 2 * hh + 2)
                    return st.mark(v.copy_predicated(dsel[:, 2 * hh:2 * hh + 2, :], bc(dmk[:, k, g], D),
                                                     bank[:, 4 + 2 * hh:6 + 2 * hh, (k + 1) * D:(k + 2) * D]))

                for q in range(Q):
                    for hh in range(2):
                        n = i * 8 + q * 2 + hh
                        g = slice(q * G + 2 * hh, q * G + 2 * hh + 2)
                        st.wait(d_s0, n + 1, met)
                        mark = choose(q, hh, 0)
                        if not hh and q >= 2:
                            done = recip(q - 2)
                        beside(3 * Q + 2 * q + hh)
                        st.until(mark, met)
                        mark = choose(q, hh, 1)
                        if not hh and q >= 2:
                            norm(q - 2, done)
                        st.until(mark)
                        v.scalar_tensor_tensor(out=dy[:, g, :], in0=dxh[:, g, :], scalar=2.0,
                                               in1=dsel[:, 2 * hh:2 * hh + 2, :],
                                               op0=ALU.mult, op1=ALU.add).then_inc(d_sel, 1)
                for q in range(Q - 2, Q):
                    norm(q, recip(q))

            def run_dense(lo, hi, peel=()):
                cut[0] = lo
                leave = st.loop(hi - lo, DENSE)
                run(dve, dense, lo, hi, peel)
                leave()

            def beside(piece, n, part=0, parts=1, slots=SLOTS):
                def at(slot):
                    for c in pieces(slot, n, part, parts, slots):
                        piece(c)
                return at

            def p1(l):
                n0 = l * T

                def body(i):
                    for tt in range(TU):
                        n = n0 + i * TU + tt
                        b = bank[:, 2 + tt % 2, :].rearrange("p (o n) -> p o n", o=1)
                        dve.wait_ge(q_h, n + 1)
                        v.tensor_copy(rows[:, bass.ds(i * TU + tt, 1), :], b[:, :, 0:D])
                        v.tensor_copy(ls[:, bass.ds(i * TU + tt, 1), :], b[:, :, D:WA]).then_inc(q_ev, 1)
                run(dve, body, 0, IT)

            def softmax(l, slot):
                def lrelu(dest, a_, b_):
                    st.did(v.tensor_tensor(dest[:, :, :], a_, b_, ALU.add))
                    st.did(v.scalar_tensor_tensor(out=dest[:, :, :], in0=dest[:, :, :], scalar=NEG_SLOPE,
                                                  in1=dest[:, :, :], op0=ALU.mult, op1=ALU.max))

                def summary(k, product, value):
                    v.tensor_copy(sm[:, k, :], product)
                    v.tensor_copy(sm[:, k + 1, :], value[:, :, T - 1:T].rearrange("p h o -> p (h o)")).then_inc(m_dve, 1)

                def answer(n):
                    dve.wait_ge(m_pe, MB[l] + n + (1 if l else -1))
                    if n % 2:
                        ins = v.tensor_copy(ci[:, :], bank[:, 7, 0:H])
                        if n == 5:
                            ins.then_inc(m_ci, 1)
                            dve.wait_ge(m_ci, l + 1)
                        else:
                            st.did(ins)
                    else:
                        r = bank[0:H, 6, 0:2 * P].rearrange("h (k p) -> h k p", k=2)
                        st.did(v.tensor_copy(smr[:, :, :], r if n else r[:, :, ::-1]))

                lsv, ldv = (b[:, :, :].rearrange("p t h -> p h t") for b in (ls, ld))
                row = (lambda z: z[:, :].rearrange("p (o t) -> p o t", o=1).broadcast_to((P, H, T)))
                m = mp[:, :, 1:T + 1]
                step = SOFTMAX.get(slot)
                if step == 0:
                    dve.wait_ge(q_ea, (l + 1) * T)
                    dve.wait_ge(q_ev, (l + 1) * T)
                if step == 0 and l:
                    st.did(v.tensor_tensor(fm[:, :, :], ldv[:, H:2 * H, ::-1], row(last_r), ALU.mult))
                    for h in range(H):
                        last = v.tensor_tensor_scan(fm[:, h, :], more_r[:, :], fm[:, h, :], 0.0, ALU.mult, ALU.add)
                    st.did(last)
                    summary(4, none_r[:, T - 1:T].broadcast_to((P, H)), fm)
                if step == 1 and l:
                    v.memset(smo[:, 0:1], 0.0)
                    answer(0)
                    st.did(v.tensor_tensor_scan(smo[:, 1:P + 1], smr[:, 0, :], smr[:, 1, :], 0.0,
                                                ALU.mult, ALU.add))
                    v.tensor_copy(smb, smo[:, P - 1::-1]).then_inc(m_dve, 1)
                if step == 2:
                    of_target = ldv[:, H:2 * H, :]
                    if l:
                        answer(1)
                        for h in range(H):
                            last = v.scalar_tensor_tensor(out=fm[:, h, :], in0=none_r[:, :], scalar=ci[:, h:h + 1],
                                                          in1=fm[:, h, :], op0=ALU.mult, op1=ALU.add)
                        st.did(last)
                        of_target = fm[:, :, ::-1]
                    lrelu(e_s, lsv[:, 0:H, :], of_target)
                    lrelu(e_f, ldv[:, 0:H, :], ldv[:, H:2 * H, :])
                    st.did(v.tensor_tensor(e_f[:, :, :], e_f[:, :, :], row(unlast), ALU.add))
                    st.did(v.tensor_tensor(fm[:, :, :], e_s[:, :, :], e_f[:, :, :], ALU.max))
                    for h in range(H):
                        last = v.tensor_tensor_scan(fm[:, h, :], negns[:, :], fm[:, h, :], -BIG, ALU.add, ALU.max)
                    st.did(last)
                    summary(0, negseen[:, T - 1:T].broadcast_to((P, H)), fm)
                if step == 3:
                    answer(2)
                    if l:
                        st.did(v.memset(smo[:, 0:1], -BIG))
                    v.tensor_tensor_scan(smo[:, 1:P + 1], smr[:, 0, :], smr[:, 1, :], -BIG, ALU.add, ALU.max)\
                        .then_inc(m_dve, 1)
                if step == 4:
                    answer(3)
                    v.tensor_copy(mp[:, :, 0:1].rearrange("p h o -> p (h o)"), ci[:, :])
                    for h in range(H):
                        last = v.scalar_tensor_tensor(out=mp[:, h, 1:T + 1], in0=negseen[:, :], scalar=ci[:, h:h + 1],
                                                      in1=fm[:, h, :], op0=ALU.add, op1=ALU.max)
                    st.did(last)
                    st.did(v.tensor_tensor(ea[:, :, :], mp[:, :, 0:T], m, ALU.subtract))
                    v.tensor_tensor(ea[:, :, :], ea[:, :, :], row(negns), ALU.add).then_inc(m_log, 1)
                    v.tensor_tensor(e_s[:, :, :], e_s[:, :, :], m, ALU.subtract).then_inc(m_log, 1)
                    v.tensor_tensor(e_f[:, :, :], e_f[:, :, :], m, ALU.subtract).then_inc(m_log, 1)
                if step == 5:
                    dve.wait_ge(m_act, 3 * l + 3)
                    st.did(v.tensor_tensor(es[:, :, :], e_s[:, :, :], e_f[:, :, :], ALU.add))
                    for h in range(H):
                        v.tensor_tensor_scan(es[:, h, :], ea[:, h, :], es[:, h, :], 0.0, ALU.mult, ALU.add)
                        last = v.tensor_tensor_scan(ep[:, h, :], ea[:, h, :], zero[:, :], 1.0, ALU.mult, ALU.add)
                    st.did(last)
                    summary(2, ep[:, :, T - 1:T].rearrange("p h o -> p (h o)"), es)
                if step == 6:
                    v.memset(smo[:, 0:1], 0.0)
                    answer(4)
                    v.tensor_tensor_scan(smo[:, 1:P + 1], smr[:, 0, :], smr[:, 1, :], 0.0, ALU.mult, ALU.add)\
                        .then_inc(m_dve, 1)
                if step == 7:
                    answer(5)
                    for h in range(H):
                        last = v.scalar_tensor_tensor(out=es[:, h, :], in0=ep[:, h, :], scalar=ci[:, h:h + 1],
                                                      in1=es[:, h, :], op0=ALU.mult, op1=ALU.add)
                    st.did(last)
                    st.did(v.reciprocal(es[:, :, :], es[:, :, :]))

            def message(l, piece):
                c, part = divmod(piece, 3)
                h, ts = c % 2, slice(c * CH, (c + 1) * CH)
                hs = std_[:, h * CH:(h + 1) * CH, :].rearrange("p t (h c) -> p t h c", h=H)
                dest = msg_f[:, :, ts].rearrange("p (h c) t -> p t h c", h=H)
                if part == 0:
                    v.tensor_tensor(dest, rows[:, ts, :].rearrange("p t (h c) -> p t h c", h=H),
                                    heads(e_s, c * CH, CH), ALU.mult)
                if part == 1:
                    dve.wait_ge(l_h[h], 16 * (l * IT + c // 2 + 1))
                    v.tensor_tensor(hs, hs, heads(e_f, c * CH, CH), ALU.mult).then_inc(m_own, 1)
                if part == 2:
                    dve.wait_ge(m_own, l * NM + c + 1)
                    d2 = msg_f[:, :, ts].rearrange("p f t -> p t f")
                    v.tensor_tensor(d2, d2, std_[:, h * CH:(h + 1) * CH, :], ALU.add).then_inc(p3, 1)

            def scan(a_of, c):
                for h in range(H):
                    f = msg_f[:, c + h * C, :]
                    last = v.tensor_tensor_scan(f, a_of(h), f, 0.0, ALU.mult, ALU.add)
                return last

            def carry(l, p_of, after):
                dve.wait_ge(*after)
                for h in range(H):
                    v.tensor_copy(rowa[:, 0, h * C:(h + 1) * C], p_of(h)[:, T - 1:T].broadcast_to((P, C)))
                v.tensor_copy(rowa[:, 1, :], msg_f[:, :, T - 1:T].rearrange("p f o -> p (f o)")).then_inc(r_dve, 1)
                dve.wait_ge(r_pe, 2 * l + 1)
                st.did(v.tensor_copy(rowt[:, :, :], bank[:, 6, 0:2 * P].rearrange("f (k p) -> f k p", k=2)))
                v.tensor_tensor_scan(rowo[:, 1:P + 1], rowt[:, 0, :], rowt[:, 1, :], 0.0, ALU.mult, ALU.add)\
                    .then_inc(r_dve, 1)
                dve.wait_ge(r_pe, 2 * l + 2)
                st.did(v.tensor_copy(cin, bank[:, 7, 0:P]))

            def fix(p_of, c):
                for h in range(H):
                    f = msg_f[:, c + h * C, :]
                    last = v.scalar_tensor_tensor(out=f, in0=p_of(h), scalar=cin[:, bass.ds(c + h * C, 1)],
                                                  in1=f, op0=ALU.mult, op1=ALU.add)
                return last

            def finish(l, piece):
                c, part = divmod(piece, 3)
                h = c % 2
                hs = slice(h * CH, (h + 1) * CH)
                o = stg[:, hs, :]
                if part == 0:
                    if l * IT + c // 2:
                        dve.wait_ge(f_st[h], 16 * (l * IT + c // 2))
                    v.tensor_tensor(o.rearrange("p t (h c) -> p t h c", h=H),
                                    msg_f[:, :, c * CH:(c + 1) * CH].rearrange("p (h c) t -> p t h c", h=H),
                                    heads(es, c * CH, CH), ALU.mult).then_inc(f_o, 1)
                    return
                if part == 2:
                    if c:
                        reciprocals(l, c - 1)
                        normalise(l, c - 1)
                    return
                dve.wait_ge(f_o, l * NM + c + 1)
                if l == 2:
                    dve.wait_ge(l_x[h], 32 * (c // 2 + 1))
                    st.did(v.tensor_tensor(o, o, std_[:, hs, :], ALU.add))
                for j in range(CH):
                    last = v.bn_stats(fst6[:, j, :], o[:, j, :])
                st.did(last)
                if l * NM + c >= NR:
                    dve.wait_ge(f_src, l * NM + c + 1 - NR)
                for j in range(CH):
                    last = v.bn_aggr(fmv[:, c % NR * CH + j, :], fst6[:, j, :])
                last.then_inc(f_v, 1)

            def reciprocals(l, c):
                cs = slice(c % NR * CH, (c % NR + 1) * CH)
                dve.wait_ge(f_std, l * NM + c + 1)
                v.reciprocal(csm[:, 4:6, cs], csm[:, 2:4, cs]).then_inc(f_y, 1)

            def normalise(l, c):
                dve.wait_ge(f_y, l * NM + c + 1)
                for j in range(CH):
                    m = c % NR * CH + j
                    o = stg[:, c % 2 * CH + j, :]
                    last = v.tensor_scalar(o, o, fmv[:, m, 0:1], csm[:, 4, m:m + 1], ALU.subtract, ALU.mult)
                last.then_inc(f_out, 1)

            def typed_messages():
                def select(i, tt):
                    n = i * TU + tt
                    st.wait(v_s0, n + 1, met)
                    st.did(v.copy_predicated(ev[:, tt % 2, :], ntc[:, 0, tt:tt + 1].broadcast_to((P, D)),
                                             bank[:, 6 + tt % 2, D:2 * D]), met)
                    v.copy_predicated(ev[:, tt % 2, :], ntc[:, 1, tt:tt + 1].broadcast_to((P, D)),
                                      bank[:, 6 + tt % 2, 2 * D:3 * D]).then_inc(v_sel, 1)
                    dve.wait_ge(v_sel, n + 1)
                    v.tensor_copy(msg_f[:, :, bass.ds(i * TU + tt, 1)].rearrange("p f o -> p (f o)"),
                                  ev[:, tt % 2, :]).then_inc(v_put, 1)

                def body(i):
                    DP = 1 + TU
                    st.enter(i, DP)
                    if not isinstance(i, int) or i:
                        dve.wait_ge(v_w, i * TU)
                    for k in range(K3):
                        last = v.tensor_scalar(etm[:, k, :], et_i[:, bass.ds(i * TU, TU)], float(k), -BIG,
                                               ALU.not_equal, ALU.mult)
                    last.then_inc(v_et, 1)
                    st.did(v.tensor_copy(ntc[:, :, :], ntm[:, :, bass.ds(i * TU, TU)]))
                    for tt in range(TU):
                        select(i, tt)
                    assert st.c == DP
                leave = st.loop(IT, 1 + TU)
                run(dve, body, 0, IT, (0,))
                leave()

            def typed_targets():
                def chunk(h):
                    hs = slice(h * CH, (h + 1) * CH)
                    v.scalar_tensor_tensor(out=stg[:, hs, :], in0=std_[:, hs, :], scalar=2.0, in1=stg[:, hs, :],
                                           op0=ALU.mult, op1=ALU.add).then_inc(u_y, 1)

                def body(i):
                    DP = 1 + TU
                    st.enter(i, DP)
                    st.did(v.tensor_copy(ntc[:, :, :], ntm[:, :, bass.ds(i * TU, TU)]))
                    for tt in range(TU):
                        n = i * TU + tt
                        st.wait(u_s0, n + 1, met)
                        for k in range(2):
                            ins = v.copy_predicated(stg[:, tt, :], ntc[:, k, tt:tt + 1].broadcast_to((P, D)),
                                                    bank[:, 2 + tt % 2, (k + 1) * D:(k + 2) * D])
                            if k == 0:
                                st.did(ins, met)
                        ins.then_inc(u_sel, 1)
                        if tt % CH == CH - 1:
                            dve.wait_ge(u_sel, n + 1)
                            chunk(tt // CH)
                    assert st.c == DP
                leave = st.loop(IT, 1 + TU)
                run(dve, body, 0, IT, (0,))
                leave()

            def last_rows():
                def chunk(i, h):
                    c = 2 * i + h
                    hs = slice(h * CH, (h + 1) * CH)
                    o = stg[:, hs, :]
                    st.did(v.tensor_tensor(o, kept[:, bass.ds(c * CH, CH)].rearrange("p (t o) -> p t o", o=1)
                                           .broadcast_to((P, CH, D)),
                                           cin.rearrange("p (o f) -> p o f", o=1).broadcast_to((P, CH, D)),
                                           ALU.mult))
                    st.did(v.tensor_tensor(o, o, msg_f[:, :, bass.ds(c * CH, CH)].rearrange("p f t -> p t f"),
                                           ALU.add))
                    dve.wait_ge(l_w[h], 16 * (i + 1))
                    v.tensor_tensor(o, o, std_[:, hs, :], ALU.add).then_inc(w_y, 1)
                    dve.wait_ge(w_sq, c + 1)
                    v.tensor_reduce(csm[:, 0, hs], st3[:, hs, :], AX_X, ALU.add).then_inc(w_v, 1)
                    dve.wait_ge(w_std, c + 1)
                    st.did(v.reciprocal(csm[:, 4, hs], csm[:, 0, hs]))
                    v.tensor_tensor(rows[:, bass.ds(c * CH, CH), :], o, bc(csm[:, 4, hs], D), ALU.mult)\
                        .then_inc(u_o, 1)

                def body(i):
                    st.enter(i, 6)
                    for h in range(2):
                        chunk(i, h)
                    assert st.c == 6
                leave = st.loop(IT, 6)
                run(dve, body, 0, IT)
                leave()

            run_dense(0, PRE, (0,))
            a_gat, p_gat = (lambda h: ea[:, h, :]), (lambda h: ep[:, h, :])
            for l in range(3):
                i = first[l]
                if l == 0:
                    dve.wait_ge(s_sv, 16 * NM)
                p1(l)
                dense(i, lambda slot: softmax(l, slot))
                if l == 0:
                    dve.wait_ge(s_svd, 16 * NM)
                for k in range(2):
                    dense(i + 1 + k, beside(lambda c: message(l, c), 3 * NM, k, 2))
                dve.wait_ge(p3, (l + 1) * NM)
                dense(i + 3, beside(lambda c: scan(a_gat, c).then_inc(s_scan, 1), C))
                carry(l, p_gat, (s_scan, 2 * l * C + C))
                dense(i + 4, beside(lambda c: fix(p_gat, c).then_inc(s_scan, 1), C))
                dve.wait_ge(s_scan, 2 * (l + 1) * C)
                for k in range(2):
                    dense(i + 5 + k, beside(lambda c: finish(l, c), 3 * NM, k, 2, LAYERS))
                reciprocals(l, NM - 1)
                normalise(l, NM - 1)
            dve.wait_ge(s_ntg, 16 * T)
            for k in range(2):
                last = v.tensor_scalar(ntm[:, k, :], nt_i[:, :], float(k + 1), None, ALU.is_equal)
            st.did(last)
            typed_targets()
            typed_messages()
            dve.wait_ge(v_put, T)
            dense(NS - 1, beside(lambda c: scan(lambda h: keep[:, :], c).then_inc(s_scan, 1), C))
            carry(3, lambda h: kept[:, :], (s_scan, 7 * C))
            last_rows()


_INS = ["x", "src", "dst", "edge_type_3", "node_type_3",
        *(f"L0_gnn_{n}{l}" for l in range(3) for n in ("W", "a_src", "a_dst", "b")),
        "L0_gnn_ln0_g", "L0_gnn_ln0_b", "L0_gnn_ln1_g", "L0_gnn_ln1_b",
        "L1_gnn_W_e", "L1_gnn_b_e", "L1_gnn_W_n", "L1_gnn_b_n"]


def kernel(**inputs):
    import numpy as _np
    import concourse.bacc as _bacc
    from concourse import mybir as _mybir
    from concourse.bass_utils import run_bass_kernel_spmd as _run

    nc = _bacc.Bacc("TRN2", target_bir_lowering=False, num_devices=1)
    arrays, aps = {}, {}
    for name in _INS:
        v = _np.ascontiguousarray(inputs[name])
        arrays[f"in_{name}_dram"] = v
        aps[name] = nc.dram_tensor(f"in_{name}_dram", v.shape, _mybir.dt.from_np(v.dtype), kind="ExternalInput").ap()
    shape = inputs["x"].shape
    out = nc.dram_tensor("out_0_dram", shape, _mybir.dt.from_np(_np.dtype("float32")), kind="ExternalOutput").ap()
    build(nc, aps, out)
    r = _run(nc, [arrays], core_ids=[0])
    return r.results[0]["out_0_dram"]
```
